# Optimizing a Trainium2 kernel written in Bass

```python
import numpy as np
import jax
import jax.numpy as jnp

def _softmax(x, axis=-1):
    return jax.nn.softmax(x, axis=axis)

def _gelu(x):
    return jax.nn.gelu(x, approximate=True)

def _silu(x):
    return jax.nn.silu(x)

def _sigmoid(x):
    return jax.nn.sigmoid(x)

def _layernorm(x, axis=-1, eps=1e-05):
    m = jnp.mean(x, axis=axis, keepdims=True)
    v = jnp.var(x, axis=axis, keepdims=True)
    return (x - m) / jnp.sqrt(v + eps)

def _scatter_add(tgt, idx, src, axis=0):
    return tgt.at[idx].add(src)

def _segment_sum(src, seg, n):
    return jax.ops.segment_sum(src, seg, n)
kernel_name = 'mk_decoder_preln_d2_seqx_r8_9e7971'

def setup_inputs(seed: int=0):
    np.random.seed(seed)
    _w = jnp.asarray

    def _rec_inputs():
        import jax
        import jax.numpy as jnp
        _rk = jax.random.key(seed)
        x = 7.22e-05 + 1 * jax.random.normal(jax.random.fold_in(_rk, 1), (4, 512, 128), jnp.float32)
        _lenS = 512 - jax.random.randint(jax.random.fold_in(_rk, 7), (4,), 0, max(1, 512 // 4) + 1, jnp.int32)
        _lenS2 = 77 - jax.random.randint(jax.random.fold_in(_rk, 8), (4,), 0, max(1, 77 // 4) + 1, jnp.int32)
        _ctx_1024P = jax.random.normal(jax.random.fold_in(_rk, 11), (4, 16, 128), jnp.float32)
        _ctx_1024c = jax.random.dirichlet(jax.random.fold_in(_rk, 511), 0.3 * jnp.ones((16,), jnp.float32), (4, 77))
        _ctx_1024t = jnp.einsum('bsk,bkd->bsd', _ctx_1024c, _ctx_1024P)
        _ctx_1024t = _ctx_1024t * jax.lax.rsqrt(jnp.mean(jnp.square(_ctx_1024t)) + 1e-12) * 0.953939
        ctx_1024 = 4.13588e-05 + 0.999923 * (_ctx_1024t + 0.3 * jax.random.normal(jax.random.fold_in(_rk, 611), (4, 77, 128), jnp.float32))
        return (x, ctx_1024)
    x, ctx_1024 = _rec_inputs()

    def _L0_attn_setup():
        import jax, jax.numpy as jnp
        import numpy as np
        DIM = 128
        HEADS = 16
        HD = DIM // HEADS
        HID = 4 * DIM
        TPF = 1374
        LR = 0.1
        NS_ITERS = 5
        TTT_STEPS = 2
        B, S = (2, 4)
        SN = S * TPF

        def _newton_schulz(G, iters=NS_ITERS):
            a, b, c = (3.4445, -4.775, 2.0315)
            X = G / (jnp.linalg.norm(G) + 1e-07)
            transposed = G.shape[0] > G.shape[1]
            if transposed:
                X = X.T
            for _ in range(iters):
                A = X @ X.T
                X = a * X + (b * A + c * (A @ A)) @ X
            return X.T if transposed else X

        def _muon_update(p, g):
            return p - LR * _newton_schulz(g)
        key = jax.random.key(seed)
        ks = jax.random.split(key, 8)
        inp = {'x': jax.random.normal(ks[0], (B, SN, DIM), jnp.float32), 'qkv_w': jax.random.normal(ks[1], (DIM, 3 * DIM), jnp.float32) * DIM ** (-0.5), 'qkv_b': jnp.zeros((3 * DIM,), jnp.float32), 'qn_scale': jnp.ones((HD,), jnp.float32), 'qn_bias': jnp.zeros((HD,), jnp.float32), 'kn_scale': jnp.ones((HD,), jnp.float32), 'kn_bias': jnp.zeros((HD,), jnp.float32), 'ttt_gate': jax.random.normal(ks[2], (DIM, HID), jnp.float32) * DIM ** (-0.5), 'ttt_val': jax.random.normal(ks[3], (DIM, HID), jnp.float32) * DIM ** (-0.5), 'ttt_proj': jax.random.normal(ks[4], (HID, DIM), jnp.float32) * HID ** (-0.5), 'proj_w': jax.random.normal(ks[5], (DIM, DIM), jnp.float32) * DIM ** (-0.5), 'proj_b': jnp.zeros((DIM,), jnp.float32)}
        return inp
    _L0_attn_all = _L0_attn_setup()
    _L0_attn_in = {k: v for k, v in _L0_attn_all.items() if k in ('qkv_w', 'qkv_b', 'qn_scale', 'qn_bias', 'kn_scale', 'kn_bias', 'ttt_gate', 'ttt_val', 'ttt_proj', 'proj_w', 'proj_b')}
    del _L0_attn_all

    def _L0_xattn_setup():
        import jax, jax.numpy as jnp
        import numpy as np
        D_MODEL = 128
        NUM_HEADS = 16
        D_K = D_MODEL // NUM_HEADS

        def _split_heads(x):
            B, S, _ = x.shape
            return x.reshape(B, S, NUM_HEADS, D_K).transpose(0, 2, 1, 3)
        key = jax.random.key(seed)
        ks = jax.random.split(key, 11)
        B, S = (4, 256)
        s = 1.0 / np.sqrt(D_MODEL)
        inp = {'q': jax.random.normal(ks[0], (B, S, D_MODEL), dtype=jnp.float32), 'k': jax.random.normal(ks[1], (B, S, D_MODEL), dtype=jnp.float32), 'v': jax.random.normal(ks[2], (B, S, D_MODEL), dtype=jnp.float32), 'Wq': jax.random.normal(ks[3], (D_MODEL, D_MODEL), dtype=jnp.float32) * s, 'bq': jnp.zeros((D_MODEL,), dtype=jnp.float32), 'Wk': jax.random.normal(ks[4], (D_MODEL, D_MODEL), dtype=jnp.float32) * s, 'bk': jnp.zeros((D_MODEL,), dtype=jnp.float32), 'Wv': jax.random.normal(ks[5], (D_MODEL, D_MODEL), dtype=jnp.float32) * s, 'bv': jnp.zeros((D_MODEL,), dtype=jnp.float32), 'Wo': jax.random.normal(ks[6], (D_MODEL, D_MODEL), dtype=jnp.float32) * s, 'bo': jnp.zeros((D_MODEL,), dtype=jnp.float32)}
        return inp
    _L0_xattn_all = _L0_xattn_setup()
    _L0_xattn_in = {k: v for k, v in _L0_xattn_all.items() if k in ('Wq', 'bq', 'Wk', 'bk', 'Wv', 'bv', 'Wo', 'bo')}
    del _L0_xattn_all

    def _L0_ffn_setup():
        import jax, jax.numpy as jnp
        import numpy as np
        EPS = 1e-08

        def _ternary_linear(x, w):
            alpha = jnp.mean(jnp.abs(w))
            w_t = jnp.sign(w) * (jnp.abs(w) > 0.5 * alpha).astype(w.dtype)
            w_q = w + jax.lax.stop_gradient(w_t - w)
            d = x.shape[-1]
            rms = jnp.sqrt(jnp.sum(x * x, axis=-1, keepdims=True)) / jnp.sqrt(jnp.asarray(d, x.dtype))
            x_norm = x / (rms + EPS)
            return jnp.einsum('bsd,fd->bsf', x_norm, w_q)
        key = jax.random.key(seed)
        k1, k2, k3 = jax.random.split(key, 3)
        d_model, d_ff = (128, 512)
        B, S = (4, 512)
        x = jax.random.normal(k1, (B, S, d_model), dtype=jnp.float32)
        w_up = jax.random.normal(k2, (d_ff, d_model), dtype=jnp.float32) * 0.02
        w_down = jax.random.normal(k3, (d_model, d_ff), dtype=jnp.float32) * 0.02
        return {'x': x, 'w_up': w_up, 'w_down': w_down}
    _L0_ffn_all = _L0_ffn_setup()
    _L0_ffn_in = {k: v for k, v in _L0_ffn_all.items() if k in ('w_up', 'w_down')}
    del _L0_ffn_all

    def _L1_attn_setup():
        import jax, jax.numpy as jnp
        import numpy as np
        N_INPUT = 128
        N_HEAD = 16
        ATT_DIM = N_INPUT // N_HEAD * N_HEAD
        V_DIM = N_INPUT // 2 * N_HEAD
        COMB_DIM = 2 * ATT_DIM + V_DIM
        SCALE = (N_INPUT // N_HEAD) ** 0.5
        key = jax.random.key(seed)
        k1, k2, k3 = jax.random.split(key, 3)
        B, T = (8, 128)
        representations = jax.random.normal(k1, (B, T, N_INPUT), dtype=jnp.float32)
        Wc = jax.random.normal(k2, (COMB_DIM, N_INPUT), dtype=jnp.float32) * (0.1 * np.sqrt(2.0 / (COMB_DIM + N_INPUT)))
        bc = jnp.zeros((COMB_DIM,), dtype=jnp.float32)
        Wo = jax.random.normal(k3, (N_INPUT, V_DIM), dtype=jnp.float32) * (0.1 * np.sqrt(2.0 / (N_INPUT + V_DIM)))
        bo = jnp.zeros((N_INPUT,), dtype=jnp.float32)
        return {'representations': representations, 'Wc': Wc, 'bc': bc, 'Wo': Wo, 'bo': bo}
    _L1_attn_all = _L1_attn_setup()
    _L1_attn_in = {k: v for k, v in _L1_attn_all.items() if k in ('Wc', 'bc', 'Wo', 'bo')}
    del _L1_attn_all

    def _L1_xattn_setup():
        import jax, jax.numpy as jnp
        import numpy as np
        D_MODEL = 128
        D_HEAD = 64
        NHEADS = 8
        IN_DIM = D_HEAD * NHEADS
        EPS = 1e-05

        def layernorm(x, g, b):
            mu = jnp.mean(x, axis=-1, keepdims=True)
            var = jnp.var(x, axis=-1, keepdims=True)
            return (x - mu) * jax.lax.rsqrt(var + EPS) * g + b
        key = jax.random.key(seed)
        ks = jax.random.split(key, 8)
        B, M, L = (4, 1024, 64)
        x = jax.random.normal(ks[0], (B, M, D_MODEL), dtype=jnp.float32)
        latents = jax.random.normal(ks[1], (B, L, D_MODEL), dtype=jnp.float32)
        s = 1.0 / np.sqrt(D_MODEL)
        Wq = jax.random.normal(ks[2], (D_MODEL, IN_DIM), dtype=jnp.float32) * s
        Wkv = jax.random.normal(ks[3], (D_MODEL, 2 * IN_DIM), dtype=jnp.float32) * s
        Wout = jax.random.normal(ks[4], (IN_DIM, D_MODEL), dtype=jnp.float32) * (1.0 / np.sqrt(IN_DIM))
        gm = jnp.ones((D_MODEL,), jnp.float32)
        bm = jnp.zeros((D_MODEL,), jnp.float32)
        gl = jnp.ones((D_MODEL,), jnp.float32)
        bl = jnp.zeros((D_MODEL,), jnp.float32)
        return {'x': x, 'latents': latents, 'Wq': Wq, 'Wkv': Wkv, 'Wout': Wout, 'gm': gm, 'bm': bm, 'gl': gl, 'bl': bl}
    _L1_xattn_all = _L1_xattn_setup()
    _L1_xattn_in = {k: v for k, v in _L1_xattn_all.items() if k in ('Wq', 'Wkv', 'Wout', 'gm', 'bm', 'gl', 'bl')}
    del _L1_xattn_all

    def _L1_ffn_setup():
        import jax, jax.numpy as jnp
        import numpy as np
        B, T, D, H, E, K = (2, 128, 128, 16, 8, 2)
        HS = D // H
        FF = 4 * D

        def layernorm(x, g, b, eps=1e-05):
            m = jnp.mean(x, axis=-1, keepdims=True)
            v = jnp.mean((x - m) ** 2, axis=-1, keepdims=True)
            return (x - m) * jax.lax.rsqrt(v + eps) * g + b
        key = jax.random.key(seed)
        ks = jax.random.split(key, 10)
        s = 0.02
        return {'x': jax.random.normal(ks[0], (B, T, D), jnp.float32), 'Wq': jax.random.normal(ks[1], (H, D, HS), jnp.float32) * s, 'Wk': jax.random.normal(ks[2], (H, D, HS), jnp.float32) * s, 'Wv': jax.random.normal(ks[3], (H, D, HS), jnp.float32) * s, 'gate_W': jax.random.normal(ks[4], (D, E), jnp.float32) * s, 'W1': jax.random.normal(ks[5], (E, D, FF), jnp.float32) * s, 'b1': jnp.zeros((E, FF), jnp.float32), 'W2': jax.random.normal(ks[6], (E, FF, D), jnp.float32) * s, 'b2': jnp.zeros((E, D), jnp.float32), 'ln1_g': jnp.ones((D,), jnp.float32), 'ln1_b': jnp.zeros((D,), jnp.float32), 'ln2_g': jnp.ones((D,), jnp.float32), 'ln2_b': jnp.zeros((D,), jnp.float32)}
    _L1_ffn_all = _L1_ffn_setup()
    _L1_ffn_in = {k: v for k, v in _L1_ffn_all.items() if k in ('Wq', 'Wk', 'Wv', 'gate_W', 'W1', 'b1', 'W2', 'b2', 'ln1_g', 'ln1_b', 'ln2_g', 'ln2_b')}
    del _L1_ffn_all
    return {'x': x, 'ctx_1024': ctx_1024, 'L0_attn_qkv_w': _L0_attn_in['qkv_w'], 'L0_attn_qkv_b': _L0_attn_in['qkv_b'], 'L0_attn_qn_scale': _L0_attn_in['qn_scale'], 'L0_attn_qn_bias': _L0_attn_in['qn_bias'], 'L0_attn_kn_scale': _L0_attn_in['kn_scale'], 'L0_attn_kn_bias': _L0_attn_in['kn_bias'], 'L0_attn_ttt_gate': _L0_attn_in['ttt_gate'], 'L0_attn_ttt_val': _L0_attn_in['ttt_val'], 'L0_attn_ttt_proj': _L0_attn_in['ttt_proj'], 'L0_attn_proj_w': _L0_attn_in['proj_w'], 'L0_attn_proj_b': _L0_attn_in['proj_b'], 'L0_xattn_Wq': _L0_xattn_in['Wq'], 'L0_xattn_bq': _L0_xattn_in['bq'], 'L0_xattn_Wk': _L0_xattn_in['Wk'], 'L0_xattn_bk': _L0_xattn_in['bk'], 'L0_xattn_Wv': _L0_xattn_in['Wv'], 'L0_xattn_bv': _L0_xattn_in['bv'], 'L0_xattn_Wo': _L0_xattn_in['Wo'], 'L0_xattn_bo': _L0_xattn_in['bo'], 'L0_ffn_w_up': _L0_ffn_in['w_up'], 'L0_ffn_w_down': _L0_ffn_in['w_down'], 'L1_attn_Wc': _L1_attn_in['Wc'], 'L1_attn_bc': _L1_attn_in['bc'], 'L1_attn_Wo': _L1_attn_in['Wo'], 'L1_attn_bo': _L1_attn_in['bo'], 'L1_xattn_Wq': _L1_xattn_in['Wq'], 'L1_xattn_Wkv': _L1_xattn_in['Wkv'], 'L1_xattn_Wout': _L1_xattn_in['Wout'], 'L1_xattn_gm': _L1_xattn_in['gm'], 'L1_xattn_bm': _L1_xattn_in['bm'], 'L1_xattn_gl': _L1_xattn_in['gl'], 'L1_xattn_bl': _L1_xattn_in['bl'], 'L1_ffn_Wq': _L1_ffn_in['Wq'], 'L1_ffn_Wk': _L1_ffn_in['Wk'], 'L1_ffn_Wv': _L1_ffn_in['Wv'], 'L1_ffn_gate_W': _L1_ffn_in['gate_W'], 'L1_ffn_W1': _L1_ffn_in['W1'], 'L1_ffn_b1': _L1_ffn_in['b1'], 'L1_ffn_W2': _L1_ffn_in['W2'], 'L1_ffn_b2': _L1_ffn_in['b2'], 'L1_ffn_ln1_g': _L1_ffn_in['ln1_g'], 'L1_ffn_ln1_b': _L1_ffn_in['ln1_b'], 'L1_ffn_ln2_g': _L1_ffn_in['ln2_g'], 'L1_ffn_ln2_b': _L1_ffn_in['ln2_b']}

def reference(x, ctx_1024, L0_attn_qkv_w, L0_attn_qkv_b, L0_attn_qn_scale, L0_attn_qn_bias, L0_attn_kn_scale, L0_attn_kn_bias, L0_attn_ttt_gate, L0_attn_ttt_val, L0_attn_ttt_proj, L0_attn_proj_w, L0_attn_proj_b, L0_xattn_Wq, L0_xattn_bq, L0_xattn_Wk, L0_xattn_bk, L0_xattn_Wv, L0_xattn_bv, L0_xattn_Wo, L0_xattn_bo, L0_ffn_w_up, L0_ffn_w_down, L1_attn_Wc, L1_attn_bc, L1_attn_Wo, L1_attn_bo, L1_xattn_Wq, L1_xattn_Wkv, L1_xattn_Wout, L1_xattn_gm, L1_xattn_bm, L1_xattn_gl, L1_xattn_bl, L1_ffn_Wq, L1_ffn_Wk, L1_ffn_Wv, L1_ffn_gate_W, L1_ffn_W1, L1_ffn_b1, L1_ffn_W2, L1_ffn_b2, L1_ffn_ln1_g, L1_ffn_ln1_b, L1_ffn_ln2_g, L1_ffn_ln2_b):
    import jax
    import jax.numpy as jnp

    def _L0_attn_ref(x, qkv_w, qkv_b, qn_scale, qn_bias, kn_scale, kn_bias, ttt_gate, ttt_val, ttt_proj, proj_w, proj_b):
        import jax, jax.numpy as jnp
        import numpy as np
        DIM = 128
        HEADS = 16
        HD = DIM // HEADS
        HID = 4 * DIM
        TPF = 1374
        LR = 0.1
        NS_ITERS = 5
        TTT_STEPS = 2
        B, S = (2, 4)
        SN = S * TPF

        def _newton_schulz(G, iters=NS_ITERS):
            a, b, c = (3.4445, -4.775, 2.0315)
            X = G / (jnp.linalg.norm(G) + 1e-07)
            transposed = G.shape[0] > G.shape[1]
            if transposed:
                X = X.T
            for _ in range(iters):
                A = X @ X.T
                X = a * X + (b * A + c * (A @ A)) @ X
            return X.T if transposed else X

        def _muon_update(p, g):
            return p - LR * _newton_schulz(g)
        Bx, SNx, _ = x.shape
        qkv = x @ qkv_w + qkv_b
        q, k, v = jnp.split(qkv, 3, axis=-1)
        q = q.reshape(Bx, SNx, HEADS, HD)
        k = k.reshape(Bx, SNx, HEADS, HD)
        q = q / (jnp.linalg.norm(q, axis=-1, keepdims=True) + 1e-06) * qn_scale + qn_bias
        k = k / (jnp.linalg.norm(k, axis=-1, keepdims=True) + 1e-06) * kn_scale + kn_bias
        q_ttt = q.reshape(-1, DIM)
        k_ttt = k.reshape(-1, DIM)
        v_ttt = v.reshape(-1, DIM)
        theta = {'gate': ttt_gate, 'val': ttt_val, 'proj': ttt_proj}

        def loss_fn(p):
            h = jax.nn.swish(k_ttt @ p['gate']) * (k_ttt @ p['val'])
            pred = h @ p['proj']
            return jnp.mean((pred - v_ttt) ** 2)
        for _ in range(TTT_STEPS):
            grads = jax.grad(loss_fn)(theta)
            theta = {kk: _muon_update(theta[kk], grads[kk]) for kk in theta}
        h_q = jax.nn.swish(q_ttt @ theta['gate']) * (q_ttt @ theta['val'])
        o = h_q @ theta['proj'] @ proj_w + proj_b
        return o.reshape(Bx, SNx, DIM)

    def _L0_xattn_ref(q, k, v, Wq, bq, Wk, bk, Wv, bv, Wo, bo):
        import jax, jax.numpy as jnp
        import numpy as np
        D_MODEL = 128
        NUM_HEADS = 16
        D_K = D_MODEL // NUM_HEADS

        def _split_heads(x):
            B, S, _ = x.shape
            return x.reshape(B, S, NUM_HEADS, D_K).transpose(0, 2, 1, 3)
        B, S, _ = q.shape
        qh = _split_heads(q @ Wq.T + bq)
        kh = _split_heads(k @ Wk.T + bk)
        vh = _split_heads(v @ Wv.T + bv)
        scale = 1.0 / jnp.sqrt(jnp.asarray(D_K, dtype=qh.dtype))
        scores = jnp.einsum('bhqd,bhkd->bhqk', qh, kh) * scale
        attn = jax.nn.softmax(scores, axis=-1)
        out = jnp.einsum('bhqk,bhkd->bhqd', attn, vh)
        out = out.transpose(0, 2, 1, 3).reshape(B, S, D_MODEL)
        return out @ Wo.T + bo

    def _L0_ffn_ref(x, w_up, w_down):
        import jax, jax.numpy as jnp
        import numpy as np
        EPS = 1e-08

        def _ternary_linear(x, w):
            alpha = jnp.mean(jnp.abs(w))
            w_t = jnp.sign(w) * (jnp.abs(w) > 0.5 * alpha).astype(w.dtype)
            w_q = w + jax.lax.stop_gradient(w_t - w)
            d = x.shape[-1]
            rms = jnp.sqrt(jnp.sum(x * x, axis=-1, keepdims=True)) / jnp.sqrt(jnp.asarray(d, x.dtype))
            x_norm = x / (rms + EPS)
            return jnp.einsum('bsd,fd->bsf', x_norm, w_q)
        h = jax.nn.gelu(_ternary_linear(x, w_up), approximate=False)
        return _ternary_linear(h, w_down)

    def _L1_attn_ref(representations, Wc, bc, Wo, bo):
        import jax, jax.numpy as jnp
        import numpy as np
        N_INPUT = 128
        N_HEAD = 16
        ATT_DIM = N_INPUT // N_HEAD * N_HEAD
        V_DIM = N_INPUT // 2 * N_HEAD
        COMB_DIM = 2 * ATT_DIM + V_DIM
        SCALE = (N_INPUT // N_HEAD) ** 0.5
        B, T, D = representations.shape
        H = N_HEAD
        dh = ATT_DIM // H
        dv = V_DIM // H
        cp = jax.nn.leaky_relu(jnp.einsum('btd,cd->btc', representations, Wc) + bc)
        q = cp[..., :ATT_DIM].reshape(B, T, H, dh)
        k = cp[..., ATT_DIM:2 * ATT_DIM].reshape(B, T, H, dh)
        v = cp[..., 2 * ATT_DIM:].reshape(B, T, H, dv)
        scores = jnp.einsum('bqhd,bkhd->bhqk', q, k) / SCALE
        attn = jax.nn.softmax(scores, axis=-1)
        out = jnp.einsum('bhqk,bkhd->bqhd', attn, v).reshape(B, T, V_DIM)
        proj = jax.nn.leaky_relu(jnp.einsum('btv,dv->btd', out, Wo) + bo)
        return representations + proj

    def _L1_xattn_ref(x, latents, Wq, Wkv, Wout, gm, bm, gl, bl):
        import jax, jax.numpy as jnp
        import numpy as np
        D_MODEL = 128
        D_HEAD = 64
        NHEADS = 8
        IN_DIM = D_HEAD * NHEADS
        EPS = 1e-05

        def layernorm(x, g, b):
            mu = jnp.mean(x, axis=-1, keepdims=True)
            var = jnp.var(x, axis=-1, keepdims=True)
            return (x - mu) * jax.lax.rsqrt(var + EPS) * g + b
        scale = D_HEAD ** (-0.5)
        xn = layernorm(x, gm, bm)
        ln = layernorm(latents, gl, bl)
        q = ln @ Wq
        kv_input = jnp.concatenate([xn, ln], axis=-2)
        kv = kv_input @ Wkv
        k, v = jnp.split(kv, 2, axis=-1)

        def heads(t):
            B, S, _ = t.shape
            return t.reshape(B, S, NHEADS, D_HEAD).transpose(0, 2, 1, 3)
        q, k, v = (heads(q), heads(k), heads(v))
        q = q / scale
        sim = jnp.einsum('bhid,bhjd->bhij', q, k)
        sim = sim - jax.lax.stop_gradient(jnp.max(sim, axis=-1, keepdims=True))
        attn = jax.nn.softmax(sim, axis=-1)
        out = jnp.einsum('bhij,bhjd->bhid', attn, v)
        B, H, L, dh = out.shape
        out = out.transpose(0, 2, 1, 3).reshape(B, L, H * dh)
        return out @ Wout

    def _L1_ffn_ref(x, Wq, Wk, Wv, gate_W, W1, b1, W2, b2, ln1_g, ln1_b, ln2_g, ln2_b):
        import jax, jax.numpy as jnp
        import numpy as np
        B, T, D, H, E, K = (2, 128, 128, 16, 8, 2)
        HS = D // H
        FF = 4 * D

        def layernorm(x, g, b, eps=1e-05):
            m = jnp.mean(x, axis=-1, keepdims=True)
            v = jnp.mean((x - m) ** 2, axis=-1, keepdims=True)
            return (x - m) * jax.lax.rsqrt(v + eps) * g + b
        b, t, d = x.shape
        q = jnp.einsum('btd,hdf->bhtf', x, Wq)
        k = jnp.einsum('btd,hdf->bhtf', x, Wk)
        v = jnp.einsum('btd,hdf->bhtf', x, Wv)
        wei = jnp.einsum('bhtf,bhsf->bhts', q, k) * d ** (-0.5)
        mask = jnp.tril(jnp.ones((t, t), bool))
        wei = jnp.where(mask, wei, -jnp.inf)
        wei = jax.nn.softmax(wei, axis=-1)
        attn = jnp.einsum('bhts,bhsf->bhtf', wei, v)
        attn = attn.transpose(0, 2, 1, 3).reshape(b, t, d)
        y = x + layernorm(attn, ln1_g, ln1_b)
        flat = y.reshape(-1, d)
        logits = flat @ gate_W
        topv, topi = jax.lax.top_k(logits, K)
        w = jax.nn.softmax(topv, axis=-1)
        combine = jnp.sum(jax.nn.one_hot(topi, E, dtype=flat.dtype) * w[..., None], axis=1)
        h = jax.nn.relu(jnp.einsum('nd,edf->enf', flat, W1) + b1[:, None, :])
        eo = jnp.einsum('enf,efd->end', h, W2) + b2[:, None, :]
        moe = jnp.einsum('ne,end->nd', combine, eo)
        out = y + layernorm(moe.reshape(b, t, d), ln2_g, ln2_b)
        return out
    x = x + _L0_attn_ref(_layernorm(x, axis=-1), L0_attn_qkv_w, L0_attn_qkv_b, L0_attn_qn_scale, L0_attn_qn_bias, L0_attn_kn_scale, L0_attn_kn_bias, L0_attn_ttt_gate, L0_attn_ttt_val, L0_attn_ttt_proj, L0_attn_proj_w, L0_attn_proj_b)
    x = x + _L0_xattn_ref(_layernorm(x, axis=-1), ctx_1024, ctx_1024, L0_xattn_Wq, L0_xattn_bq, L0_xattn_Wk, L0_xattn_bk, L0_xattn_Wv, L0_xattn_bv, L0_xattn_Wo, L0_xattn_bo)
    x = x + _L0_ffn_ref(_layernorm(x, axis=-1), L0_ffn_w_up, L0_ffn_w_down)
    x = x + _L1_attn_ref(_layernorm(x, axis=-1), L1_attn_Wc, L1_attn_bc, L1_attn_Wo, L1_attn_bo)
    x = x + _L1_xattn_ref(ctx_1024, _layernorm(x, axis=-1), L1_xattn_Wq, L1_xattn_Wkv, L1_xattn_Wout, L1_xattn_gm, L1_xattn_bm, L1_xattn_gl, L1_xattn_bl)
    x = x + _L1_ffn_ref(_layernorm(x, axis=-1), L1_ffn_Wq, L1_ffn_Wk, L1_ffn_Wv, L1_ffn_gate_W, L1_ffn_W1, L1_ffn_b1, L1_ffn_W2, L1_ffn_b2, L1_ffn_ln1_g, L1_ffn_ln1_b, L1_ffn_ln2_g, L1_ffn_ln2_b)
    return x

_drawn_inputs = setup_inputs


def setup_inputs(seed=0):
    import zlib

    import numpy as np

    out = dict(_drawn_inputs(seed))
    spreads = {'L0_attn_qkv_b': (0.0, 0.57),
     'L0_attn_qn_scale': (1.0, 0.6),
     'L0_attn_qn_bias': (0.0, 0.334),
     'L0_attn_kn_scale': (1.0, 0.6),
     'L0_attn_kn_bias': (0.0, 0.676),
     'L0_attn_proj_b': (0.0, 0.1),
     'L0_xattn_bq': (0.0, 0.327),
     'L0_xattn_bk': (0.0, 2.0),
     'L0_xattn_bv': (0.0, 0.1),
     'L0_xattn_bo': (0.0, 0.1),
     'L1_attn_bc': (0.0, 2.0),
     'L1_attn_bo': (0.0, 2.0),
     'L1_xattn_gm': (1.0, 0.6),
     'L1_xattn_bm': (0.0, 0.789),
     'L1_xattn_gl': (1.0, 0.2),
     'L1_xattn_bl': (0.0, 0.401),
     'L1_ffn_b1': (0.0, 0.696),
     'L1_ffn_b2': (0.0, 0.326),
     'L1_ffn_ln1_g': (1.0, 0.6),
     'L1_ffn_ln1_b': (0.0, 0.701),
     'L1_ffn_ln2_g': (1.0, 0.6),
     'L1_ffn_ln2_b': (0.0, 0.8)}
    factors = {'L1_attn_Wc': 64.0, 'L1_attn_Wo': 8.0, 'L1_ffn_Wq': 27.001, 'L1_ffn_Wk': 26.21}
    for name, (base, spread) in spreads.items():
        noise = np.random.default_rng([zlib.crc32(name.encode()), seed]).standard_normal(out[name].shape)
        drawn = base * np.exp(spread * noise) if base else spread * noise
        out[name] = jnp.asarray(drawn.astype(out[name].dtype))
    for name, factor in factors.items():
        out[name] = (out[name] * factor).astype(out[name].dtype)
    return out
```

```python
import numpy as np
import concourse.bass as bass
from concourse import mybir
from contextlib import ExitStack

F32 = mybir.dt.float32
BF16 = mybir.dt.bfloat16
U32 = mybir.dt.uint32
ALU = mybir.AluOpType
ACT = mybir.ActivationFunctionType
AX = mybir.AxisListType

BATCH, SEQ, D = 4, 512, 128
P = 128
QT = SEQ // P
TILES = BATCH * QT
CTX = 77
HEADS, HD = 16, 8
GROUPS, LANE = 4, 32
HID = 512
M = HID // P
STEPS, NS_ITERS, LR = 2, 5, 0.1
NS_A, NS_B, NS_C = 3.4445, -4.775, 2.0315
VD = 64
XH, XD = 8, 64
XK = SEQ + CTX
E = 8
LN_EPS = 1e-5
SLOPE = 0.01
MASKED = -3.0e38


def decoder_kernel(nc, x, ctx_1024, qkv_w, qkv_b, qn_scale, qn_bias, kn_scale, kn_bias, ttt_gate, ttt_val,
                   ttt_proj, proj_w, proj_b, x0_Wq, x0_bq, x0_Wk, x0_bk, x0_Wv, x0_bv, x0_Wo, x0_bo, w_up, w_down,
                   a1_Wc, a1_bc, a1_Wo, a1_bo, x1_Wq, x1_Wkv, x1_Wout, x1_gm, x1_bm, x1_gl, x1_bl,
                   f1_Wq, f1_Wk, f1_Wv, f1_gate, f1_W1, f1_b1, f1_W2, f1_b2, f1_g1, f1_c1, f1_g2, f1_c2, out):
    stack = ExitStack()
    with stack:
        def sb(name, shape, dt=F32):
            return stack.enter_context(nc.sbuf_tensor(name, shape, dt))

        def sem(name):
            return stack.enter_context(nc.semaphore(name))

        X = sb("X", [P, TILES, D])
        ident = sb("ident", [P, P])
        ones = sb("ones", [P, P])
        ident_bf = sb("ident_bf", [P, P], BF16)
        causal_bf = sb("causal_bf", [P, P], BF16)
        head_mask = sb("head_mask", [P, HEADS])
        half_mask = sb("half_mask", [P, 2])
        iota8 = sb("iota8", [P, E])
        iota_i = sb("iota_i", [P, E], mybir.dt.int32)
        neg_half = sb("neg_half", [P, 8])
        pos_half = sb("pos_half", [P, P])
        W0T = sb("W0T", [P, 3, D])
        WoA = sb("WoA", [P, GROUPS, D])
        SEL = sb("SEL", [P, GROUPS, D])
        upT = sb("upT", [P, HID])
        downT = sb("downT", [P, M, D])
        WcT = sb("WcT", [P, 1280])
        Wo1T = sb("Wo1T", [P, 8, D])
        Wq1 = sb("Wq1", [P, 512])
        Wkv1 = sb("Wkv1", [P, 1024])
        Wout1 = sb("Wout1", [P, 4, D])
        WF = sb("WF", [P, 3, HEADS, HD])
        gateW = sb("gateW", [P, E])
        W1 = sb("W1", [P, E, HID])
        W2 = sb("W2", [P, E, M, D])
        b2r = sb("b2r", [E, D])
        NVEC = 44
        vrow = sb("vrow", [NVEC, P])
        V = sb("V", [P, NVEC])
        vs = sb("vs", [P, 2])
        bc = sb("bc", [P, 7, D])
        BV0, BO0, BO1, G1, C1, G2, C2 = range(7)
        bcv = sb("bcv", [P, 1024])
        CT_all = sb("CT_all", [P, BATCH, CTX])
        CN_all = sb("CN_all", [P, BATCH, CTX])

        PTA = sb("PTA", [P, 10240])
        OTA = sb("OTA", [P, 4096])
        KMA = sb("KMA", [P, 8 * 592])
        VA = sb("VA", [P, 4096])
        VPA = sb("VPA", [P, 2048])
        QXA = sb("QXA", [P, 2048])
        PB = sb("PB", [P, 2, 640])
        YN = sb("YN", [P, QT, D])
        Y2 = sb("Y2", [P, QT, D])
        YT = sb("YT", [P, SEQ])
        YF = sb("YF", [P, QT, D])
        CT = sb("CT", [P, CTX])
        CN = sb("CN", [P, CTX])
        st = sb("st", [P, QT, 6])
        mv = sb("mv", [P, QT, 2])
        var = sb("var", [P, QT])
        rstd = sb("rstd", [P, QT])
        nmax = sb("nmax", [P, 2, 4])
        rsum = sb("rsum", [P, 2, 4])
        rinv = sb("rinv", [P, 2, 4])
        sm = sb("sm", [P, 64])

        w0raw = VPA[:, 0:512].rearrange("p (w d) -> p w d", w=4)
        wo0pad = VPA[:, 512:1024].rearrange("p (j g c) -> p j g c", j=4, g=4)
        idpad = VPA[:, 1024:1536].rearrange("p (j g c) -> p j g c", j=4, g=4)
        upraw = QXA[:, 0:512]
        downraw = QXA[:, 512:1024]
        ctxraw = QXA[:, 1024:1536].rearrange("p (b d) -> p b d", b=4)
        ctxn = QXA[:, 1536:2048].rearrange("p (b d) -> p b d", b=4)
        wcraw = PTA[:, 0:1280]
        wo1raw = PTA[:, 1280:2304]
        tern = PTA[:, 2304:3328].rearrange("p (w n) -> p w n", w=2)
        ternq = PTA[:, 3328:4352].rearrange("p (w n) -> p w n", w=2)
        wqkv = KMA[:, 0:384]
        gate = KMA[:, 384:896]
        val = KMA[:, 896:1408]
        proj = KMA[:, 1408:1920].rearrange("p (m d) -> p m d", m=M)
        projT = KMA[:, 1920:2432]
        pw = KMA[:, 2432:2560]
        bqkv = KMA[:, 2560:2944]
        kscale8 = KMA[:, 2944:2952]
        kbias8 = KMA[:, 2952:2960]
        kscale = KMA[:, 2960:3088]
        kbias = KMA[:, 3088:3216]
        bproj = KMA[:, 3456:3584]
        normw = KMA[:, 3584:3840]
        QTall = OTA[:, 0:2048]
        Kn = PTA[:, 0:2048].rearrange("p (t d) -> p t d", d=D)
        KTall = PTA[:, 2048:4096]
        Vn = PTA[:, 4096:6144].rearrange("p (t d) -> p t d", d=D)
        sg = [VA[:, 0:512], VA[:, 512:1024]]
        t1 = [VA[:, 1024:1536], VA[:, 1536:2048]]
        us = [VA[:, 2048:2560], VA[:, 2560:3072]]
        dg = VA[:, 3072:3584]
        du = VA[:, 3584:4096]
        hh = [OTA[:, 2048:2560], OTA[:, 2560:3072]]
        ww = [OTA[:, 3072:3584], OTA[:, 3584:4096]]
        zz = VPA[:, 512:1024]
        hTs = QXA[:, 0:512]
        dp = QXA[:, 512:640]
        dpT = QXA[:, 640:768]
        nx = [PTA[:, 6144 + 512 * i:6656 + 512 * i] for i in range(3)]
        nxT = [PTA[:, 7680 + 512 * i:8192 + 512 * i] for i in range(3)]
        nA = [QXA[:, 1024 + 128 * i:1152 + 128 * i] for i in range(3)]
        nB = [QXA[:, 1408 + 128 * i:1536 + 128 * i] for i in range(3)]
        nC = [VPA[:, 128 * i:128 * i + 128] for i in range(3)]
        aI = VPA[:, 384:512]

        qkvs = VA[:, 0:1024].rearrange("p (t w d) -> p t w d", t=QT, w=2)
        kraw = VA[:, 1024:1536].rearrange("p (t d) -> p t d", t=QT)
        sq4 = VA[:, 2048:3072]
        fh = VA[:, 0:2048].rearrange("p (m n) -> p m n", m=M)
        foT = VA[:, 2048:2560]
        fsg = VA[:, 2560:3584].rearrange("p (k n) -> p k n", k=2)
        ft = VPA[:, 512:1536].rearrange("p (k n) -> p k n", k=2)

        PSUM = stack.enter_context(nc.psum_tensor("PSUM", [P, 8, 512], F32))

        def bank(i, n=512):
            return PSUM[:, i, 0:n]

        s_x, s_w0, s_wt, s_wr, s_out = (sem(n) for n in ("x_loaded", "raw_loaded", "ttt_loaded", "rest_loaded", "stored"))
        s_const = sem("consts_ready")
        s_pad, s_absum, s_thr, s_tern = (sem(n) for n in ("pads_ready", "abs_sums", "abs_total", "ternary_ready"))
        s_tr, s_ev = sem("prep_transposed"), sem("prep_evacuated")

        class Norm:
            def __init__(self, name):
                self.var, self.rstd, self.done = sem(name + "_var"), sem(name + "_rstd"), sem(name + "_done")

        n_ctx, n_in, n_b = Norm("ctx_ln"), Norm("in_ln"), Norm("batch_ln")

        def ln_vector(dve, norm, n, srcs, dsts, rows=P):
            for j, s in enumerate(srcs):
                nc.vector.bn_stats(st[0:rows, j, :], s)
            dve.drain()
            for j in range(len(srcs)):
                nc.vector.bn_aggr(mv[0:rows, j, :], st[0:rows, j, :])
            dve.drain()
            k = len(srcs)
            nc.vector.tensor_scalar(var[0:rows, 0:k], mv[0:rows, 0:k, 1], LN_EPS, None, ALU.add).then_inc(norm.var, 1)
            dve.wait_ge(norm.rstd, n)
            for j, (s, d) in enumerate(zip(srcs, dsts)):
                last = nc.vector.tensor_scalar(d, s, mv[0:rows, j, 0:1], rstd[0:rows, j:j + 1],
                                               ALU.subtract, ALU.mult)
            last.then_inc(norm.done, 1)

        def ln_pool(pool, norm, n, rows=P, k=QT):
            pool.wait_ge(norm.var, n)
            nc.gpsimd.tensor_tensor(rstd[0:rows, 0:k], var[0:rows, 0:k], neg_half[0:rows, 0:k], ALU.pow)\
                .then_inc(norm.rstd, 1)

        prep = []

        def group(srcs, dst, rows=P, after=None):
            prep.append((srcs, dst, rows, after))

        group([vrow[:, :]], V[:, :], NVEC, None)
        group([w0raw[:, i, :] for i in range(3)], W0T[:, :, :])
        group([ttt_tile for ttt_tile in (proj[:, m, :] for m in range(M))], projT)
        group([wcraw[:, i * P:(i + 1) * P] for i in range(0, 4)], WcT[:, 0:512])
        group([wcraw[:, i * P:(i + 1) * P] for i in range(4, 8)], WcT[:, 512:1024])
        group([wcraw[:, i * P:(i + 1) * P] for i in range(8, 10)], WcT[:, 1024:1280])
        group([wo1raw[:, i * P:(i + 1) * P] for i in range(0, 4)], Wo1T[:, 0:4, :])
        group([wo1raw[:, i * P:(i + 1) * P] for i in range(4, 8)], Wo1T[:, 4:8, :])
        group([ctxraw[0:CTX, b, :] for b in range(BATCH)], CT_all[:, :, :], CTX)
        group([wo0pad[:, j, :, :] for j in range(4)], WoA[:, :, :], P, "pads")
        group([idpad[:, j, :, :] for j in range(4)], SEL[:, :, :], P, "pads")
        group([ctxn[0:CTX, b, :] for b in range(BATCH)], CN_all[:, :, :], CTX, "ctx")
        group([ternq[:, 0, i * P:(i + 1) * P] for i in range(4)], upT[:, :], P, "tern")
        group([ternq[:, 1, i * P:(i + 1) * P] for i in range(4)], downT[:, :, :], P, "tern")
        NPREP = len(prep)

        NLN = 8
        NTR = 6
        s_zero = sem("value_pads_zero")
        s_ctx = sem("context_row_ready")
        s_bT, s_bTs = sem("rows_transposed"), sem("rows_T_ready")
        s_pow, s_powd = sem("square_sums_ready"), sem("roots_ready")
        s_rowdone = sem("row_done")

        (s_scores, s_max, s_exp, s_norm, s_turned, s_moved, s_values, s_outs) = (
            sem(w) for w in ("scores_ready", "maxima_ready", "exp_ready", "probs_normalised", "probs_turned", "probs_T_ready",
                             "values_ready", "values_copied"))

        class Attention:
            all_units, all_groups = 16 + 64 + 32 + 64, 4 + 8 + 4 + 4

            def __init__(self, before, units, group, out_banks, free):
                self.units, self.group, self.out_banks, self.free = units, group, out_banks, free
                self.groups = units // group
                self.first_unit = before.first_unit + before.units if before else 0
                self.first_group = before.first_group + before.groups if before else 0

            def unit(self, b, i):
                return b * self.all_units + (self.first_unit + i)

            def summed(self, b, v):
                return b * self.all_groups + (self.first_group + v)

        def attention_tensor(pe, b, a, score, turn, value):
            U = a.units

            def values(v):
                pe.wait_ge(s_moved, a.unit(b, (v + 1) * a.group))
                if v >= a.out_banks:
                    pe.wait_ge(s_outs, a.summed(b, v + 1 - a.out_banks))
                value(v).then_inc(s_values, 1)

            for i in range(U + 2):
                if i < U:
                    if i >= 2:
                        pe.wait_ge(s_exp, a.unit(b, i - 1))
                    score(i).then_inc(s_scores, 1)
                k = i - 2
                if k >= 0:
                    pe.wait_ge(s_norm, a.unit(b, k + 1))
                    if k >= 2:
                        pe.wait_ge(s_moved, a.unit(b, k - 1))
                    turn(k).then_inc(s_turned, 1)
                    if k >= a.group and k % a.group == 1:
                        values(k // a.group - 1)
            values(a.groups - 1)

        def attention_scalar(act, b, a, exp, move):
            U = a.units
            for i in range(U + 2):
                if i < U:
                    act.wait_ge(s_max, a.unit(b, i + 1))
                    if i >= 2:
                        act.wait_ge(s_turned, a.unit(b, i - 1))
                    exp(i).then_inc(s_exp, 1)
                k = i - 2
                if k >= 0:
                    act.wait_ge(s_turned, a.unit(b, k + 1))
                    if a.free(k):
                        act.wait_ge(s_values, a.summed(b, a.free(k)))
                    move(k).then_inc(s_moved, 1)

        def attention_vector(dve, b, a, maximum, normalise, copy_out):
            U = a.units

            def out_of(v):
                dve.wait_ge(s_values, a.summed(b, v + 1))
                copy_out(v).then_inc(s_outs, 1)

            done = 0
            for i in range(U + 1):
                if i < U:
                    dve.wait_ge(s_scores, a.unit(b, i + 1))
                    maximum(i).then_inc(s_max, 1)
                if i >= 1:
                    dve.wait_ge(s_exp, a.unit(b, i))
                    normalise(i - 1).then_inc(s_norm, 1)
                if i == a.group * (done + 1) + 4:
                    out_of(done)
                    done += 1
            for v in range(done, a.groups):
                out_of(v)

        GH = GROUPS
        a0 = Attention(None, 16, 4, 2, lambda k: k // 4 - 1 if k % 4 == 0 and k >= 8 else 0)
        a1 = Attention(a0, 64, 8, 2, lambda k: (k // 4 - 4) // 2 + 1 if k % 4 == 0 and k >= 16 else 0)
        ax = Attention(a1, 32, 8, 1, lambda k: (k // 4 - 4) // 2 + 1 if k % 4 == 0 and k >= 16 else 0)
        af = Attention(ax, 64, 16, 2, lambda k: (k // 4 - 5) // 4 + 1 if k % 4 == 0 and k >= 20 else 0)

        s_b_k, s_b_v, s_b_q, s_b_ks, s_b_vs, s_b_qs, s_b_km, s_b_o = (sem("x0_" + n) for n in (
            "k", "v", "q", "k_biased", "v_biased", "q_scaled", "k_masked", "out"))
        s_c_u, s_c_g, s_c_r1, s_c_T, s_c_Ts, s_c_o, s_c_x = (sem("ffn_" + n) for n in (
            "up", "gelu", "rms", "turned", "moved", "down", "added"))
        s_d_q, s_d_qb, s_d_qs, s_d_v, s_d_vs, s_d_km, s_d_o = (sem("a1_" + n) for n in (
            "qk", "qk_biased", "qk_ready", "v", "v_ready", "k_masked", "out"))
        s_e_q, s_e_qs, s_e_k, s_e_ks, s_e_v, s_e_vs, s_e_o = (sem("x1_" + n) for n in (
            "q", "q_ready", "k", "k_masked", "v", "v_ready", "out"))
        s_f_q, s_f_qs, s_f_v, s_f_vs, s_f_km, s_f_o, s_f_y, s_f_g, s_f_gs, s_f_d, s_f_e, s_f_c, s_f_cT, s_f_cTs, s_f_b2, s_f_acc0 = (
            sem("f1_" + n) for n in ("qk", "qk_ready", "v", "v_ready", "k_masked", "attn", "y_ready", "gate", "logits",
                                     "top_gap", "top_exp", "combine", "combine_turned", "combine_T", "b2", "acc_started"))
        s_f_h, s_f_hs, s_f_dn, s_f_acc = (sem("moe_" + n) for n in ("hidden", "relu", "down", "added"))

        PSF = PSUM[:, :, :].rearrange("p b n -> p (b n)")
        VP = VPA[:, :].rearrange("p (t h c) -> p t h c", t=QT, h=HEADS)
        QS = QXA[:, 0:512]
        Qraw = QXA[:, 512:1024]
        Kraw = QXA[:, 1024:1536]
        KT0 = QXA[:, 1536:2048]
        KM0 = KMA[:, 0:HEADS * CTX].rearrange("p (h k) -> p h k", h=HEADS)
        KMr = KMA[:, 0:8 * 512].rearrange("p (h k) -> p h k", h=8)
        KM8 = KMA[:, :].rearrange("p (h k) -> p h k", h=8)
        PT0 = PTA[:, 0:4096].rearrange("p (r g q) -> p r g q", r=2, g=4)
        PTd = PTA[:, :].rearrange("p (r k q) -> p r k q", r=5, k=4)
        PTe = PTA[:, :].rearrange("p (r k q) -> p r k q", r=4, k=5)
        OT = OTA[:, :].rearrange("p (g q) -> p g q", q=SEQ)
        V1 = VA[:, :].rearrange("p (k n) -> p k n", k=QT)
        VX = VA[:, 0:2560].rearrange("p (k n) -> p k n", k=5)
        HC = VA[:, 0:2048].rearrange("p (t n) -> p t n", t=QT)
        HTC = PTA[:, 0:2048].rearrange("p (t n) -> p t n", t=QT)
        HE = PTA[:, 0:4096].rearrange("p (r m n) -> p r m n", r=2, m=M)
        QX = QXA[:, :].rearrange("p (g q) -> p g q", q=SEQ)
        ssq = sb("ssq", [P, 2, QT])
        root = sb("root", [P, 2, QT])
        logit = sb("logit", [P, QT, E])
        top = sb("top", [P, QT, E])
        topi = sb("topi", [P, QT, E], U32)
        topf = sb("topf", [P, QT, E])
        comb = sb("comb", [P, QT, E])
        comb2 = sb("comb2", [P, QT, E])
        tw = sb("tw", [P, 4, QT])
        combT = QXA[0:E, 512:1024]

        GM, BM, GL, BL, BQ0, BK0, BCQ, BCK = range(8)
        B1C = 8
        QSC, QBI, KSC, KBI = range(40, 44)

        block = stack.enter_context(nc.Block())

        s_yT, s_yTs = sem("in_transposed"), sem("in_yT_ready")
        s_qkv, s_qkvb, s_ss, s_nrm, s_qk = (sem(n) for n in ("qkv_ready", "qkv_biased", "head_sums", "head_norms", "qk_ready"))
        s_qkT, s_qkTs, s_kn, s_sqr, s_uc = (sem(n) for n in ("qk_transposed", "qkT_stored", "k_stored", "qk_squared", "value_copied"))
        s_gu, s_sig, s_t, s_h, s_w = (sem(n) for n in ("gu_ready", "sigmoid_ready", "silu_ready", "h_ready", "w_ready"))
        s_hT, s_hTs, s_pred, s_dp, s_dpT, s_dpTs, s_dh, s_dgu = (sem(n) for n in (
            "hT_ready", "hT_stored", "pred_ready", "dpred_ready", "dpredT_ready", "dpredT_stored", "dh_ready", "dgu_ready"))
        s_grad, s_gs, s_sq, s_tot, s_tots, s_nrt, s_x0 = (sem(n) for n in (
            "grads_ready", "grads_stored", "square_sums", "square_total", "total_stored", "norm_ready", "x_scaled"))
        s_xt0, s_xt0s = sem("ns_xT_ready"), sem("ns_xT_stored")
        s_A, s_As, s_A2, s_B, s_XN, s_XTN, s_XNs, s_XTNs, s_upd = (sem(n) for n in (
            "ns_A", "ns_A_stored", "ns_A2", "ns_B", "ns_X", "ns_XT", "ns_X_stored", "ns_XT_stored", "weights_updated"))
        s_fg, s_fu, s_fs, s_ft, s_fh, s_fo, s_fos, s_fy, s_fx = (sem(n) for n in (
            "f_gate", "f_val", "f_sigmoid", "f_silu", "f_h", "f_o", "f_oT", "f_y", "f_x"))

        @block.sync
        def _(sp):
            def load(dst, src, s):
                sp.dma_start(dst, src).then_inc(s, 16)

            load(X[:, :, :], x.rearrange("b (t p) d -> p (b t) d", p=P), s_x)
            for i, w in enumerate((x1_gm, x1_bm, x1_gl, x1_bl, x0_bq, x0_bk)):
                load(vrow[i:i + 1, :], w.rearrange("(o d) -> o d", o=1), s_w0)
            load(vrow[6:8, :], a1_bc[0:256].rearrange("(o d) -> o d", o=2), s_w0)
            load(vrow[8:40, :], f1_b1.rearrange("e (m d) -> (e m) d", d=D), s_w0)
            for i, w in enumerate((qn_scale, qn_bias, kn_scale, kn_bias)):
                load(vrow[40 + i:41 + i, :].rearrange("o (h d) -> o h d", d=HD),
                     w.rearrange("(o d) -> o d", o=1).unsqueeze(1).to_broadcast([1, HEADS, HD]), s_w0)
            for i, w in enumerate((x0_Wq, x0_Wk, x0_Wv, x0_Wo)):
                load(w0raw[:, i, :], w, s_w0)
            load(proj, ttt_proj.rearrange("(m p) d -> p m d", p=P), s_w0)
            load(wcraw.rearrange("p (t d) -> p t d", d=D), a1_Wc.rearrange("(t p) d -> p t d", p=P), s_w0)
            load(wo1raw, a1_Wo, s_w0)
            load(ctxraw[0:CTX, :, :], ctx_1024.rearrange("b s d -> s b d"), s_w0)
            load(upraw.rearrange("p (t d) -> p t d", d=D), w_up.rearrange("(t p) d -> p t d", p=P), s_w0)
            load(downraw, w_down, s_w0)
            load(wqkv, qkv_w, s_wt)
            load(gate, ttt_gate, s_wt)
            load(val, ttt_val, s_wt)
            load(pw, proj_w, s_wt)
            load(bqkv, qkv_b.partition_broadcast(P), s_wt)
            load(bproj, proj_b.partition_broadcast(P), s_wt)
            load(kscale8, kn_scale.partition_broadcast(P), s_wt)
            load(kbias8, kn_bias.partition_broadcast(P), s_wt)
            for i, w in enumerate((x0_bv, x0_bo, a1_bo, f1_g1, f1_c1, f1_g2, f1_c2)):
                load(bc[:, i, :], w.partition_broadcast(P), s_wr)
            load(bcv[:, :], a1_bc[256:1280].partition_broadcast(P), s_wr)
            load(Wq1[:, :], x1_Wq, s_wr)
            load(Wkv1[:, :], x1_Wkv, s_wr)
            load(Wout1[:, :, :], x1_Wout.rearrange("(m p) d -> p m d", p=P), s_wr)
            for i, w in enumerate((f1_Wq, f1_Wk, f1_Wv)):
                load(WF[:, i, :, :], w.rearrange("h d f -> d h f"), s_wr)
            load(gateW[:, :], f1_gate, s_wr)
            load(b2r[:, :], f1_b2, s_wr)
            load(W1[:, :, :], f1_W1.rearrange("e d f -> d e f"), s_wr)
            load(W2[:, :, :, :].rearrange("p e m d -> p (e m) d"), f1_W2.rearrange("e (m p) d -> p (e m) d", p=P), s_wr)
            with sp.Fori(0, BATCH) as b:
                sp.wait_ge(s_rowdone, b + 1)
                sp.dma_start(out[bass.ds(b, 1), :, :].rearrange("o (t p) d -> p (o t) d", p=P),
                             X[:, bass.ds(b * QT, QT), :]).then_inc(s_out, 16)
            sp.wait_ge(s_out, 16 * BATCH)

        N_W0, N_WT, N_WR = 16 * 22, 16 * 8, 16 * 18

        @block.gpsimd
        def _(pool):
            g = nc.gpsimd
            g.memset(ident[:, :], 0.0)
            g.memset(ones[:, :], 1.0)
            g.memset(head_mask[:, :], 1.0)
            g.memset(half_mask[:, :], 0.0)
            g.memset(causal_bf[:, :], 0.0)
            g.memset(neg_half[:, :], -0.5)
            g.memset(pos_half[:, :], 0.5)
            g.memset(VPA[:, 512:1536], 0.0)
            g.iota(iota_i[:, :], pattern=[[1, E]], base=0, channel_multiplier=0)
            pool.drain()
            g.tensor_copy(iota8[:, :], iota_i[:, :])
            g.memset(half_mask[0:64, 0:1], 1.0)
            pool.drain()
            g.memset(half_mask[64:128, 1:2], 1.0)
            pool.drain()
            g.affine_select(out=ident[:, :], in_=ident[:, :], compare_op=ALU.not_equal, fill=1.0, base=0,
                            pattern=[[-1, P]], channel_multiplier=1)
            g.affine_select(out=head_mask[:, :], in_=head_mask[:, :], compare_op=ALU.is_ge, fill=0.0, base=0,
                            pattern=[[-HD, HEADS]], channel_multiplier=1)
            g.affine_select(out=causal_bf[:, :], in_=causal_bf[:, :], compare_op=ALU.is_ge, fill=MASKED, base=0,
                            pattern=[[-1, P]], channel_multiplier=1)
            pool.drain()
            g.affine_select(out=head_mask[:, :], in_=head_mask[:, :], compare_op=ALU.is_ge, fill=0.0, base=HD - 1,
                            pattern=[[HD, HEADS]], channel_multiplier=-1)
            g.tensor_copy(ident_bf[:, :], ident[:, :])
            g.tensor_scalar(idpad[:, :, :, 0:HD], ident[:, :].rearrange("p (j g c) -> p j g c", j=4, g=4),
                            1.0, None, ALU.mult).then_inc(s_const, 1)
            pool.wait_ge(s_const, 1)
            pool.wait_ge(s_w0, N_W0)
            g.tensor_copy(wo0pad[:, :, :, 0:HD], w0raw[:, 3, :].rearrange("p (j g c) -> p j g c", j=4, g=4))\
                .then_inc(s_pad, 1)
            ln_pool(pool, n_ctx, 1, CTX)
            with pool.Fori(0, BATCH) as c:
                ln_pool(pool, n_in, c + 1)
            with pool.Fori(0, STEPS) as step:
                for t in range(TILES):
                    n, par = step * TILES + t, t % 2
                    pool.wait_ge(s_t, n + 1)
                    g.tensor_tensor(zz, sg[par], t1[par], ALU.mult)
                    if t >= 2:
                        pool.wait_ge(s_dgu, n - 1)
                    g.tensor_tensor(ww[par], sg[par], t1[par], ALU.add)
                    pool.drain()
                    g.tensor_tensor(ww[par], ww[par], zz, ALU.subtract)
                    pool.drain()
                    pool.wait_ge(s_uc, n + 1)
                    g.tensor_tensor(ww[par], ww[par], us[par], ALU.mult).then_inc(s_w, 1)
                pool.wait_ge(s_tots, step + 1)
                g.tensor_tensor(sm[:, 8:11], sm[:, 4:7], pos_half[:, 0:3], ALU.pow).then_inc(s_nrt, 1)


            with pool.Fori(0, BATCH) as b:
                g.tensor_copy(CT[:, :], CT_all[:, bass.ds(b, 1), :].rearrange("p o s -> p (o s)"))
                g.tensor_copy(CN[:, :], CN_all[:, bass.ds(b, 1), :].rearrange("p o s -> p (o s)")).then_inc(s_ctx, 1)
                ln = iter(range(1, NLN + 1))

                def norm():
                    ln_pool(pool, n_b, b * NLN + next(ln))

                def masked_keys(a, s_in, n_in_, s_out_, after):
                    for h in range(HEADS):
                        if h == 0:
                            pool.wait_ge(s_in, n_in_)
                        if h >= 8:
                            pool.wait_ge(s_scores, a.unit(b, 4 * (h - 8) + 4))
                        g.tensor_tensor(KMr[:, h % 8, :], KT0, head_mask[:, h:h + 1].to_broadcast([P, SEQ]), ALU.mult)\
                            .then_inc(s_out_, 1)

                norm()
                norm()
                for i in range(2):
                    pool.wait_ge(s_pow, 2 * b + i + 1)
                    g.tensor_tensor(root[:, i, :], ssq[:, i, :], pos_half[:, 0:QT], ALU.pow).then_inc(s_powd, 1)
                norm()
                masked_keys(a1, s_d_qs, 2 * b + 2, s_d_km, None)
                norm()
                norm()
                norm()
                masked_keys(af, s_f_qs, 2 * b + 2, s_f_km, None)
                norm()
                norm()
                pool.wait_ge(s_rowdone, b + 1)

        @block.tensor
        def _(pe):
            T = nc.tensor
            pe.wait_ge(s_const, 1)
            pe.wait_ge(s_w0, N_W0)
            pe.wait_ge(s_absum, 1)
            T.matmul(bank(7, 2), ones[:, :], sm[:, 0:2], start=True, stop=True).then_inc(s_thr, 1)
            for i, (srcs, dst, rows, after) in enumerate(prep):
                if after == "pads":
                    pe.wait_ge(s_pad, 1)
                if after == "ctx":
                    pe.wait_ge(n_ctx.done, 1)
                if after == "tern":
                    pe.wait_ge(s_tern, 1)
                if i >= 7:
                    pe.wait_ge(s_ev, i - 6)
                for j, s in enumerate(srcs):
                    last = T.transpose(PSUM[:, i % 7, j * rows:(j + 1) * rows], s, ident[0:rows, 0:rows])
                last.then_inc(s_tr, 1)
            pe.wait_ge(s_ev, NPREP)
            pe.wait_ge(s_wt, N_WT)
            with pe.Fori(0, BATCH) as c:
                pe.wait_ge(n_in.done, c + 1)
                for j in range(QT):
                    last = T.transpose(PSUM[:, 0, j * P:(j + 1) * P], YN[:, j, :], ident[:, :])
                last.then_inc(s_yT, 1)
                pe.wait_ge(s_yTs, c + 1)
                for j in range(QT):
                    T.matmul(PSUM[:, 1 + j, 0:384], YT[:, j * P:(j + 1) * P], wqkv, start=True, stop=True)\
                        .then_inc(s_qkv, 1)
                for w in range(2):
                    pe.wait_ge(s_qk, c + 1)
                    for j in range(QT):
                        last = T.transpose(PSUM[:, 5 + w, j * P:(j + 1) * P], qkvs[:, j, w, :], ident[:, :])
                    last.then_inc(s_qkT, 1)
            pe.wait_ge(s_qkTs, 2 * BATCH)
            pe.wait_ge(s_kn, BATCH)

            with pe.Fori(0, STEPS) as step:
                def gate_val(t):
                    T.matmul(bank(0), KTall[:, t * P:(t + 1) * P], gate, start=True, stop=True)
                    T.matmul(bank(1), KTall[:, t * P:(t + 1) * P], val, start=True, stop=True).then_inc(s_gu, 1)

                def up_grads(t):
                    pe.wait_ge(s_dgu, step * TILES + t + 1)
                    T.matmul(bank(5), Kn[:, t, :], dg, start=(t == 0), stop=(t == TILES - 1))
                    return T.matmul(bank(6), Kn[:, t, :], du, start=(t == 0), stop=(t == TILES - 1))

                gate_val(0)
                for t in range(TILES):
                    n, par = step * TILES + t, t % 2
                    pe.wait_ge(s_h, n + 1)
                    for m in range(M):
                        last = T.transpose(PSUM[:, 2, m * P:(m + 1) * P], hh[par][:, m * P:(m + 1) * P], ident[:, :])
                    last.then_inc(s_hT, 1)
                    if t + 1 < TILES:
                        pe.wait_ge(s_uc, n + 1)
                        gate_val(t + 1)
                    if t:
                        up_grads(t - 1)
                    pe.wait_ge(s_hTs, n + 1)
                    for m in range(M):
                        last = T.matmul(bank(3, P), hTs[:, m * P:(m + 1) * P], proj[:, m, :], start=(m == 0), stop=(m == M - 1))
                    last.then_inc(s_pred, 1)
                    pe.wait_ge(s_dp, n + 1)
                    T.transpose(PSUM[:, 3, 128:256], dp, ident[:, :]).then_inc(s_dpT, 1)
                    T.matmul(bank(7), dp, hh[par], start=(t == 0), stop=(t == TILES - 1))
                    pe.wait_ge(s_dpTs, n + 1)
                    T.matmul(bank(4), dpT, projT, start=True, stop=True).then_inc(s_dh, 1)
                up_grads(TILES - 1).then_inc(s_grad, 1)
                pe.wait_ge(s_sq, step + 1)
                T.matmul(bank(0, 3), ones[:, :], sm[:, 0:3], start=True, stop=True).then_inc(s_tot, 1)
                for i in range(3):
                    pe.wait_ge(s_x0, step * 3 + i + 1)
                    for m in range(M):
                        last = T.transpose(PSUM[:, 1 + i, m * P:(m + 1) * P], nx[i][:, m * P:(m + 1) * P], ident[:, :])
                    last.then_inc(s_xt0, 1)
                with pe.Fori(0, NS_ITERS) as it:
                    pe.wait_ge(s_xt0s, step * 3 + 3)
                    k = (step * NS_ITERS + it) * 3
                    for i in range(3):
                        for m in range(M):
                            last = T.matmul(PSUM[:, i, 0:P], nxT[i][:, m * P:(m + 1) * P], nxT[i][:, m * P:(m + 1) * P],
                                            start=(m == 0), stop=(m == M - 1))
                        last.then_inc(s_A, 1)
                    for i in range(3):
                        pe.wait_ge(s_As, k + i + 1)
                        T.matmul(PSUM[:, i, P:2 * P], nA[i], nA[i], start=True, stop=True).then_inc(s_A2, 1)
                    for i, (bx, bt) in enumerate(((3, 4), (5, 6), (7, 3))):
                        pe.wait_ge(s_B, k + i + 1)
                        T.matmul(bank(bx), nB[i], nx[i], start=True, stop=True).then_inc(s_XN, 1)
                        if i == 2:
                            pe.wait_ge(s_XNs, k + 1)
                        for m in range(M):
                            last = T.matmul(PSUM[:, bt, m * P:(m + 1) * P], nx[i][:, m * P:(m + 1) * P], nB[i],
                                            start=True, stop=True)
                        last.then_inc(s_XTN, 1)
                    pe.wait_ge(s_XNs, k + 3)
                    pe.wait_ge(s_XTNs, k + 3)
                pe.wait_ge(s_upd, step + 1)

            with pe.Fori(0, BATCH) as c:
                q = QTall[:, bass.ds(c * SEQ, SEQ)]
                for m in range(M):
                    n = c * M + m
                    if m >= 2:
                        pe.wait_ge(s_fh, n - 1)
                    T.matmul(bank(m % 2), gate[:, m * P:(m + 1) * P], q, start=True, stop=True).then_inc(s_fg, 1)
                    T.matmul(bank(2 + m % 2), val[:, m * P:(m + 1) * P], q, start=True, stop=True).then_inc(s_fu, 1)
                for m in range(M):
                    pe.wait_ge(s_fh, c * M + m + 1)
                    last = T.matmul(bank(4), proj[:, m, :], fh[:, m, :], start=(m == 0), stop=(m == M - 1))
                last.then_inc(s_fo, 1)
                pe.wait_ge(s_fos, c + 1)
                for j in range(QT):
                    last = T.matmul(PSUM[:, 5, j * P:(j + 1) * P], foT[:, j * P:(j + 1) * P], pw, start=True, stop=True)
                last.then_inc(s_fy, 1)
                pe.wait_ge(s_fx, c + 1)

            with pe.Fori(0, BATCH) as b:
                lns = iter(range(1, NLN + 1))
                trs = iter(range(1, NTR + 1))

                def turn_rows(src, norm_done=True, extra=0):
                    for _ in range(extra):
                        next(lns)
                    if norm_done:
                        pe.wait_ge(n_b.done, b * NLN + next(lns))
                    for j in range(QT):
                        last = T.transpose(PSUM[:, 7, j * P:(j + 1) * P], src[:, j, :], ident[:, :])
                    last.then_inc(s_bT, 1)
                    pe.wait_ge(s_bTs, b * NTR + next(trs))

                def project(dst, n, weights, s):
                    for j in range(QT):
                        for k in range(n):
                            last = T.matmul(PSUM[:, dst, j * P:(j + 1) * P], OT[:, k, j * P:(j + 1) * P], weights[:, k, :],
                                            start=(k == 0), stop=(k == n - 1))
                    last.then_inc(s, 1)

                def turn4(k):
                    for c in range(4):
                        last = T.transpose(PSUM[:, 2 + k % 2, c * P:(c + 1) * P], PB[:, k % 2, c * P:(c + 1) * P], ident[:, :])
                    return last

                pe.wait_ge(s_ctx, b + 1)
                T.matmul(bank(4, CTX), W0T[:, 1, :], CT[:, :], start=True, stop=True).then_inc(s_b_k, 1)
                T.matmul(PSUM[0:CTX, 5, 0:P], CT[:, :], W0T[:, 2, :], start=True, stop=True).then_inc(s_b_v, 1)
                turn_rows(YN)
                T.matmul(bank(6), W0T[:, 0, :], YT[:, :], start=True, stop=True).then_inc(s_b_q, 1)
                pe.wait_ge(s_b_qs, b + 1)
                pe.wait_ge(s_b_km, b + 1)
                pe.wait_ge(s_b_vs, b + 1)
                pe.wait_ge(s_zero, 1)

                def score(i):
                    j, t = i // 4, i % 4
                    return T.matmul(bank(i % 2, 4 * CTX), QS[:, t * P:(t + 1) * P], KM0[:, 4 * j:4 * j + 4, :],
                                    start=True, stop=True)

                def turn(k):
                    for g in range(GH):
                        last = T.transpose(PSUM[0:CTX, 2 + k % 2, g * P:(g + 1) * P], PB[:, k % 2, g * CTX:(g + 1) * CTX],
                                           ident[:, :])
                    return last

                def value(v):
                    for g in range(GH):
                        last = T.matmul(PSUM[g * LANE:(g + 1) * LANE, 4 + v % 2, :], VP[0:CTX, 0, 4 * v + g, :],
                                        PT0[0:CTX, v % 2, g, :], start=True, stop=True)
                    return last

                attention_tensor(pe, b, a0, score, turn, value)
                pe.wait_ge(s_outs, a0.summed(b, 4))
                project(6, GROUPS, WoA, s_b_o)

                turn_rows(YN)
                for t in range(QT):
                    T.matmul(bank(t), YT[:, t * P:(t + 1) * P], upT[:, :], start=True, stop=True).then_inc(s_c_u, 1)
                for t in range(QT):
                    pe.wait_ge(s_c_g, b * QT + t + 1)
                    if t >= 2:
                        pe.wait_ge(s_c_Ts, b * QT + t - 1)
                    for m in range(M):
                        last = T.transpose(PSUM[:, 4 + t % 2, m * P:(m + 1) * P], HC[:, t, m * P:(m + 1) * P], ident[:, :])
                    last.then_inc(s_c_T, 1)
                for t in range(QT):
                    pe.wait_ge(s_c_Ts, b * QT + t + 1)
                    for m in range(M):
                        last = T.matmul(PSUM[:, 6, t * P:(t + 1) * P], HTC[:, t, m * P:(m + 1) * P], downT[:, m, :],
                                        start=(m == 0), stop=(m == M - 1))
                last.then_inc(s_c_o, 1)

                turn_rows(YN)
                T.matmul(bank(0), WcT[:, 0:P], YT[:, :], start=True, stop=True).then_inc(s_d_q, 1)
                T.matmul(bank(1), WcT[:, P:2 * P], YT[:, :], start=True, stop=True).then_inc(s_d_q, 1)
                for n in range(8):
                    if n >= 4:
                        pe.wait_ge(s_d_vs, b * 8 + n - 3)
                    T.matmul(bank(2 + n % 4), YT[:, (n // 2) * P:(n // 2 + 1) * P],
                             WcT[:, 256 + 512 * (n % 2):768 + 512 * (n % 2)], start=True, stop=True).then_inc(s_d_v, 1)
                pe.wait_ge(s_d_qs, 2 * b + 2)
                pe.wait_ge(s_d_vs, b * 8 + 8)

                def score(i):
                    h, t = i // 4, i % 4
                    if t == 0:
                        pe.wait_ge(s_d_km, b * HEADS + h + 1)
                    return T.matmul(bank(i % 2), QS[:, t * P:(t + 1) * P], KMr[:, h % 8, :], start=True, stop=True)

                def value(v):
                    for c in range(QT):
                        for e in range(2):
                            h = 2 * v + e
                            last = T.matmul(PSUM[e * VD:(e + 1) * VD, 4 + v % 2, :], V1[:, c, h * VD:(h + 1) * VD],
                                            PTd[:, h % 4, c, :], start=(c == 0), stop=(c == QT - 1))
                    return last

                attention_tensor(pe, b, a1, score, turn4, value)
                pe.wait_ge(s_outs, a1.summed(b, 8))
                project(6, 8, Wo1T, s_d_o)

                turn_rows(Y2, extra=1)
                for p in range(4):
                    T.matmul(bank(p), Wq1[:, p * P:(p + 1) * P], YT[:, :], start=True, stop=True).then_inc(s_e_q, 1)
                for p in range(4):
                    kb = 4 + 2 * (p % 2)
                    if p >= 2:
                        pe.wait_ge(s_e_ks, b * 4 + p - 1)
                    T.matmul(bank(kb), Wkv1[:, p * P:(p + 1) * P], YT[:, :], start=True, stop=True)
                    T.matmul(bank(kb + 1, CTX), Wkv1[:, p * P:(p + 1) * P], CN[:, :], start=True, stop=True)\
                        .then_inc(s_e_k, 1)
                for c in range(5):
                    if c < 4:
                        pe.wait_ge(s_e_qs, b * 4 + c + 1)
                        T.matmul(bank(c), YT[:, c * P:(c + 1) * P], Wkv1[:, 512:1024], start=True, stop=True)\
                            .then_inc(s_e_v, 1)
                    else:
                        pe.wait_ge(s_e_ks, b * 4 + 3)
                        T.matmul(PSUM[0:CTX, 4, :], CN[:, :], Wkv1[:, 512:1024], start=True, stop=True)\
                            .then_inc(s_e_v, 1)
                pe.wait_ge(s_e_ks, b * 4 + 4)
                pe.wait_ge(s_e_vs, b * 5 + 5)

                def score(i):
                    h, t, sb_ = i // 4, i % 4, 2 * (i % 2)
                    T.matmul(bank(sb_), QX[:, h // 2, t * P:(t + 1) * P], KM8[:, h, 0:SEQ], start=True, stop=True)
                    return T.matmul(bank(sb_ + 1, CTX), QX[:, h // 2, t * P:(t + 1) * P], KM8[:, h, SEQ:XK],
                                    start=True, stop=True)

                def turn(k):
                    for c in range(4):
                        T.transpose(PSUM[:, 4 + k % 2, c * P:(c + 1) * P], PB[:, k % 2, c * P:(c + 1) * P], ident[:, :])
                    if k >= 1:
                        pe.wait_ge(s_moved, ax.unit(b, k))
                    return T.transpose(PSUM[0:CTX, 7, 0:P], PB[:, k % 2, SEQ:XK], ident[:, :])

                def value(v):
                    for c in range(5):
                        rows = P if c < 4 else CTX
                        for e in range(2):
                            h = 2 * v + e
                            last = T.matmul(PSUM[e * XD:(e + 1) * XD, 6, :], VX[0:rows, c, h * XD:(h + 1) * XD],
                                            PTe[0:rows, h % 4, c, :], start=(c == 0), stop=(c == 4))
                    return last

                attention_tensor(pe, b, ax, score, turn, value)
                pe.wait_ge(s_outs, ax.summed(b, 4))
                project(7, 4, Wout1, s_e_o)

                turn_rows(YN)
                for i in range(2):
                    T.matmul(bank(i), WF[:, i, :, :].rearrange("p h d -> p (h d)"), YT[:, :], start=True, stop=True)\
                        .then_inc(s_f_q, 1)
                for c in range(QT):
                    last = T.matmul(PSUM[:, 2, c * P:(c + 1) * P], YT[:, c * P:(c + 1) * P],
                                    WF[:, 2, :, :].rearrange("p h d -> p (h d)"), start=True, stop=True)
                last.then_inc(s_f_v, 1)
                pe.wait_ge(s_f_qs, 2 * b + 2)
                pe.wait_ge(s_f_vs, b + 1)

                def score(i):
                    h, t = i // 4, i % 4
                    if t == 0:
                        pe.wait_ge(s_f_km, b * HEADS + h + 1)
                    T.matmul(bank(i % 2, (t + 1) * P), QS[:, t * P:(t + 1) * P], KMr[:, h % 8, 0:(t + 1) * P],
                             start=True, stop=False)
                    return T.matmul(PSUM[:, i % 2, t * P:(t + 1) * P], ident_bf[:, :], causal_bf[:, :],
                                    start=False, stop=True)

                def turn(k):
                    for c in range(k % 4 + 1):
                        last = T.transpose(PSUM[:, 2 + k % 2, c * P:(c + 1) * P], PB[:, k % 2, c * P:(c + 1) * P],
                                           ident[:, :])
                    return last

                def value(v):
                    for c in range(QT):
                        for g in range(GH):
                            h = 4 * v + g
                            last = T.matmul(PSUM[g * LANE:(g + 1) * LANE, 4 + v % 2, c * P:SEQ], VP[:, c, h, :],
                                            PTd[:, h % 5, c, c * P:SEQ], start=(c == 0), stop=(c == QT - 1))
                    return last

                attention_tensor(pe, b, af, score, turn, value)
                pe.wait_ge(s_outs, af.summed(b, 4))
                project(6, GROUPS, SEL, s_f_o)
                pe.wait_ge(s_f_y, b + 1)
                turn_rows(YF, norm_done=False)
                for t in range(QT):
                    last = T.matmul(PSUM[:, 6, t * E:(t + 1) * E], YT[:, t * P:(t + 1) * P], gateW[:, :],
                                    start=True, stop=True)
                last.then_inc(s_f_g, 1)

                def up(e):
                    for m in range(M):
                        if e >= 1:
                            pe.wait_ge(s_f_hs, (b * E + e - 1) * M + m + 1)
                        T.matmul(bank(m), W1[:, e, m * P:(m + 1) * P], YT[:, :], start=True, stop=True).then_inc(s_f_h, 1)

                def down(e):
                    pe.wait_ge(s_f_hs, (b * E + e + 1) * M)
                    if e >= 2:
                        pe.wait_ge(s_f_acc, b * E + e - 1)
                    for t in range(QT):
                        for m in range(M):
                            last = T.matmul(PSUM[:, 4 + e % 2, t * P:(t + 1) * P], HE[:, e % 2, m, t * P:(t + 1) * P],
                                            W2[:, e, m, :], start=(m == 0), stop=(m == M - 1))
                    last.then_inc(s_f_dn, 1)

                up(0)
                up(1)
                pe.wait_ge(s_f_c, b + 1)
                for t in range(QT):
                    last = T.transpose(PSUM[0:E, 7, t * P:(t + 1) * P], comb[:, t, :], ident[:, :])
                last.then_inc(s_f_cT, 1)
                down(0)
                pe.wait_ge(s_f_cTs, b + 1)
                for t in range(QT):
                    last = T.matmul(PSUM[:, 6, t * P:(t + 1) * P], combT[:, t * P:(t + 1) * P], b2r[:, :],
                                    start=True, stop=True)
                last.then_inc(s_f_b2, 1)
                for e in range(1, E):
                    if e + 1 < E:
                        up(e + 1)
                    down(e)
                pe.wait_ge(s_rowdone, b + 1)



        @block.scalar
        def _(act):
            A = nc.scalar
            for i, (srcs, dst, rows, after) in enumerate(prep):
                n = len(srcs) * rows
                act.wait_ge(s_tr, i + 1)
                if after == "ctx":
                    A.activation(dst, PSUM[:, i % 7, 0:n].rearrange("p (b s) -> p b s", b=BATCH), ACT.Identity,
                                 bias=V[:, BM:BM + 1], scale=V[:, GM:GM + 1]).then_inc(s_ev, 1)
                else:
                    A.activation(dst, PSUM[:, i % 7, 0:n].rearrange("p (b s) -> p b s", s=rows) if len(dst.shape) == 3
                                 else PSUM[:, i % 7, 0:n], ACT.Copy).then_inc(s_ev, 1)
                if i == 0:
                    act.wait_ge(s_ev, 1)
            A.activation(vs[:, 0:1], V[:, BQ0:BQ0 + 1], ACT.Copy, scale=HD ** -0.5)
            A.activation(vs[:, 1:2], V[:, BCQ:BCQ + 1], ACT.Copy, scale=HD ** -0.5)
            A.activation(aI, ident[:, :], ACT.Copy, scale=NS_A)
            with act.Fori(0, BATCH) as c:
                act.wait_ge(s_yT, c + 1)
                A.activation(YT[:, :], bank(0), ACT.Copy).then_inc(s_yTs, 1)
                act.wait_ge(s_qkvb, c + 1)
                A.activation(sq4, VA[:, 0:1024], ACT.Square).then_inc(s_sqr, 1)
                act.wait_ge(s_ss, c + 1)
                A.activation(normw[:, 128:256], normw[:, 0:128], ACT.Sqrt).then_inc(s_nrm, 1)
                act.wait_ge(s_qkT, 2 * c + 1)
                A.activation(QTall[:, bass.ds(c * SEQ, SEQ)], bank(5), ACT.Identity, scale=V[:, QSC:QSC + 1],
                             bias=V[:, QBI:QBI + 1]).then_inc(s_qkTs, 1)
                act.wait_ge(s_qkT, 2 * c + 2)
                A.activation(KTall[:, bass.ds(c * SEQ, SEQ)], bank(6), ACT.Identity, scale=V[:, KSC:KSC + 1],
                             bias=V[:, KBI:KBI + 1]).then_inc(s_qkTs, 1)
            with act.Fori(0, STEPS) as step:
                def gate_val(t):
                    n, par = step * TILES + t, t % 2
                    act.wait_ge(s_gu, n + 1)
                    if t >= 2:
                        act.wait_ge(s_w, n - 1)
                    A.activation(sg[par], bank(0), ACT.Sigmoid).then_inc(s_sig, 1)
                    A.activation(us[par], bank(1), ACT.Copy).then_inc(s_uc, 1)

                gate_val(0)
                for t in range(TILES):
                    n = step * TILES + t
                    act.wait_ge(s_hT, n + 1)
                    A.activation(hTs, bank(2), ACT.Copy).then_inc(s_hTs, 1)
                    if t + 1 < TILES:
                        gate_val(t + 1)
                    act.wait_ge(s_dpT, n + 1)
                    A.activation(dpT, PSUM[:, 3, 128:256], ACT.Copy).then_inc(s_dpTs, 1)
                act.wait_ge(s_gs, step * 3 + 3)
                for i in range(3):
                    last = A.activation(nxT[i], nx[i], ACT.Square, accum_out=sm[:, i:i + 1])
                last.then_inc(s_sq, 1)
                for i in range(3):
                    act.wait_ge(s_xt0, step * 3 + i + 1)
                    A.activation(nxT[i], bank(1 + i), ACT.Copy).then_inc(s_xt0s, 1)
                with act.Fori(0, NS_ITERS) as it:
                    k = (step * NS_ITERS + it) * 3
                    for i in range(3):
                        act.wait_ge(s_A, k + i + 1)
                        A.activation(nA[i], PSUM[:, i, 0:P], ACT.Copy).then_inc(s_As, 1)
                    for i, bx in enumerate((3, 5, 7)):
                        act.wait_ge(s_XN, k + i + 1)
                        act.wait_ge(s_XTN, k + i + 1)
                        A.activation(nx[i], bank(bx), ACT.Copy).then_inc(s_XNs, 1)
            with act.Fori(0, BATCH) as c:
                for m in range(M):
                    n = c * M + m
                    act.wait_ge(s_fg, n + 1)
                    A.activation(fsg[:, m % 2, :], bank(m % 2), ACT.Sigmoid).then_inc(s_fs, 1)
                act.wait_ge(s_fo, c + 1)
                A.activation(foT, bank(4), ACT.Copy).then_inc(s_fos, 1)

            with act.Fori(0, BATCH) as b:
                trs = iter(range(1, NTR + 1))

                def rows_T(scale=None, bias=None):
                    act.wait_ge(s_bT, b * NTR + next(trs))
                    if scale is None:
                        A.activation(YT[:, :], bank(7), ACT.Copy).then_inc(s_bTs, 1)
                    else:
                        A.activation(YT[:, :], bank(7), ACT.Identity, scale=scale, bias=bias).then_inc(s_bTs, 1)

                act.wait_ge(s_b_k, b + 1)
                A.activation(KT0[:, 0:CTX], bank(4, CTX), ACT.Identity, bias=V[:, BK0:BK0 + 1]).then_inc(s_b_ks, 1)
                rows_T()
                act.wait_ge(s_b_q, b + 1)
                A.activation(QS, bank(6), ACT.Identity, scale=HD ** -0.5, bias=vs[:, 0:1]).then_inc(s_b_qs, 1)

                def exp(i):
                    for g in range(GH):
                        last = A.activation(PB[:, i % 2, g * CTX:(g + 1) * CTX], PSUM[:, i % 2, g * CTX:(g + 1) * CTX], ACT.Exp,
                                            bias=nmax[:, i % 2, g:g + 1], accum_out=rsum[:, i % 2, g:g + 1])
                    return last

                def move(k):
                    j, t = k // 4, k % 4
                    return A.activation(PT0[0:CTX, j % 2, :, t * P:(t + 1) * P],
                                        PSUM[0:CTX, 2 + k % 2, :].rearrange("p (g q) -> p g q", g=4), ACT.Copy)

                attention_scalar(act, b, a0, exp, move)

                rows_T()
                act.wait_ge(s_c_r1, b + 1)
                for t in range(QT):
                    act.wait_ge(s_c_u, b * QT + t + 1)
                    A.activation(HC[:, t, :], bank(t), ACT.Gelu, scale=root[:, 0, t:t + 1]).then_inc(s_c_g, 1)
                for t in range(QT):
                    act.wait_ge(s_c_T, b * QT + t + 1)
                    A.activation(HTC[:, t, :], bank(4 + t % 2), ACT.Copy).then_inc(s_c_Ts, 1)

                def exp_at(base, width):
                    def exp(i):
                        w = width(i)
                        return A.activation(PB[:, i % 2, 0:w], PSF[:, base(i):base(i) + w], ACT.Exp, bias=nmax[:, i % 2, 0:1],
                                            accum_out=rsum[:, i % 2, 0:1])
                    return exp

                rows_T()
                act.wait_ge(s_d_q, 2 * b + 1)
                A.activation(Qraw, bank(0), ACT.Identity, scale=HD ** -0.5, bias=vs[:, 1:2]).then_inc(s_d_qb, 1)
                act.wait_ge(s_d_q, 2 * b + 2)
                A.activation(Kraw, bank(1), ACT.Identity, bias=V[:, BCK:BCK + 1]).then_inc(s_d_qb, 1)

                def move(k):
                    h, t = k // 4, k % 4
                    return A.activation(PTd[:, h % 4, :, t * P:(t + 1) * P],
                                        bank(2 + k % 2).rearrange("p (c q) -> p c q", c=4), ACT.Copy)

                attention_scalar(act, b, a1, exp_at(lambda i: 512 * (i % 2), lambda i: SEQ), move)

                rows_T(V[:, GL:GL + 1], V[:, BL:BL + 1])
                for p in range(4):
                    act.wait_ge(s_e_q, b * 4 + p + 1)
                    A.activation(QX[:, p, :], bank(p), ACT.Copy, scale=XD ** 0.5).then_inc(s_e_qs, 1)
                for c in range(5):
                    rows = P if c < 4 else CTX
                    act.wait_ge(s_e_v, b * 5 + c + 1)
                    A.activation(VX[0:rows, c, :], PSUM[0:rows, c, :], ACT.Copy).then_inc(s_e_vs, 1)

                def move(k):
                    h, t = k // 4, k % 4
                    A.activation(PTe[0:CTX, h % 4, 4, t * P:(t + 1) * P], PSUM[0:CTX, 7, 0:P], ACT.Copy)
                    return A.activation(PTe[:, h % 4, 0:4, t * P:(t + 1) * P],
                                        bank(4 + k % 2).rearrange("p (c q) -> p c q", c=4), ACT.Copy)

                attention_scalar(act, b, ax, exp_at(lambda i: 1024 * (i % 2), lambda i: XK), move)

                rows_T()
                act.wait_ge(s_f_q, 2 * b + 1)
                A.activation(QS, bank(0), ACT.Copy, scale=D ** -0.5).then_inc(s_f_qs, 1)
                act.wait_ge(s_f_q, 2 * b + 2)
                A.activation(KT0, bank(1), ACT.Copy).then_inc(s_f_qs, 1)

                def move(k):
                    h, t = k // 4, k % 4
                    w = (t + 1) * P
                    return A.activation(PTd[:, h % 5, 0:t + 1, t * P:(t + 1) * P],
                                        bank(2 + k % 2, w).rearrange("p (c q) -> p c q", q=P), ACT.Copy)

                attention_scalar(act, b, af, exp_at(lambda i: 512 * (i % 2), lambda i: (i % 4 + 1) * P), move)
                rows_T()

                def relu(e):
                    if e >= 2:
                        act.wait_ge(s_f_dn, b * E + e - 1)
                    for m in range(M):
                        act.wait_ge(s_f_h, (b * E + e) * M + m + 1)
                        A.activation(HE[:, e % 2, m, :], bank(m), ACT.Relu, bias=V[:, B1C + e * M + m:B1C + e * M + m + 1])\
                            .then_inc(s_f_hs, 1)

                relu(0)
                act.wait_ge(s_f_d, b + 1)
                A.activation(tw[:, 1, :], tw[:, 0, :], ACT.Exp).then_inc(s_f_e, 1)
                relu(1)
                act.wait_ge(s_f_cT, b + 1)
                A.activation(combT, PSUM[0:E, 7, :], ACT.Copy).then_inc(s_f_cTs, 1)
                for e in range(2, E):
                    relu(e)
                act.wait_ge(s_rowdone, b + 1)

        @block.vector
        def _(dve):
            Vv = nc.vector

            def head_groups(ap):
                return ap.rearrange("p t w (h d) -> p (t w h) d", d=HD)

            dve.wait_ge(s_w0, N_W0)
            Vv.tensor_reduce(sm[:, 0:1], upraw, AX.X, ALU.add, apply_absolute_value=True)
            Vv.tensor_reduce(sm[:, 1:2], downraw, AX.X, ALU.add, apply_absolute_value=True).then_inc(s_absum, 1)
            dve.wait_ge(s_thr, 1)
            Vv.tensor_scalar(sm[:, 2:4], bank(7, 2), 0.5 / (HID * D), None, ALU.mult)
            dve.drain()
            Vv.tensor_scalar(sm[:, 4:6], sm[:, 2:4], -1.0, None, ALU.mult)
            dve.drain()
            for i, w in enumerate((upraw, downraw)):
                Vv.tensor_scalar(tern[:, i, :], w, sm[:, 2 + i:3 + i], None, ALU.is_gt)
                dve.drain()
                Vv.scalar_tensor_tensor(tern[:, i, :], w, sm[:, 4 + i:5 + i], tern[:, i, :], ALU.is_lt, ALU.subtract)
                dve.drain()
                Vv.scalar_tensor_tensor(tern[:, i, :], tern[:, i, :], -1.0, w, ALU.mult, ALU.subtract)
                dve.drain()
                last = Vv.tensor_tensor(ternq[:, i, :], tern[:, i, :], w, ALU.add)
            last.then_inc(s_tern, 1)
            ln_vector(dve, n_ctx, 1, [ctxraw[0:CTX, b, :] for b in range(BATCH)],
                      [ctxn[0:CTX, b, :] for b in range(BATCH)], CTX)
            dve.wait_ge(s_wt, N_WT)
            dve.wait_ge(s_x, 16)
            dve.wait_ge(s_ev, NPREP)
            for dst, src in ((kscale, kscale8), (kbias, kbias8)):
                Vv.tensor_copy(dst.rearrange("p (h d) -> p h d", d=HD), src.unsqueeze(1).to_broadcast([P, HEADS, HD]))
            with dve.Fori(0, BATCH) as c:
                ln_vector(dve, n_in, c + 1, [X[:, bass.ds(c * QT + j, 1), :].rearrange("p o d -> p (o d)") for j in range(QT)],
                          [YN[:, j, :] for j in range(QT)])
                for j in range(QT):
                    dve.wait_ge(s_qkv, c * QT + j + 1)
                    Vv.tensor_tensor(qkvs[:, j, :, :].rearrange("p w d -> p (w d)"), PSUM[:, 1 + j, 0:256], bqkv[:, 0:256], ALU.add)
                    last = Vv.tensor_tensor(Vn[:, bass.ds(c * QT + j, 1), :].rearrange("p o d -> p (o d)"), PSUM[:, 1 + j, 256:384],
                                     bqkv[:, 256:384], ALU.add)
                last.then_inc(s_qkvb, 1)
                dve.wait_ge(s_sqr, c + 1)
                Vv.tensor_reduce(normw[:, 0:128], sq4.rearrange("p (g d) -> p g d", d=HD), AX.X, ALU.add).then_inc(s_ss, 1)
                dve.wait_ge(s_nrm, c + 1)
                Vv.tensor_scalar(normw[:, 128:256], normw[:, 128:256], 1e-6, None, ALU.add)
                dve.drain()
                Vv.reciprocal(normw[:, 0:128], normw[:, 128:256])
                dve.drain()
                g3 = VA[:, 0:1024].rearrange("p (g d) -> p g d", d=HD)
                Vv.tensor_tensor(g3, g3, normw[:, 0:128].unsqueeze(2).to_broadcast([P, P, HD]), ALU.mult).then_inc(s_qk, 1)
                dve.drain()
                Vv.tensor_tensor(kraw, qkvs[:, :, 1, :], kscale.unsqueeze(1).to_broadcast([P, QT, D]), ALU.mult)
                dve.drain()
                Vv.tensor_tensor(Kn[:, bass.ds(c * QT, QT), :], kraw, kbias.unsqueeze(1).to_broadcast([P, QT, D]), ALU.add)\
                    .then_inc(s_kn, 1)
                dve.wait_ge(s_qkTs, 2 * c + 2)

            with dve.Fori(0, STEPS) as step:
                def silu(t):
                    n, par = step * TILES + t, t % 2
                    if t >= 2:
                        dve.wait_ge(s_w, n - 1)
                        dve.wait_ge(s_dgu, n - 1)
                    dve.wait_ge(s_sig, n + 1)
                    Vv.tensor_tensor(t1[par], bank(0), sg[par], ALU.mult).then_inc(s_t, 1)
                    dve.wait_ge(s_t, n + 1)
                    dve.wait_ge(s_uc, n + 1)
                    Vv.tensor_tensor(hh[par], us[par], t1[par], ALU.mult).then_inc(s_h, 1)

                silu(0)
                for t in range(TILES):
                    n, par = step * TILES + t, t % 2
                    if t + 1 < TILES:
                        silu(t + 1)
                    dve.wait_ge(s_pred, n + 1)
                    Vv.tensor_tensor(dp, bank(3, P), Vn[:, t, :], ALU.subtract)
                    dve.drain()
                    Vv.tensor_scalar(dp, dp, 2.0 / (TILES * P * D), None, ALU.mult).then_inc(s_dp, 1)
                    dve.wait_ge(s_dh, n + 1)
                    Vv.tensor_tensor(du, bank(4), t1[par], ALU.mult)
                    dve.wait_ge(s_w, n + 1)
                    Vv.tensor_tensor(dg, bank(4), ww[par], ALU.mult).then_inc(s_dgu, 1)
                dve.wait_ge(s_grad, step + 1)
                for i in range(3):
                    Vv.tensor_copy(nx[i], bank(5 + i)).then_inc(s_gs, 1)
                dve.wait_ge(s_tot, step + 1)
                Vv.tensor_copy(sm[:, 4:7], bank(0, 3)).then_inc(s_tots, 1)
                dve.wait_ge(s_nrt, step + 1)
                Vv.tensor_scalar(sm[:, 8:11], sm[:, 8:11], 1e-7, None, ALU.add)
                dve.drain()
                Vv.reciprocal(sm[:, 12:15], sm[:, 8:11])
                dve.drain()
                for i in range(3):
                    Vv.tensor_scalar(nx[i], nx[i], sm[:, 12 + i:13 + i], None, ALU.mult).then_inc(s_x0, 1)
                with dve.Fori(0, NS_ITERS) as it:
                    k = (step * NS_ITERS + it) * 3
                    for i in range(3):
                        dve.wait_ge(s_As, k + i + 1)
                        Vv.scalar_tensor_tensor(nC[i], nA[i], NS_B, aI, ALU.mult, ALU.add)
                    dve.drain()
                    for i in range(3):
                        dve.wait_ge(s_A2, k + i + 1)
                        Vv.scalar_tensor_tensor(nB[i], PSUM[:, i, P:2 * P], NS_C, nC[i], ALU.mult, ALU.add).then_inc(s_B, 1)
                    for i, bt in enumerate((4, 6, 3)):
                        dve.wait_ge(s_XTN, k + i + 1)
                        Vv.tensor_copy(nxT[i], bank(bt)).then_inc(s_XTNs, 1)
                dve.wait_ge(s_XNs, (step + 1) * NS_ITERS * 3)
                dve.wait_ge(s_XTNs, (step + 1) * NS_ITERS * 3)
                Vv.scalar_tensor_tensor(gate, nx[0], -LR, gate, ALU.mult, ALU.add)
                Vv.scalar_tensor_tensor(val, nx[1], -LR, val, ALU.mult, ALU.add)
                Vv.scalar_tensor_tensor(projT, nx[2], -LR, projT, ALU.mult, ALU.add)
                Vv.scalar_tensor_tensor(proj.rearrange("p m d -> p (m d)"), nxT[2], -LR,
                                        proj.rearrange("p m d -> p (m d)"), ALU.mult, ALU.add).then_inc(s_upd, 1)
            with dve.Fori(0, BATCH) as c:
                for m in range(M):
                    n = c * M + m
                    dve.wait_ge(s_fs, n + 1)
                    Vv.tensor_tensor(ft[:, m % 2, :], bank(m % 2), fsg[:, m % 2, :], ALU.mult)
                    dve.drain()
                    dve.wait_ge(s_fu, n + 1)
                    Vv.tensor_tensor(fh[:, m, :], bank(2 + m % 2), ft[:, m % 2, :], ALU.mult).then_inc(s_fh, 1)
                dve.wait_ge(s_fy, c + 1)
                xs = X[:, bass.ds(c * QT, QT), :]
                Vv.tensor_tensor(Y2[:, :, :], PSUM[:, 5, :].rearrange("p (t d) -> p t d", d=D),
                                 bproj.unsqueeze(1).to_broadcast([P, QT, D]), ALU.add)
                dve.drain()
                Vv.tensor_tensor(xs, xs, Y2[:, :, :], ALU.add).then_inc(s_fx, 1)

            Vv.memset(VPA[:, :], 0.0).then_inc(s_zero, 1)
            dve.wait_ge(s_wr, N_WR)
            dve.drain()
            with dve.Fori(0, BATCH) as b:
                lns = iter(range(1, NLN + 1))
                xs = X[:, bass.ds(b * QT, QT), :]

                def xt(j):
                    return X[:, bass.ds(b * QT + j, 1), :].rearrange("p o d -> p (o d)")

                def tiles(y):
                    return [y[:, j, :] for j in range(QT)]

                def norm(src, dst):
                    dve.drain()
                    ln_vector(dve, n_b, b * NLN + next(lns), src, dst)

                def rows(i):
                    return bc[:, i, :].unsqueeze(1).to_broadcast([P, QT, D])

                def tok(n):
                    return bank(n).rearrange("p (t d) -> p t d", d=D)

                def normaliser(width):
                    def normalise(k):
                        Vv.reciprocal(rinv[:, k % 2, 0:1], rsum[:, k % 2, 0:1])
                        dve.drain()
                        w = width(k)
                        return Vv.tensor_scalar(PB[:, k % 2, 0:w], PB[:, k % 2, 0:w], rinv[:, k % 2, 0:1], None, ALU.mult)
                    return normalise

                def maximum_of(base, width):
                    def maximum(i):
                        return Vv.tensor_reduce(nmax[:, i % 2, 0:1], PSF[:, base(i):base(i) + width(i)], AX.X, ALU.max, negate=True)
                    return maximum

                dve.wait_ge(s_b_v, b + 1)
                Vv.tensor_tensor(VP[0:CTX, 0, :, 0:HD], PSUM[0:CTX, 5, 0:P].rearrange("p (h d) -> p h d", d=HD),
                                 bc[0:CTX, BV0, :].rearrange("p (h d) -> p h d", d=HD), ALU.add).then_inc(s_b_vs, 1)
                norm([xt(j) for j in range(QT)], tiles(YN))
                dve.wait_ge(s_b_ks, b + 1)
                Vv.tensor_tensor(KM0, KT0[:, 0:CTX].unsqueeze(1).to_broadcast([P, HEADS, CTX]),
                                 head_mask[:, :].unsqueeze(2).to_broadcast([P, HEADS, CTX]), ALU.mult).then_inc(s_b_km, 1)

                def maximum(i):
                    return Vv.tensor_reduce(nmax[:, i % 2, :], bank(i % 2, 4 * CTX).rearrange("p (g k) -> p g k", g=4),
                                            AX.X, ALU.max, negate=True)

                def normalise(k):
                    Vv.reciprocal(rinv[:, k % 2, :], rsum[:, k % 2, :])
                    dve.drain()
                    p3 = PB[:, k % 2, 0:4 * CTX].rearrange("p (g k) -> p g k", g=4)
                    return Vv.tensor_tensor(p3, p3, rinv[:, k % 2, :].unsqueeze(2).to_broadcast([P, 4, CTX]), ALU.mult)

                attention_vector(dve, b, a0, maximum, normalise, lambda v: Vv.tensor_copy(OT[:, v, :], bank(4 + v % 2)))
                dve.wait_ge(s_b_o, b + 1)
                Vv.tensor_tensor(Y2[:, :, :], tok(6), rows(BO0), ALU.add)
                dve.drain()
                Vv.tensor_tensor(xs, xs, Y2[:, :, :], ALU.add)

                norm([xt(j) for j in range(QT)], tiles(YN))
                dve.drain()
                for j in range(QT):
                    last = Vv.tensor_tensor_reduce(out=KMA[:, j * P:(j + 1) * P], in0=YN[:, j, :], in1=YN[:, j, :], scale=1.0,
                                                   scalar=0.0, op0=ALU.mult, op1=ALU.add, accum_out=ssq[:, 0, j:j + 1])
                last.then_inc(s_pow, 1)
                dve.wait_ge(s_powd, 2 * b + 1)
                Vv.tensor_scalar(root[:, 0, :], root[:, 0, :], float(D) ** -0.5, 1e-8, ALU.mult, ALU.add)
                dve.drain()
                Vv.reciprocal(root[:, 0, :], root[:, 0, :]).then_inc(s_c_r1, 1)
                for j in range(QT):
                    dve.wait_ge(s_c_g, b * QT + j + 1)
                    last = Vv.tensor_tensor_reduce(out=KMA[:, 512 * (j + 1):512 * (j + 2)], in0=HC[:, j, :], in1=HC[:, j, :],
                                                   scale=1.0, scalar=0.0, op0=ALU.mult, op1=ALU.add, accum_out=ssq[:, 1, j:j + 1])
                last.then_inc(s_pow, 1)
                dve.wait_ge(s_powd, 2 * b + 2)
                Vv.tensor_scalar(root[:, 1, :], root[:, 1, :], float(HID) ** -0.5, 1e-8, ALU.mult, ALU.add)
                dve.drain()
                Vv.reciprocal(root[:, 1, :], root[:, 1, :])
                dve.drain()
                dve.wait_ge(s_c_o, b + 1)
                for j in range(QT):
                    Vv.scalar_tensor_tensor(xt(j), PSUM[:, 6, j * P:(j + 1) * P], root[:, 1, j:j + 1], xt(j), ALU.mult, ALU.add)

                norm([xt(j) for j in range(QT)], tiles(YN))
                for i, (raw, dst) in enumerate(((Qraw, QS), (Kraw, KT0))):
                    dve.wait_ge(s_d_qb, 2 * b + i + 1)
                    Vv.scalar_tensor_tensor(dst, raw, SLOPE, raw, ALU.mult, ALU.max).then_inc(s_d_qs, 1)
                for n in range(8):
                    half = slice(512 * (n % 2), 512 * (n % 2 + 1))
                    dve.wait_ge(s_d_v, b * 8 + n + 1)
                    Vv.tensor_tensor(V1[:, n // 2, half], bank(2 + n % 4), bcv[:, half], ALU.add)
                    dve.drain()
                    Vv.scalar_tensor_tensor(V1[:, n // 2, half], V1[:, n // 2, half], SLOPE, V1[:, n // 2, half],
                                            ALU.mult, ALU.max).then_inc(s_d_vs, 1)
                attention_vector(dve, b, a1, maximum_of(lambda i: 512 * (i % 2), lambda i: SEQ), normaliser(lambda i: SEQ),
                                 lambda v: Vv.tensor_copy(OT[:, v, :], bank(4 + v % 2)))
                Vv.tensor_tensor(xs, xs, YN[:, :, :], ALU.add)
                dve.wait_ge(s_d_o, b + 1)
                Vv.tensor_tensor(Y2[:, :, :], tok(6), rows(BO1), ALU.add)
                dve.drain()
                Vv.scalar_tensor_tensor(Y2[:, :, :], Y2[:, :, :], SLOPE, Y2[:, :, :], ALU.mult, ALU.max)
                dve.drain()
                Vv.tensor_tensor(xs, xs, Y2[:, :, :], ALU.add)

                norm([xt(j) for j in range(QT)], tiles(YN))
                norm(tiles(YN), tiles(Y2))
                for p in range(4):
                    dve.wait_ge(s_e_k, b * 4 + p + 1)
                    kb = 512 * (4 + 2 * (p % 2))
                    for e in range(2):
                        last = Vv.tensor_scalar(KM8[:, 2 * p + e, 0:XK], PSF[:, kb:kb + XK], half_mask[:, e:e + 1], None, ALU.mult)
                    last.then_inc(s_e_ks, 1)
                attention_vector(dve, b, ax, maximum_of(lambda i: 1024 * (i % 2), lambda i: XK), normaliser(lambda i: XK),
                                 lambda v: Vv.tensor_copy(OT[:, v, :], bank(6)))
                dve.wait_ge(s_e_o, b + 1)
                Vv.tensor_tensor(xs, tok(7), xs, ALU.add)

                norm([xt(j) for j in range(QT)], tiles(YN))
                dve.wait_ge(s_f_v, b + 1)
                Vv.tensor_copy(VP[:, :, :, 0:HD].rearrange("p t h d -> p (t h) d"),
                               bank(2).rearrange("p (g d) -> p g d", d=HD)).then_inc(s_f_vs, 1)
                attention_vector(dve, b, af, maximum_of(lambda i: 512 * (i % 2), lambda i: (i % 4 + 1) * P),
                                 normaliser(lambda i: (i % 4 + 1) * P),
                                 lambda v: Vv.tensor_copy(OT[:, v, :], bank(4 + v % 2)))
                dve.wait_ge(s_f_o, b + 1)
                Vv.tensor_copy(Y2[:, :, :], tok(6))
                norm(tiles(Y2), tiles(Y2))
                dve.drain()
                Vv.tensor_tensor(Y2[:, :, :], Y2[:, :, :], rows(G1), ALU.mult)
                dve.drain()
                Vv.tensor_tensor(Y2[:, :, :], Y2[:, :, :], rows(C1), ALU.add)
                dve.drain()
                Vv.tensor_tensor(YF[:, :, :], Y2[:, :, :], YN[:, :, :], ALU.add).then_inc(s_f_y, 1)
                dve.wait_ge(s_f_g, b + 1)
                Vv.tensor_copy(logit[:, :, :], bank(6, QT * E).rearrange("p (t e) -> p t e", e=E))
                dve.drain()
                for j in range(QT):
                    Vv.max(top[:, j, :], logit[:, j, :])
                dve.drain()
                for j in range(QT):
                    Vv.max_index(topi[:, j, :], top[:, j, :], logit[:, j, :])
                Vv.tensor_tensor(tw[:, 0, :], top[:, :, 1], top[:, :, 0], ALU.subtract).then_inc(s_f_d, 1)
                dve.drain()
                Vv.tensor_copy(topf[:, :, :], topi[:, :, :])
                dve.wait_ge(s_f_e, b + 1)
                Vv.tensor_scalar(tw[:, 2, :], tw[:, 1, :], 1.0, None, ALU.add)
                dve.drain()
                Vv.reciprocal(tw[:, 2, :], tw[:, 2, :])
                dve.drain()
                Vv.tensor_tensor(tw[:, 3, :], tw[:, 1, :], tw[:, 2, :], ALU.mult)
                dve.drain()
                for j in range(QT):
                    Vv.tensor_scalar(comb[:, j, :], iota8[:, :], topf[:, j, 0:1], tw[:, 2, j:j + 1], ALU.is_equal, ALU.mult)
                    Vv.tensor_scalar(comb2[:, j, :], iota8[:, :], topf[:, j, 1:2], tw[:, 3, j:j + 1], ALU.is_equal, ALU.mult)
                dve.drain()
                Vv.tensor_tensor(comb[:, :, :], comb[:, :, :], comb2[:, :, :], ALU.add).then_inc(s_f_c, 1)
                dve.wait_ge(s_f_b2, b + 1)
                Vv.tensor_copy(Y2[:, :, :], tok(6))
                for e in range(E):
                    dve.drain()
                    dve.wait_ge(s_f_dn, b * E + e + 1)
                    for j in range(QT):
                        last = Vv.scalar_tensor_tensor(Y2[:, j, :], PSUM[:, 4 + e % 2, j * P:(j + 1) * P], comb[:, j, e:e + 1],
                                                       Y2[:, j, :], ALU.mult, ALU.add)
                    last.then_inc(s_f_acc, 1)
                norm(tiles(Y2), tiles(Y2))
                dve.drain()
                Vv.tensor_tensor(Y2[:, :, :], Y2[:, :, :], rows(G2), ALU.mult)
                dve.drain()
                Vv.tensor_tensor(Y2[:, :, :], Y2[:, :, :], rows(C2), ALU.add)
                dve.drain()
                Vv.tensor_tensor(YF[:, :, :], YF[:, :, :], Y2[:, :, :], ALU.add)
                dve.drain()
                Vv.tensor_tensor(xs, xs, YF[:, :, :], ALU.add).then_inc(s_rowdone, 1)


_INS = ["x", "ctx_1024", "L0_attn_qkv_w", "L0_attn_qkv_b", "L0_attn_qn_scale", "L0_attn_qn_bias", "L0_attn_kn_scale",
        "L0_attn_kn_bias", "L0_attn_ttt_gate", "L0_attn_ttt_val", "L0_attn_ttt_proj", "L0_attn_proj_w",
        "L0_attn_proj_b", "L0_xattn_Wq", "L0_xattn_bq", "L0_xattn_Wk", "L0_xattn_bk", "L0_xattn_Wv", "L0_xattn_bv",
        "L0_xattn_Wo", "L0_xattn_bo", "L0_ffn_w_up", "L0_ffn_w_down", "L1_attn_Wc", "L1_attn_bc", "L1_attn_Wo",
        "L1_attn_bo", "L1_xattn_Wq", "L1_xattn_Wkv", "L1_xattn_Wout", "L1_xattn_gm", "L1_xattn_bm", "L1_xattn_gl",
        "L1_xattn_bl", "L1_ffn_Wq", "L1_ffn_Wk", "L1_ffn_Wv", "L1_ffn_gate_W", "L1_ffn_W1", "L1_ffn_b1",
        "L1_ffn_W2", "L1_ffn_b2", "L1_ffn_ln1_g", "L1_ffn_ln1_b", "L1_ffn_ln2_g", "L1_ffn_ln2_b"]


def kernel(**inputs):
    import numpy as _np
    import concourse.bacc as _bacc
    from concourse import mybir as _mybir
    from concourse.bass_utils import run_bass_kernel_spmd as _run

    nc = _bacc.Bacc("TRN2", target_bir_lowering=False, num_devices=1)
    arrays, args = {}, []
    for name in _INS:
        a = _np.ascontiguousarray(inputs[name])
        arrays[f"in_{name}_dram"] = a
        args.append(nc.dram_tensor(f"in_{name}_dram", a.shape, _mybir.dt.from_np(a.dtype), kind="ExternalInput").ap())
    out = nc.dram_tensor("out_dram", (BATCH, SEQ, D), F32, kind="ExternalOutput").ap()
    decoder_kernel(nc, *args, out)
    r = _run(nc, [arrays], core_ids=[0])
    return r.results[0]["out_dram"]
```

```python
import numpy as np
import concourse.bass as bass
from concourse import mybir
from contextlib import ExitStack

F32 = mybir.dt.float32
BF16 = mybir.dt.bfloat16
F32R = mybir.dt.float32r
U32 = mybir.dt.uint32
ALU = mybir.AluOpType
ACT = mybir.ActivationFunctionType
AX = mybir.AxisListType

BATCH, SEQ, D = 4, 512, 128
P = 128
QT = SEQ // P
TILES = BATCH * QT
CTX = 77
HEADS, HD = 16, 8
PAIRS = 8
GROUPS, LANE = 4, 32
HID = 512
M = HID // P
STEPS, NS_ITERS, LR = 2, 5, 0.1
NS_A, NS_B, NS_C = 3.4445, -4.775, 2.0315
VD = 64
XH, XD = 8, 64
XK = SEQ + CTX
E = 8
LN_EPS = 1e-5
SLOPE = 0.01
MASKED = -3.0e38


def decoder_kernel(nc, x, ctx_1024, qkv_w, qkv_b, qn_scale, qn_bias, kn_scale, kn_bias, ttt_gate, ttt_val,
                   ttt_proj, proj_w, proj_b, x0_Wq, x0_bq, x0_Wk, x0_bk, x0_Wv, x0_bv, x0_Wo, x0_bo, w_up, w_down,
                   a1_Wc, a1_bc, a1_Wo, a1_bo, x1_Wq, x1_Wkv, x1_Wout, x1_gm, x1_bm, x1_gl, x1_bl,
                   f1_Wq, f1_Wk, f1_Wv, f1_gate, f1_W1, f1_b1, f1_W2, f1_b2, f1_g1, f1_c1, f1_g2, f1_c2, out):
    stack = ExitStack()
    with stack:
        def sb(name, shape, dt=F32):
            return stack.enter_context(nc.sbuf_tensor(name, shape, dt))

        def sem(name):
            return stack.enter_context(nc.semaphore(name))

        X = sb("X", [P, TILES, D])
        ident = sb("ident", [P, P])
        ident_bf = sb("ident_bf", [P, P], BF16)
        causal_bf = sb("causal_bf", [P, P], BF16)
        head_mask = sb("head_mask", [P, HEADS])
        half_mask = sb("half_mask", [P, 2])
        iota8 = sb("iota8", [P, E])
        iota_i = sb("iota_i", [P, E], mybir.dt.int32)
        neg_half = sb("neg_half", [P, 8])
        pos_half = sb("pos_half", [P, 8])
        W0T = sb("W0T", [P, 3, D])
        WoA = sb("WoA", [P, GROUPS, D])
        SEL = sb("SEL", [P, GROUPS, D])
        upT = sb("upT", [P, HID])
        downT = sb("downT", [P, M, D])
        WcT = sb("WcT", [P, 1280])
        Wo1T = sb("Wo1T", [P, 8, D])
        Wq1 = sb("Wq1", [P, 512])
        Wkv1 = sb("Wkv1", [P, 1024])
        Wout1 = sb("Wout1", [P, 4, D])
        WF = sb("WF", [P, 3, HEADS, HD])
        gateW = sb("gateW", [P, E])
        W1 = sb("W1", [P, E, HID])
        W2 = sb("W2", [P, E, M, D])
        b2r = sb("b2r", [E, D])
        NVEC = 44
        V = sb("V", [P, NVEC])
        vs = sb("vs", [P, 2])
        bc = sb("bc", [P, 7, D])
        BV0, BO0, BO1, G1, C1, G2, C2 = range(7)
        bcv = sb("bcv", [P, 1024])
        CT_all = sb("CT_all", [P, BATCH, CTX])
        CN_all = sb("CN_all", [P, BATCH, CTX])

        with nc.sbuf_tensor("PARTS", [P, 4, SEQ], F32R) as PARTS:
            pass
        PTA = sb("PTA", [P, 7680])
        OTA = sb("OTA", [P, 4096])
        with nc.sbuf_tensor("QSTACK", [P, PAIRS, SEQ], F32R) as QSTACK:
            pass
        KMA = sb("KMA", [P, 8 * XK])
        VA = sb("VA", [P, 4096])
        VPA = sb("VPA", [P, 2048])
        QXA = sb("QXA", [P, 2048])
        PB = sb("PB", [P, 2, XK])
        YN = sb("YN", [P, QT, D])
        Y2 = sb("Y2", [P, QT, D])
        YT = sb("YT", [P, SEQ])
        YF = sb("YF", [P, QT, D])
        CT = sb("CT", [P, CTX])
        CN = sb("CN", [P, CTX])
        st = sb("st", [P, QT, 6])
        mv = sb("mv", [P, QT, 2])
        var = sb("var", [P, QT])
        rstd = sb("rstd", [P, QT])
        nmax = sb("nmax", [P, 2, 4])
        rsum = sb("rsum", [P, 2, 4])
        rinv = sb("rinv", [P, 2, 4])
        sm = sb("sm", [P, 16])

        KRING = sb("KRING", [P, 6, SEQ], F32R)
        PICKQ = sb("PICKQ", [P, 577], F32R)
        PICKK = sb("PICKK", [P, 578], F32R)
        row_mask = sb("row_mask", [P, 2])
        negmax = sb("negmax", [P, 2, 2, QT])
        maxparts = sb("maxparts", [P, 2, QT, 2, 2], F32R)
        ones_col = sb("ones_col", [P, 1])
        SELsum = sb("SELsum", [P, GROUPS, HEADS])
        rsums = sb("rsums", [P, QT, HEADS])

        ones = YF[:, 0, :]
        vrow = Y2[0:NVEC, 0, :]
        scratch = VA[:, 0:1155]
        w0raw = VPA[:, 0:512].rearrange("p (w d) -> p w d", w=4)
        wo0pad = VPA[:, 512:1024].rearrange("p (j g c) -> p j g c", j=4, g=4)
        idpad = VPA[:, 1024:1536].rearrange("p (j g c) -> p j g c", j=4, g=4)
        upraw = QXA[:, 0:512]
        downraw = QXA[:, 512:1024]
        ctxraw = QXA[:, 1024:1536].rearrange("p (b d) -> p b d", b=4)
        ctxn = QXA[:, 1536:2048].rearrange("p (b d) -> p b d", b=4)
        wcraw = PTA[:, 0:1280]
        wo1raw = PTA[:, 1280:2304]
        tern = PTA[:, 2304:3328].rearrange("p (w n) -> p w n", w=2)
        ternq = PTA[:, 3328:4352].rearrange("p (w n) -> p w n", w=2)
        wqkv = KMA[:, 0:384]
        gate = KMA[:, 384:896]
        val = KMA[:, 896:1408]
        proj = KMA[:, 1408:1920].rearrange("p (m d) -> p m d", m=M)
        projT = KMA[:, 1920:2432]
        pw = KMA[:, 2432:2560]
        bqkv = KMA[:, 2560:2944]
        kscale8 = KMA[:, 2944:2952]
        kbias8 = KMA[:, 2952:2960]
        kscale = KMA[:, 2960:3088]
        kbias = KMA[:, 3088:3216]
        bproj = KMA[:, 3456:3584]
        normw = KMA[:, 3584:3840]
        QTall = OTA[:, 0:2048]
        Kn = PTA[:, 0:2048].rearrange("p (t d) -> p t d", d=D)
        KTall = PTA[:, 2048:4096]
        Vn = PTA[:, 4096:6144].rearrange("p (t d) -> p t d", d=D)
        sg = [VA[:, 0:512], VA[:, 512:1024]]
        t1 = [VA[:, 1024:1536], VA[:, 1536:2048]]
        us = [VA[:, 2048:2560], VA[:, 2560:3072]]
        dg = VA[:, 3072:3584]
        du = VA[:, 3584:4096]
        hh = [OTA[:, 2048:2560], OTA[:, 2560:3072]]
        ww = [OTA[:, 3072:3584], OTA[:, 3584:4096]]
        zz = VPA[:, 512:1024]
        hTs = QXA[:, 0:512]
        dp = QXA[:, 512:640]
        dpT = QXA[:, 640:768]
        nx = [PTA[:, 6144 + 512 * i:6656 + 512 * i] for i in range(3)]
        nxT = [VA[:, 512 * i:512 * i + 512] for i in range(3)]
        nA = [QXA[:, 1024 + 128 * i:1152 + 128 * i] for i in range(3)]
        nB = [QXA[:, 1408 + 128 * i:1536 + 128 * i] for i in range(3)]
        nC = [VPA[:, 128 * i:128 * i + 128] for i in range(3)]
        aI = VPA[:, 384:512]

        qkvs = VA[:, 0:1024].rearrange("p (t w d) -> p t w d", t=QT, w=2)
        kraw = VA[:, 1024:1536].rearrange("p (t d) -> p t d", t=QT)
        sq4 = VA[:, 2048:3072]
        fh = VA[:, 0:2048].rearrange("p (m n) -> p m n", m=M)
        foT = VA[:, 2048:2560]
        fsg = VA[:, 2560:3584].rearrange("p (k n) -> p k n", k=2)
        ft = VPA[:, 512:1536].rearrange("p (k n) -> p k n", k=2)

        PSUM = stack.enter_context(nc.psum_tensor("PSUM", [P, 8, 512], F32))

        def bank(i, n=512):
            return PSUM[:, i, 0:n]

        s_x, s_w0, s_wt, s_wr, s_out = (sem(n) for n in ("x_loaded", "raw_loaded", "ttt_loaded", "rest_loaded", "stored"))
        s_const = sem("consts_ready")
        s_pad, s_absum, s_thr, s_tern = (sem(n) for n in ("pads_ready", "abs_sums", "abs_total", "ternary_ready"))
        s_tr, s_ev = sem("prep_transposed"), sem("prep_evacuated")

        class Norm:
            def __init__(self, name):
                self.var, self.rstd, self.done = sem(name + "_var"), sem(name + "_rstd"), sem(name + "_done")

        n_ctx, n_in, n_b = Norm("ctx_ln"), Norm("in_ln"), Norm("batch_ln")

        def ln_vector(dve, norm, n, srcs, dsts, rows=P):
            for j, s in enumerate(srcs):
                nc.vector.bn_stats(st[0:rows, j, :], s)
            dve.drain()
            for j in range(len(srcs)):
                nc.vector.bn_aggr(mv[0:rows, j, :], st[0:rows, j, :])
            dve.drain()
            k = len(srcs)
            nc.vector.tensor_scalar(var[0:rows, 0:k], mv[0:rows, 0:k, 1], LN_EPS, None, ALU.add).then_inc(norm.var, 1)
            dve.wait_ge(norm.rstd, n)
            for j, (s, d) in enumerate(zip(srcs, dsts)):
                last = nc.vector.tensor_scalar(d, s, mv[0:rows, j, 0:1], rstd[0:rows, j:j + 1],
                                               ALU.subtract, ALU.mult)
            last.then_inc(norm.done, 1)

        def ln_pool(pool, norm, n, rows=P, k=QT):
            pool.wait_ge(norm.var, n)
            nc.gpsimd.tensor_tensor(rstd[0:rows, 0:k], var[0:rows, 0:k], neg_half[0:rows, 0:k], ALU.pow)\
                .then_inc(norm.rstd, 1)

        prep = []

        def group(srcs, dst, rows=P, after=None):
            prep.append((srcs, dst, rows, after))

        group([vrow[:, :]], V[:, :], NVEC, None)
        group([w0raw[:, i, :] for i in range(3)], W0T[:, :, :])
        group([ttt_tile for ttt_tile in (proj[:, m, :] for m in range(M))], projT)
        group([wcraw[:, i * P:(i + 1) * P] for i in range(0, 4)], WcT[:, 0:512])
        group([wcraw[:, i * P:(i + 1) * P] for i in range(4, 8)], WcT[:, 512:1024])
        group([wcraw[:, i * P:(i + 1) * P] for i in range(8, 10)], WcT[:, 1024:1280])
        group([wo1raw[:, i * P:(i + 1) * P] for i in range(0, 4)], Wo1T[:, 0:4, :])
        group([wo1raw[:, i * P:(i + 1) * P] for i in range(4, 8)], Wo1T[:, 4:8, :])
        group([ctxraw[0:CTX, b, :] for b in range(BATCH)], CT_all[:, :, :], CTX)
        group([wo0pad[:, j, :, :] for j in range(4)], WoA[:, :, :], P, "pads")
        group([idpad[:, j, :, :] for j in range(4)], SEL[:, :, :], P, "pads")
        group([ctxn[0:CTX, b, :] for b in range(BATCH)], CN_all[:, :, :], CTX, "ctx")
        group([ternq[:, 0, i * P:(i + 1) * P] for i in range(4)], upT[:, :], P, "tern")
        group([ternq[:, 1, i * P:(i + 1) * P] for i in range(4)], downT[:, :, :], P, "tern")
        NPREP = len(prep)

        NLN = 8
        NTR = 6
        s_zero = sem("value_pads_zero")
        s_ctx = sem("context_row_ready")
        s_bT, s_bTs = sem("rows_transposed"), sem("rows_T_ready")
        s_pow, s_powd = sem("square_sums_ready"), sem("roots_ready")
        s_rowdone = sem("row_done")

        (s_scores, s_max, s_exp, s_norm, s_turned, s_moved, s_values, s_outs) = (
            sem(w) for w in ("scores_ready", "maxima_ready", "exp_ready", "probs_normalised", "probs_turned", "probs_T_ready",
                             "values_ready", "values_copied"))

        class Attention:
            all_units, all_groups = 16 + 32, 4 + 4

            def __init__(self, before, units, group, out_banks, free):
                self.units, self.group, self.out_banks, self.free = units, group, out_banks, free
                self.groups = units // group
                self.first_unit = before.first_unit + before.units if before else 0
                self.first_group = before.first_group + before.groups if before else 0

            def unit(self, b, i):
                return b * self.all_units + (self.first_unit + i)

            def summed(self, b, v):
                return b * self.all_groups + (self.first_group + v)

        def attention_tensor(pe, b, a, score, turn, value):
            U = a.units

            def values(v):
                pe.wait_ge(s_moved, a.unit(b, (v + 1) * a.group))
                if v >= a.out_banks:
                    pe.wait_ge(s_outs, a.summed(b, v + 1 - a.out_banks))
                value(v).then_inc(s_values, 1)

            for i in range(U + 2):
                if i < U:
                    if i >= 2:
                        pe.wait_ge(s_exp, a.unit(b, i - 1))
                    score(i).then_inc(s_scores, 1)
                k = i - 2
                if k >= 0:
                    pe.wait_ge(s_norm, a.unit(b, k + 1))
                    if k >= 2:
                        pe.wait_ge(s_moved, a.unit(b, k - 1))
                    turn(k).then_inc(s_turned, 1)
                    if k >= a.group and k % a.group == 1:
                        values(k // a.group - 1)
            values(a.groups - 1)

        def attention_scalar(act, b, a, exp, move):
            U = a.units
            for i in range(U + 2):
                if i < U:
                    act.wait_ge(s_max, a.unit(b, i + 1))
                    if i >= 2:
                        act.wait_ge(s_turned, a.unit(b, i - 1))
                    exp(i).then_inc(s_exp, 1)
                k = i - 2
                if k >= 0:
                    act.wait_ge(s_turned, a.unit(b, k + 1))
                    if a.free(k):
                        act.wait_ge(s_values, a.summed(b, a.free(k)))
                    move(k).then_inc(s_moved, 1)

        def attention_vector(dve, b, a, maximum, normalise, copy_out):
            U = a.units

            def out_of(v):
                dve.wait_ge(s_values, a.summed(b, v + 1))
                copy_out(v).then_inc(s_outs, 1)

            done = 0
            for i in range(U + 1):
                if i < U:
                    dve.wait_ge(s_scores, a.unit(b, i + 1))
                    maximum(i).then_inc(s_max, 1)
                if i >= 1:
                    dve.wait_ge(s_exp, a.unit(b, i))
                    normalise(i - 1).then_inc(s_norm, 1)
                if i == a.group * (done + 1) + 4:
                    out_of(done)
                    done += 1
            for v in range(done, a.groups):
                out_of(v)

        GH = GROUPS
        a0 = Attention(None, 16, 4, 2, lambda k: k // 4 - 1 if k % 4 == 0 and k >= 8 else 0)
        ax = Attention(a0, 32, 8, 1, lambda k: (k // 4 - 3) // 2 + 1 if k % 4 == 0 and k >= 12 else 0)

        (m_parts, m_picked, m_stacked, m_keys, m_scores, m_max, m_split, m_turned, m_rows, m_scoresT, m_exp, m_acc01, m_acc23,
         m_acc, m_sums, m_inv, m_spread, m_norm, m_values, m_outs) = (sem("m_" + w) for w in (
            "parts", "picked", "stacked", "keys", "scores", "max", "max_split", "max_turned", "max_rows", "scores_T",
            "exp", "sum01", "sum23", "sum0123", "sums", "inverted", "spread", "normalised", "values", "values_copied"))

        class Paired:
            def __init__(self, row, causal):
                self.row, self.causal = row, causal

            def stacks(self, b, s):
                return (2 * b + self.row) * PAIRS + s

            def groups(self, b, v):
                return b * 12 + (8 if self.causal else 0) + v

            def width(self, t):
                return (t + 1) * P if self.causal else SEQ

            def first(self, c):
                return c * P if self.causal else 0

            def probsT(self, s, c):
                if self.causal:
                    w = SEQ - c * P
                    at = (s % 3) * 2560 + 2 * sum(SEQ - i * P for i in range(c))
                    return PTA[:, at:at + 2 * w].rearrange("p (e q) -> p e q", e=2)
                at = (4 * s + c) % 7 * 1024
                return PTA[:, at:at + 1024].rearrange("p (e q) -> p e q", e=2)

        full, causal = Paired(0, False), Paired(1, True)

        def paired_tensor(pe, b, a, value):
            T = nc.tensor
            for i in range(PAIRS):
                keys, s0 = i % 2 == 0, 2 * (i // 2)
                pe.wait_ge(m_parts, 4 * (2 * b + a.row) + 4)
                if i >= 2:
                    pe.wait_ge(m_stacked, a.stacks(b, i - 1))
                for j in range(2):
                    out_bank = (6 if keys else 0) + j
                    for part in range(2):
                        if keys:
                            at = 64 * (s0 + j) + (2, 0)[part]
                            pick = PICKK[:, at:at + P]
                        else:
                            at = 64 * (s0 + j) + (1, 0)[part]
                            pick = PICKQ[:, at:at + P]
                        last = T.matmul(bank(out_bank), pick, PARTS[:, (2 if keys else 0) + part, :],
                                        start=(part == 0), stop=(part == 1))
                last.then_inc(m_picked, 1)

            def scores(s, j):
                e, t = j // 4, j % 4
                w = a.width(t)
                if s == 0 and j == 0:
                    pe.wait_ge(m_stacked, a.stacks(b, PAIRS))
                if t == 0:
                    pe.wait_ge(m_keys, 2 * a.stacks(b, s) + e + 1)
                if j >= 2 or s >= 1:
                    pe.wait_ge(m_max, 8 * a.stacks(b, s) + j - 1)
                last = T.matmul(bank(j % 2, w), QSTACK[0:96, s, t * P:(t + 1) * P], KRING[0:96, (2 * s + e) % 6, 0:w],
                                start=True, stop=not a.causal)
                if a.causal:
                    last = T.matmul(PSUM[:, j % 2, t * P:(t + 1) * P], ident_bf[:, :], causal_bf[:, :], start=False, stop=True)
                last.then_inc(m_scores, 1)

            def turn_maxima(s):
                pe.wait_ge(m_split, a.stacks(b, s + 1))
                if s >= 3 and not a.causal:
                    pe.wait_ge(m_norm, b * PAIRS + s - 2)
                elif s >= 1:
                    pe.wait_ge(m_rows, a.stacks(b, s))
                for t in range(QT):
                    last = T.matmul(PSUM[96:100, 7, t * P:(t + 1) * P],
                                    maxparts[:, s % 2, t, :, :].rearrange("p e w -> p (e w)").bitcast(F32), ident[:, :],
                                    start=True, stop=True)
                last.then_inc(m_turned, 1)

            def scores_T(s, c):
                k = 4 * s + c
                if c == 0:
                    pe.wait_ge(m_rows, a.stacks(b, s + 1))
                if k >= 2:
                    pe.wait_ge(m_exp, 4 * a.stacks(b, 0) + k - 1)
                w = SEQ - a.first(c)
                for e in range(2):
                    dst = PSUM[:, 2 + 2 * (k % 2) + e, :]
                    last = T.matmul(dst[:, 0:w], KRING[:, (2 * s + e) % 6, c * P:(c + 1) * P], QSTACK[:, s, a.first(c):SEQ],
                                    start=True, stop=not a.causal)
                    if a.causal:
                        last = T.matmul(dst[:, 0:P], causal_bf[:, :], ident_bf[:, :], start=False, stop=True)
                last.then_inc(m_scoresT, 1)

            def sums(s):
                pe.wait_ge(m_acc, b * PAIRS + s + 1)
                pe.wait_ge(m_rows, a.stacks(b, min(s + 3, PAIRS)))
                if s:
                    pe.wait_ge(m_norm, b * PAIRS + s)
                for t in range(QT):
                    for e in range(2):
                        at = e * SEQ + t * P
                        last = T.matmul(PSUM[:, 7, 2 * t + e:2 * t + e + 1], acc01[s % 2][:, at:at + P], ones_col[:, :],
                                        start=True, stop=True)
                last.then_inc(m_sums, 1)

            def spread(s):
                pe.wait_ge(m_inv, b * PAIRS + s + 1)
                for t in range(QT):
                    for e in range(2):
                        last = T.matmul(PSUM[e * VD:(e + 1) * VD, 7, t * P:(t + 1) * P],
                                        inv[:, 2 * t + e:2 * t + e + 1].to_broadcast([P, VD]), ident[:, :], start=True, stop=True)
                last.then_inc(m_spread, 1)

            def tiles(first, n):
                for i in range(first, min(first + n, 8 * PAIRS)):
                    scores(i // 8, i % 8)

            tiles(0, 10)
            turn_maxima(0)
            tiles(10, 2)
            for s in range(PAIRS):
                ahead = 8 * s + 12
                scores_T(s, 0)
                tiles(ahead, 1)
                if s:
                    value(s - 1, 3)
                tiles(ahead + 1, 1)
                if s >= 2 and not a.causal:
                    spread(s - 2)
                scores_T(s, 1)
                tiles(ahead + 2, 2)
                value(s, 0)
                scores_T(s, 2)
                tiles(ahead + 4, 1)
                if s + 1 < PAIRS:
                    turn_maxima(s + 1)
                value(s, 1)
                tiles(ahead + 5, 1)
                scores_T(s, 3)
                tiles(ahead + 6, 1)
                value(s, 2)
                tiles(ahead + 7, 1)
                if s and not a.causal:
                    sums(s - 1)
            value(PAIRS - 1, 3)
            if not a.causal:
                spread(PAIRS - 2)
                sums(PAIRS - 1)
                spread(PAIRS - 1)

        def paired_scalar(act, b, a):
            A = nc.scalar
            for i in range(PAIRS):
                keys, s0 = i % 2 == 0, 2 * (i // 2)
                act.wait_ge(m_picked, a.stacks(b, i + 1))
                if keys:
                    last = A.activation(KSTACK[:, s0:s0 + 2, :], PSUM[0:64, 6:8, :], ACT.Copy)
                else:
                    last = A.activation(QSTACK[:, s0:s0 + 2, :], PSUM[:, 0:2, :], ACT.Copy)
                last.then_inc(m_stacked, 1)

            def max_rows(s):
                act.wait_ge(m_turned, a.stacks(b, s + 1))
                A.activation(QSTACK[96:100, s, :], PSUM[96:100, 7, :], ACT.Copy).then_inc(m_rows, 1)

            def copy_out(s):
                if not a.causal or s % 2:
                    v = s // 2 if a.causal else s
                    act.wait_ge(m_values, a.groups(b, v + 1))
                    A.activation(OT[:, v, :], bank(6), ACT.Copy).then_inc(m_outs, 1)

            max_rows(0)
            for s in range(PAIRS):
                for c in range(4):
                    k = 4 * s + c
                    act.wait_ge(m_scoresT, 4 * a.stacks(b, 0) + k + 1)
                    if a.causal:
                        if c == 0 and s >= 3:
                            act.wait_ge(m_values, a.groups(b, (s - 3) // 2 + 1))
                    elif k >= 7:
                        act.wait_ge(m_values, a.groups(b, (k - 7) // 4 + 1))
                        if c < 3:
                            act.wait_ge(m_acc, b * PAIRS + s - 1)
                        else:
                            act.wait_ge(m_acc01, b * PAIRS + s)
                    A.activation(a.probsT(s, c), PSUM[:, 2 + 2 * (k % 2):4 + 2 * (k % 2), 0:SEQ - a.first(c)], ACT.Exp)                        .then_inc(m_exp, 1)
                    if c == 0 and s:
                        copy_out(s - 1)
                    if c == 2 and s + 1 < PAIRS:
                        max_rows(s + 1)
            copy_out(PAIRS - 1)

        def paired_vector(dve, b, a):
            Vv = nc.vector

            def maxima(s, j):
                e, t = j // 4, j % 4
                dve.wait_ge(m_scores, 8 * a.stacks(b, s) + j + 1)
                Vv.tensor_reduce(negmax[:, s % 2, e, t:t + 1], bank(j % 2, a.width(t)), AX.X, ALU.max, negate=True)                    .then_inc(m_max, 1)

            def split_maxima(s):
                dve.drain()
                nm = negmax[:, s % 2, :, :].rearrange("p e t -> p t e")
                Vv.tensor_copy(maxparts[:, s % 2, :, :, 0], nm)
                dve.drain()
                Vv.tensor_tensor(maxparts[:, s % 2, :, :, 1], nm, maxparts[:, s % 2, :, :, 0].bitcast(F32), ALU.subtract)                    .then_inc(m_split, 1)

            def invert(s):
                dve.wait_ge(m_sums, b * PAIRS + s + 1)
                Vv.reciprocal(inv, PSUM[:, 7, 0:2 * QT]).then_inc(m_inv, 1)

            def normalise(s):
                dve.wait_ge(m_outs, a.groups(b, s + 1))
                dve.wait_ge(m_spread, b * PAIRS + s + 1)
                Vv.tensor_tensor(OT[:, s, :], OT[:, s, :], bank(7), ALU.mult).then_inc(m_norm, 1)

            def tiles(first, n):
                for i in range(first, min(first + n, 8 * PAIRS)):
                    maxima(i // 8, i % 8)
                    if i % 8 == 7:
                        split_maxima(i // 8)

            def add23(s):
                dve.wait_ge(m_exp, 4 * a.stacks(b, s + 1))
                if s:
                    dve.wait_ge(m_acc, b * PAIRS + s)
                Vv.tensor_tensor(acc23.rearrange("p (e q) -> p e q", e=2), a.probsT(s, 2), a.probsT(s, 3), ALU.add)                    .then_inc(m_acc23, 1)

            tiles(0, 12)
            for s in range(PAIRS):
                ahead = 8 * s + 12
                tiles(ahead, 2)
                if s and not a.causal:
                    add23(s - 1)
                tiles(ahead + 2, 1)
                if s >= 2 and not a.causal:
                    normalise(s - 2)
                tiles(ahead + 3, 1)
                tiles(ahead + 4, 4)
                if s and not a.causal:
                    invert(s - 1)
            if not a.causal:
                add23(PAIRS - 1)
                normalise(PAIRS - 2)
                invert(PAIRS - 1)
                normalise(PAIRS - 1)

        def paired_pool(pool, b, a):
            g = nc.gpsimd

            def keys(s):
                for e in range(2):
                    rows = slice(LANE * e, LANE * (e + 1))
                    g.tensor_tensor(KRING[rows, (2 * s + e) % 6, :], KSTACK[rows, s, :],
                                    ones_col[rows, 0:1].to_broadcast([LANE, SEQ]), ALU.mult).then_inc(m_keys, 1)

            pool.wait_ge(m_stacked, a.stacks(b, 1))
            keys(0)
            keys(1)
            pool.wait_ge(m_stacked, a.stacks(b, 3))
            keys(2)
            pool.drain()
            for s in range(PAIRS):
                if not a.causal:
                    pool.wait_ge(m_exp, 4 * a.stacks(b, s) + 2)
                    if s >= 2:
                        pool.wait_ge(m_sums, b * PAIRS + s - 1)
                    g.tensor_tensor(acc01[s % 2].rearrange("p (e q) -> p e q", e=2), a.probsT(s, 0), a.probsT(s, 1), ALU.add)                        .then_inc(m_acc01, 1)
                    pool.drain()
                if s + 3 < PAIRS:
                    pool.wait_ge(m_stacked, a.stacks(b, (s + 3) // 2 * 2 + 1))
                    pool.wait_ge(m_scoresT, 4 * a.stacks(b, s + 1))
                    keys(s + 3)
                if not a.causal:
                    pool.drain()
                    pool.wait_ge(m_acc23, b * PAIRS + s + 1)
                    g.tensor_tensor(acc01[s % 2], acc01[s % 2], acc23, ALU.add).then_inc(m_acc, 1)
            pool.drain()

        s_b_k, s_b_v, s_b_q, s_b_ks, s_b_vs, s_b_qs, s_b_km, s_b_o = (sem("x0_" + n) for n in (
            "k", "v", "q", "k_biased", "v_biased", "q_scaled", "k_masked", "out"))
        s_c_u, s_c_g, s_c_r1, s_c_T, s_c_Ts, s_c_o, s_c_x = (sem("ffn_" + n) for n in (
            "up", "gelu", "rms", "turned", "moved", "down", "added"))
        s_d_q, s_d_qb, s_d_v, s_d_vs, s_d_o = (sem("a1_" + n) for n in (
            "qk", "qk_biased", "v", "v_ready", "out"))
        s_e_q, s_e_qs, s_e_k, s_e_ks, s_e_v, s_e_vs, s_e_o = (sem("x1_" + n) for n in (
            "q", "q_ready", "k", "k_masked", "v", "v_ready", "out"))
        s_f_q, s_f_qs, s_f_v, s_f_vs, s_f_o, s_f_y, s_f_g, s_f_gs, s_f_d, s_f_e, s_f_c, s_f_cT, s_f_cTs, s_f_b2, s_f_acc0 = (
            sem("f1_" + n) for n in ("qk", "qk_ready", "v", "v_ready", "attn", "y_ready", "gate", "logits",
                                     "top_gap", "top_exp", "combine", "combine_turned", "combine_T", "b2", "acc_started"))
        s_f_h, s_f_hs, s_f_dn, s_f_acc = (sem("moe_" + n) for n in ("hidden", "relu", "down", "added"))

        PSF = PSUM[:, :, :].rearrange("p b n -> p (b n)")
        VP = VPA[:, :].rearrange("p (t h c) -> p t h c", t=QT, h=HEADS)
        QS = QXA[:, 0:512]
        Qraw = QXA[:, 512:1024]
        Kraw = QXA[:, 1024:1536]
        KT0 = QXA[:, 1536:2048]
        KM0 = KMA[:, 0:HEADS * CTX].rearrange("p (h k) -> p h k", h=HEADS)
        KSTACK = OTA[0:64, :].rearrange("p (s k) -> p s k", s=PAIRS)
        acc01 = [QXA[:, 0:1024], PB[:, :, :].rearrange("p r n -> p (r n)")[:, 0:1024]]
        acc23 = QXA[:, 1024:2048]
        inv = rinv[:, :, :].rearrange("p a b -> p (a b)")
        KM8 = KMA[:, :].rearrange("p (h k) -> p h k", h=8)
        PT0 = PTA[:, 0:4096].rearrange("p (r g q) -> p r g q", r=2, g=4)
        PTe = PTA[:, :].rearrange("p (r k q) -> p r k q", r=3, k=5)
        OT = OTA[:, :].rearrange("p (g q) -> p g q", q=SEQ)
        V1 = VA[:, :].rearrange("p (k n) -> p k n", k=QT)
        VX = VA[:, 0:2560].rearrange("p (k n) -> p k n", k=5)
        HC = VA[:, 0:2048].rearrange("p (t n) -> p t n", t=QT)
        HTC = PTA[:, 0:2048].rearrange("p (t n) -> p t n", t=QT)
        HE = PTA[:, 0:4096].rearrange("p (r m n) -> p r m n", r=2, m=M)
        QX = QXA[:, :].rearrange("p (g q) -> p g q", q=SEQ)
        ssq = sb("ssq", [P, 2, QT])
        root = sb("root", [P, 2, QT])
        logit = sb("logit", [P, QT, E])
        top = sb("top", [P, QT, E])
        topi = sb("topi", [P, QT, E], U32)
        topf = logit[:, :, :]
        comb = sb("comb", [P, QT, E])
        comb2 = rsums[:, :, 0:E]
        tw = rsums[:, :, E:E + 4]
        combT = QXA[0:E, 512:1024]

        GM, BM, GL, BL, BQ0, BK0, BCQ, BCK = range(8)
        B1C = 8
        QSC, QBI, KSC, KBI = range(40, 44)

        block = stack.enter_context(nc.Block())

        s_yT, s_yTs = sem("in_transposed"), sem("in_yT_ready")
        s_qkv, s_qkvb, s_ss, s_nrm, s_qk = (sem(n) for n in ("qkv_ready", "qkv_biased", "head_sums", "head_norms", "qk_ready"))
        s_qkT, s_qkTs, s_kn, s_sqr, s_uc = (sem(n) for n in ("qk_transposed", "qkT_stored", "k_stored", "qk_squared", "value_copied"))
        s_gu, s_sig, s_t, s_h, s_w = (sem(n) for n in ("gu_ready", "sigmoid_ready", "silu_ready", "h_ready", "w_ready"))
        s_hT, s_hTs, s_pred, s_dp, s_dpT, s_dpTs, s_dh, s_dgu = (sem(n) for n in (
            "hT_ready", "hT_stored", "pred_ready", "dpred_ready", "dpredT_ready", "dpredT_stored", "dh_ready", "dgu_ready"))
        s_grad, s_gs, s_sq, s_tot, s_tots, s_nrt, s_x0 = (sem(n) for n in (
            "grads_ready", "grads_stored", "square_sums", "square_total", "total_stored", "norm_ready", "x_scaled"))
        s_xt0, s_xt0s = sem("ns_xT_ready"), sem("ns_xT_stored")
        s_A, s_As, s_A2, s_B, s_XN, s_XTN, s_XNs, s_XTNs, s_upd = (sem(n) for n in (
            "ns_A", "ns_A_stored", "ns_A2", "ns_B", "ns_X", "ns_XT", "ns_X_stored", "ns_XT_stored", "weights_updated"))
        s_fg, s_fu, s_fs, s_ft, s_fh, s_fo, s_fos, s_fy, s_fx = (sem(n) for n in (
            "f_gate", "f_val", "f_sigmoid", "f_silu", "f_h", "f_o", "f_oT", "f_y", "f_x"))

        @block.sync
        def _(sp):
            def load(dst, src, s):
                sp.dma_start(dst, src).then_inc(s, 16)

            load(X[:, :, :], x.rearrange("b (t p) d -> p (b t) d", p=P), s_x)
            for i, w in enumerate((x1_gm, x1_bm, x1_gl, x1_bl, x0_bq, x0_bk)):
                load(vrow[i:i + 1, :], w.rearrange("(o d) -> o d", o=1), s_w0)
            load(vrow[6:8, :], a1_bc[0:256].rearrange("(o d) -> o d", o=2), s_w0)
            load(vrow[8:40, :], f1_b1.rearrange("e (m d) -> (e m) d", d=D), s_w0)
            for i, w in enumerate((qn_scale, qn_bias, kn_scale, kn_bias)):
                load(vrow[40 + i:41 + i, :].rearrange("o (h d) -> o h d", d=HD),
                     w.rearrange("(o d) -> o d", o=1).unsqueeze(1).to_broadcast([1, HEADS, HD]), s_w0)
            for i, w in enumerate((x0_Wq, x0_Wk, x0_Wv, x0_Wo)):
                load(w0raw[:, i, :], w, s_w0)
            load(proj, ttt_proj.rearrange("(m p) d -> p m d", p=P), s_w0)
            load(wcraw.rearrange("p (t d) -> p t d", d=D), a1_Wc.rearrange("(t p) d -> p t d", p=P), s_w0)
            load(wo1raw, a1_Wo, s_w0)
            load(ctxraw[0:CTX, :, :], ctx_1024.rearrange("b s d -> s b d"), s_w0)
            load(upraw.rearrange("p (t d) -> p t d", d=D), w_up.rearrange("(t p) d -> p t d", p=P), s_w0)
            load(downraw, w_down, s_w0)
            load(wqkv, qkv_w, s_wt)
            load(gate, ttt_gate, s_wt)
            load(val, ttt_val, s_wt)
            load(pw, proj_w, s_wt)
            load(bqkv, qkv_b.partition_broadcast(P), s_wt)
            load(bproj, proj_b.partition_broadcast(P), s_wt)
            load(kscale8, kn_scale.partition_broadcast(P), s_wt)
            load(kbias8, kn_bias.partition_broadcast(P), s_wt)
            for i, w in enumerate((x0_bv, x0_bo, a1_bo, f1_g1, f1_c1, f1_g2, f1_c2)):
                load(bc[:, i, :], w.partition_broadcast(P), s_wr)
            load(bcv[:, :], a1_bc[256:1280].partition_broadcast(P), s_wr)
            load(Wq1[:, :], x1_Wq, s_wr)
            load(Wkv1[:, :], x1_Wkv, s_wr)
            load(Wout1[:, :, :], x1_Wout.rearrange("(m p) d -> p m d", p=P), s_wr)
            for i, w in enumerate((f1_Wq, f1_Wk, f1_Wv)):
                load(WF[:, i, :, :], w.rearrange("h d f -> d h f"), s_wr)
            load(gateW[:, :], f1_gate, s_wr)
            load(b2r[:, :], f1_b2, s_wr)
            load(W1[:, :, :], f1_W1.rearrange("e d f -> d e f"), s_wr)
            load(W2[:, :, :, :].rearrange("p e m d -> p (e m) d"), f1_W2.rearrange("e (m p) d -> p (e m) d", p=P), s_wr)
            with sp.Fori(0, BATCH) as b:
                sp.wait_ge(s_rowdone, b + 1)
                sp.dma_start(out[bass.ds(b, 1), :, :].rearrange("o (t p) d -> p (o t) d", p=P),
                             X[:, bass.ds(b * QT, QT), :]).then_inc(s_out, 16)
            sp.wait_ge(s_out, 16 * BATCH)

        N_W0, N_WT, N_WR = 16 * 22, 16 * 8, 16 * 18

        @block.gpsimd
        def _(pool):
            g = nc.gpsimd
            g.memset(ident[:, :], 0.0)
            g.memset(ones[:, :], 1.0)
            g.memset(head_mask[:, :], 1.0)
            g.memset(half_mask[:, :], 0.0)
            g.memset(causal_bf[:, :], 0.0)
            g.memset(neg_half[:, :], -0.5)
            g.memset(pos_half[:, :], 0.5)
            g.memset(VPA[:, 512:1536], 0.0)
            g.memset(ones_col[:, :], 1.0)
            g.memset(scratch, 0.0)
            g.memset(SELsum[:, :, :], 0.0)
            g.memset(row_mask[:, :], 1.0)
            g.iota(iota_i[:, :], pattern=[[1, E]], base=0, channel_multiplier=0)
            pool.drain()
            g.tensor_copy(iota8[:, :], iota_i[:, :])
            g.memset(half_mask[0:64, 0:1], 1.0)
            pool.drain()
            g.memset(half_mask[64:128, 1:2], 1.0)
            pool.drain()
            g.affine_select(out=ident[:, :], in_=ident[:, :], compare_op=ALU.not_equal, fill=1.0, base=0,
                            pattern=[[-1, P]], channel_multiplier=1)
            g.affine_select(out=head_mask[:, :], in_=head_mask[:, :], compare_op=ALU.is_ge, fill=0.0, base=0,
                            pattern=[[-HD, HEADS]], channel_multiplier=1)
            g.affine_select(out=causal_bf[:, :], in_=causal_bf[:, :], compare_op=ALU.is_ge, fill=MASKED, base=0,
                            pattern=[[-1, P]], channel_multiplier=1)
            pq, pk = scratch[:, 0:577], scratch[:, 577:1155]
            for i in range(2):
                g.affine_select(out=pq, in_=pq, compare_op=ALU.not_equal, fill=1.0, base=1 + 2 * i, pattern=[[-1, 577]],
                                channel_multiplier=4)
                g.affine_select(out=pk, in_=pk, compare_op=ALU.not_equal, fill=1.0, base=2 + i, pattern=[[-1, 578]],
                                channel_multiplier=4)
                pool.drain()
            g.tensor_copy(PICKQ[:, :], pq)
            g.tensor_copy(PICKK[:, :], pk)
            g.affine_select(out=SELsum[:, :, :], in_=SELsum[:, :, :], compare_op=ALU.not_equal, fill=1.0, base=-HD,
                            pattern=[[P, GROUPS], [-LANE, HEADS]], channel_multiplier=1)
            g.affine_select(out=row_mask[:, :], in_=row_mask[:, :], compare_op=ALU.is_ge, fill=0.0, base=-96,
                            pattern=[[-2, 2]], channel_multiplier=1)
            pool.drain()
            g.affine_select(out=row_mask[:, :], in_=row_mask[:, :], compare_op=ALU.is_ge, fill=0.0, base=97,
                            pattern=[[2, 2]], channel_multiplier=-1)
            pool.drain()
            for i in range(6):
                g.tensor_copy(KRING[:, i, :], row_mask[:, i % 2:i % 2 + 1].to_broadcast([P, SEQ]))
            pool.drain()
            g.affine_select(out=head_mask[:, :], in_=head_mask[:, :], compare_op=ALU.is_ge, fill=0.0, base=HD - 1,
                            pattern=[[HD, HEADS]], channel_multiplier=-1)
            g.tensor_copy(ident_bf[:, :], ident[:, :])
            g.tensor_scalar(idpad[:, :, :, 0:HD], ident[:, :].rearrange("p (j g c) -> p j g c", j=4, g=4),
                            1.0, None, ALU.mult).then_inc(s_const, 1)
            pool.wait_ge(s_const, 1)
            pool.wait_ge(s_w0, N_W0)
            g.tensor_copy(wo0pad[:, :, :, 0:HD], w0raw[:, 3, :].rearrange("p (j g c) -> p j g c", j=4, g=4))\
                .then_inc(s_pad, 1)
            ln_pool(pool, n_ctx, 1, CTX)
            with pool.Fori(0, BATCH) as c:
                ln_pool(pool, n_in, c + 1)
            with pool.Fori(0, STEPS) as step:
                for t in range(TILES):
                    n, par = step * TILES + t, t % 2
                    pool.wait_ge(s_t, n + 1)
                    g.tensor_tensor(zz, sg[par], t1[par], ALU.mult)
                    if t >= 2:
                        pool.wait_ge(s_dgu, n - 1)
                    g.tensor_tensor(ww[par], sg[par], t1[par], ALU.add)
                    pool.drain()
                    g.tensor_tensor(ww[par], ww[par], zz, ALU.subtract)
                    pool.drain()
                    pool.wait_ge(s_uc, n + 1)
                    g.tensor_tensor(ww[par], ww[par], us[par], ALU.mult).then_inc(s_w, 1)
                pool.wait_ge(s_tots, step + 1)
                g.tensor_tensor(sm[:, 8:11], sm[:, 4:7], pos_half[:, 0:3], ALU.pow).then_inc(s_nrt, 1)


            with pool.Fori(0, BATCH) as b:
                g.tensor_copy(CT[:, :], CT_all[:, bass.ds(b, 1), :].rearrange("p o s -> p (o s)"))
                g.tensor_copy(CN[:, :], CN_all[:, bass.ds(b, 1), :].rearrange("p o s -> p (o s)")).then_inc(s_ctx, 1)
                ln = iter(range(1, NLN + 1))

                def norm():
                    ln_pool(pool, n_b, b * NLN + next(ln))

                norm()
                norm()
                for i in range(2):
                    pool.wait_ge(s_pow, 2 * b + i + 1)
                    g.tensor_tensor(root[:, i, :], ssq[:, i, :], pos_half[:, 0:QT], ALU.pow).then_inc(s_powd, 1)
                norm()
                paired_pool(pool, b, full)
                norm()
                norm()
                norm()
                paired_pool(pool, b, causal)
                norm()
                norm()
                pool.wait_ge(s_rowdone, b + 1)

        @block.tensor
        def _(pe):
            T = nc.tensor
            pe.wait_ge(s_const, 1)
            pe.wait_ge(s_w0, N_W0)
            pe.wait_ge(s_absum, 1)
            T.matmul(bank(7, 2), ones[:, :], sm[:, 0:2], start=True, stop=True).then_inc(s_thr, 1)
            for i, (srcs, dst, rows, after) in enumerate(prep):
                if after == "pads":
                    pe.wait_ge(s_pad, 1)
                if after == "ctx":
                    pe.wait_ge(n_ctx.done, 1)
                if after == "tern":
                    pe.wait_ge(s_tern, 1)
                if i >= 7:
                    pe.wait_ge(s_ev, i - 6)
                for j, s in enumerate(srcs):
                    last = T.transpose(PSUM[:, i % 7, j * rows:(j + 1) * rows], s, ident[0:rows, 0:rows])
                last.then_inc(s_tr, 1)
            pe.wait_ge(s_ev, NPREP)
            pe.wait_ge(s_wt, N_WT)
            with pe.Fori(0, BATCH) as c:
                pe.wait_ge(n_in.done, c + 1)
                for j in range(QT):
                    last = T.transpose(PSUM[:, 0, j * P:(j + 1) * P], YN[:, j, :], ident[:, :])
                last.then_inc(s_yT, 1)
                pe.wait_ge(s_yTs, c + 1)
                for j in range(QT):
                    T.matmul(PSUM[:, 1 + j, 0:384], YT[:, j * P:(j + 1) * P], wqkv, start=True, stop=True)\
                        .then_inc(s_qkv, 1)
                for w in range(2):
                    pe.wait_ge(s_qk, c + 1)
                    for j in range(QT):
                        last = T.transpose(PSUM[:, 5 + w, j * P:(j + 1) * P], qkvs[:, j, w, :], ident[:, :])
                    last.then_inc(s_qkT, 1)
            pe.wait_ge(s_qkTs, 2 * BATCH)
            pe.wait_ge(s_kn, BATCH)

            with pe.Fori(0, STEPS) as step:
                def gate_val(t):
                    T.matmul(bank(0), KTall[:, t * P:(t + 1) * P], gate, start=True, stop=True)
                    T.matmul(bank(1), KTall[:, t * P:(t + 1) * P], val, start=True, stop=True).then_inc(s_gu, 1)

                def up_grads(t):
                    pe.wait_ge(s_dgu, step * TILES + t + 1)
                    T.matmul(bank(5), Kn[:, t, :], dg, start=(t == 0), stop=(t == TILES - 1))
                    return T.matmul(bank(6), Kn[:, t, :], du, start=(t == 0), stop=(t == TILES - 1))

                gate_val(0)
                for t in range(TILES):
                    n, par = step * TILES + t, t % 2
                    pe.wait_ge(s_h, n + 1)
                    for m in range(M):
                        last = T.transpose(PSUM[:, 2, m * P:(m + 1) * P], hh[par][:, m * P:(m + 1) * P], ident[:, :])
                    last.then_inc(s_hT, 1)
                    if t + 1 < TILES:
                        pe.wait_ge(s_uc, n + 1)
                        gate_val(t + 1)
                    if t:
                        up_grads(t - 1)
                    pe.wait_ge(s_hTs, n + 1)
                    for m in range(M):
                        last = T.matmul(bank(3, P), hTs[:, m * P:(m + 1) * P], proj[:, m, :], start=(m == 0), stop=(m == M - 1))
                    last.then_inc(s_pred, 1)
                    pe.wait_ge(s_dp, n + 1)
                    T.transpose(PSUM[:, 3, 128:256], dp, ident[:, :]).then_inc(s_dpT, 1)
                    T.matmul(bank(7), dp, hh[par], start=(t == 0), stop=(t == TILES - 1))
                    pe.wait_ge(s_dpTs, n + 1)
                    T.matmul(bank(4), dpT, projT, start=True, stop=True).then_inc(s_dh, 1)
                up_grads(TILES - 1).then_inc(s_grad, 1)
                pe.wait_ge(s_sq, step + 1)
                T.matmul(bank(0, 3), ones[:, :], sm[:, 0:3], start=True, stop=True).then_inc(s_tot, 1)
                for i in range(3):
                    pe.wait_ge(s_x0, step * 3 + i + 1)
                    for m in range(M):
                        last = T.transpose(PSUM[:, 1 + i, m * P:(m + 1) * P], nx[i][:, m * P:(m + 1) * P], ident[:, :])
                    last.then_inc(s_xt0, 1)
                with pe.Fori(0, NS_ITERS) as it:
                    pe.wait_ge(s_xt0s, step * 3 + 3)
                    k = (step * NS_ITERS + it) * 3
                    for i in range(3):
                        for m in range(M):
                            last = T.matmul(PSUM[:, i, 0:P], nxT[i][:, m * P:(m + 1) * P], nxT[i][:, m * P:(m + 1) * P],
                                            start=(m == 0), stop=(m == M - 1))
                        last.then_inc(s_A, 1)
                    for i in range(3):
                        pe.wait_ge(s_As, k + i + 1)
                        T.matmul(PSUM[:, i, P:2 * P], nA[i], nA[i], start=True, stop=True).then_inc(s_A2, 1)
                    for i, (bx, bt) in enumerate(((3, 4), (5, 6), (7, 3))):
                        pe.wait_ge(s_B, k + i + 1)
                        T.matmul(bank(bx), nB[i], nx[i], start=True, stop=True).then_inc(s_XN, 1)
                        if i == 2:
                            pe.wait_ge(s_XNs, k + 1)
                        for m in range(M):
                            last = T.matmul(PSUM[:, bt, m * P:(m + 1) * P], nx[i][:, m * P:(m + 1) * P], nB[i],
                                            start=True, stop=True)
                        last.then_inc(s_XTN, 1)
                    pe.wait_ge(s_XNs, k + 3)
                    pe.wait_ge(s_XTNs, k + 3)
                pe.wait_ge(s_upd, step + 1)

            with pe.Fori(0, BATCH) as c:
                q = QTall[:, bass.ds(c * SEQ, SEQ)]
                for m in range(M):
                    n = c * M + m
                    if m >= 2:
                        pe.wait_ge(s_fh, n - 1)
                    T.matmul(bank(m % 2), gate[:, m * P:(m + 1) * P], q, start=True, stop=True).then_inc(s_fg, 1)
                    T.matmul(bank(2 + m % 2), val[:, m * P:(m + 1) * P], q, start=True, stop=True).then_inc(s_fu, 1)
                for m in range(M):
                    pe.wait_ge(s_fh, c * M + m + 1)
                    last = T.matmul(bank(4), proj[:, m, :], fh[:, m, :], start=(m == 0), stop=(m == M - 1))
                last.then_inc(s_fo, 1)
                pe.wait_ge(s_fos, c + 1)
                for j in range(QT):
                    last = T.matmul(PSUM[:, 5, j * P:(j + 1) * P], foT[:, j * P:(j + 1) * P], pw, start=True, stop=True)
                last.then_inc(s_fy, 1)
                pe.wait_ge(s_fx, c + 1)

            with pe.Fori(0, BATCH) as b:
                lns = iter(range(1, NLN + 1))
                trs = iter(range(1, NTR + 1))

                def turn_rows(src, norm_done=True, extra=0):
                    for _ in range(extra):
                        next(lns)
                    if norm_done:
                        pe.wait_ge(n_b.done, b * NLN + next(lns))
                    for j in range(QT):
                        last = T.transpose(PSUM[:, 7, j * P:(j + 1) * P], src[:, j, :], ident[:, :])
                    last.then_inc(s_bT, 1)
                    pe.wait_ge(s_bTs, b * NTR + next(trs))

                def project(dst, n, weights, s):
                    for j in range(QT):
                        for k in range(n):
                            last = T.matmul(PSUM[:, dst, j * P:(j + 1) * P], OT[:, k, j * P:(j + 1) * P], weights[:, k, :],
                                            start=(k == 0), stop=(k == n - 1))
                    last.then_inc(s, 1)

                def turn4(k):
                    for c in range(4):
                        last = T.transpose(PSUM[:, 2 + k % 2, c * P:(c + 1) * P], PB[:, k % 2, c * P:(c + 1) * P], ident[:, :])
                    return last

                pe.wait_ge(s_ctx, b + 1)
                T.matmul(bank(4, CTX), W0T[:, 1, :], CT[:, :], start=True, stop=True).then_inc(s_b_k, 1)
                T.matmul(PSUM[0:CTX, 5, 0:P], CT[:, :], W0T[:, 2, :], start=True, stop=True).then_inc(s_b_v, 1)
                turn_rows(YN)
                T.matmul(bank(6), W0T[:, 0, :], YT[:, :], start=True, stop=True).then_inc(s_b_q, 1)
                pe.wait_ge(s_b_qs, b + 1)
                pe.wait_ge(s_b_km, b + 1)
                pe.wait_ge(s_b_vs, b + 1)
                pe.wait_ge(s_zero, 1)

                def score(i):
                    j, t = i // 4, i % 4
                    return T.matmul(bank(i % 2, 4 * CTX), QS[:, t * P:(t + 1) * P], KM0[:, 4 * j:4 * j + 4, :],
                                    start=True, stop=True)

                def turn(k):
                    for g in range(GH):
                        last = T.transpose(PSUM[0:CTX, 2 + k % 2, g * P:(g + 1) * P], PB[:, k % 2, g * CTX:(g + 1) * CTX],
                                           ident[:, :])
                    return last

                def value(v):
                    for g in range(GH):
                        last = T.matmul(PSUM[g * LANE:(g + 1) * LANE, 4 + v % 2, :], VP[0:CTX, 0, 4 * v + g, :],
                                        PT0[0:CTX, v % 2, g, :], start=True, stop=True)
                    return last

                attention_tensor(pe, b, a0, score, turn, value)
                pe.wait_ge(s_outs, a0.summed(b, 4))
                project(6, GROUPS, WoA, s_b_o)

                turn_rows(YN)
                for t in range(QT):
                    T.matmul(bank(t), YT[:, t * P:(t + 1) * P], upT[:, :], start=True, stop=True).then_inc(s_c_u, 1)
                for t in range(QT):
                    pe.wait_ge(s_c_g, b * QT + t + 1)
                    if t >= 2:
                        pe.wait_ge(s_c_Ts, b * QT + t - 1)
                    for m in range(M):
                        last = T.transpose(PSUM[:, 4 + t % 2, m * P:(m + 1) * P], HC[:, t, m * P:(m + 1) * P], ident[:, :])
                    last.then_inc(s_c_T, 1)
                for t in range(QT):
                    pe.wait_ge(s_c_Ts, b * QT + t + 1)
                    for m in range(M):
                        last = T.matmul(PSUM[:, 6, t * P:(t + 1) * P], HTC[:, t, m * P:(m + 1) * P], downT[:, m, :],
                                        start=(m == 0), stop=(m == M - 1))
                last.then_inc(s_c_o, 1)

                turn_rows(YN)
                T.matmul(bank(0), WcT[:, 0:P], YT[:, :], start=True, stop=True).then_inc(s_d_q, 1)
                T.matmul(bank(1), WcT[:, P:2 * P], YT[:, :], start=True, stop=True).then_inc(s_d_q, 1)
                for n in range(8):
                    if n >= 4:
                        pe.wait_ge(s_d_vs, b * 8 + n - 3)
                    T.matmul(bank(2 + n % 4), YT[:, (n // 2) * P:(n // 2 + 1) * P],
                             WcT[:, 256 + 512 * (n % 2):768 + 512 * (n % 2)], start=True, stop=True).then_inc(s_d_v, 1)
                pe.wait_ge(s_d_vs, b * 8 + 8)

                def value(s, c):
                    pe.wait_ge(m_exp, 4 * full.stacks(b, s) + c + 1)
                    if c == 0 and s:
                        pe.wait_ge(m_outs, full.groups(b, s))
                    for e in range(2):
                        h = 2 * s + e
                        last = T.matmul(PSUM[e * VD:(e + 1) * VD, 6, :], V1[:, c, h * VD:(h + 1) * VD],
                                        full.probsT(s, c)[:, e, :], start=(c == 0), stop=(c == QT - 1))
                    if c == QT - 1:
                        last.then_inc(m_values, 1)

                paired_tensor(pe, b, full, value)
                pe.wait_ge(m_norm, (b + 1) * PAIRS)
                project(6, 8, Wo1T, s_d_o)

                turn_rows(Y2, extra=1)
                for p in range(4):
                    T.matmul(bank(p), Wq1[:, p * P:(p + 1) * P], YT[:, :], start=True, stop=True).then_inc(s_e_q, 1)
                for p in range(4):
                    kb = 4 + 2 * (p % 2)
                    if p >= 2:
                        pe.wait_ge(s_e_ks, b * 4 + p - 1)
                    T.matmul(bank(kb), Wkv1[:, p * P:(p + 1) * P], YT[:, :], start=True, stop=True)
                    T.matmul(bank(kb + 1, CTX), Wkv1[:, p * P:(p + 1) * P], CN[:, :], start=True, stop=True)\
                        .then_inc(s_e_k, 1)
                for c in range(5):
                    if c < 4:
                        pe.wait_ge(s_e_qs, b * 4 + c + 1)
                        T.matmul(bank(c), YT[:, c * P:(c + 1) * P], Wkv1[:, 512:1024], start=True, stop=True)\
                            .then_inc(s_e_v, 1)
                    else:
                        pe.wait_ge(s_e_ks, b * 4 + 3)
                        T.matmul(PSUM[0:CTX, 4, :], CN[:, :], Wkv1[:, 512:1024], start=True, stop=True)\
                            .then_inc(s_e_v, 1)
                pe.wait_ge(s_e_ks, b * 4 + 4)
                pe.wait_ge(s_e_vs, b * 5 + 5)

                def score(i):
                    h, t, sb_ = i // 4, i % 4, 2 * (i % 2)
                    T.matmul(bank(sb_), QX[:, h // 2, t * P:(t + 1) * P], KM8[:, h, 0:SEQ], start=True, stop=True)
                    return T.matmul(bank(sb_ + 1, CTX), QX[:, h // 2, t * P:(t + 1) * P], KM8[:, h, SEQ:XK],
                                    start=True, stop=True)

                def turn(k):
                    for c in range(4):
                        T.transpose(PSUM[:, 4 + k % 2, c * P:(c + 1) * P], PB[:, k % 2, c * P:(c + 1) * P], ident[:, :])
                    if k >= 1:
                        pe.wait_ge(s_moved, ax.unit(b, k))
                    return T.transpose(PSUM[0:CTX, 7, 0:P], PB[:, k % 2, SEQ:XK], ident[:, :])

                def value(v):
                    for c in range(5):
                        rows = P if c < 4 else CTX
                        for e in range(2):
                            h = 2 * v + e
                            last = T.matmul(PSUM[e * XD:(e + 1) * XD, 6, :], VX[0:rows, c, h * XD:(h + 1) * XD],
                                            PTe[0:rows, h % 3, c, :], start=(c == 0), stop=(c == 4))
                    return last

                attention_tensor(pe, b, ax, score, turn, value)
                pe.wait_ge(s_outs, ax.summed(b, 4))
                project(7, 4, Wout1, s_e_o)

                turn_rows(YN)
                for i in range(2):
                    T.matmul(bank(i), WF[:, i, :, :].rearrange("p h d -> p (h d)"), YT[:, :], start=True, stop=True)\
                        .then_inc(s_f_q, 1)
                for c in range(QT):
                    last = T.matmul(PSUM[:, 2, c * P:(c + 1) * P], YT[:, c * P:(c + 1) * P],
                                    WF[:, 2, :, :].rearrange("p h d -> p (h d)"), start=True, stop=True)
                last.then_inc(s_f_v, 1)
                pe.wait_ge(s_f_vs, b + 1)

                def value(s, c):
                    if s % 2 == 0:
                        return
                    pe.wait_ge(m_exp, 4 * causal.stacks(b, s) + c + 1)
                    if c == 0 and s >= 3:
                        pe.wait_ge(m_outs, causal.groups(b, s // 2))
                    for lane in range(4):
                        st_, h = s - 1 + lane // 2, 2 * (s - 1) + lane
                        last = T.matmul(PSUM[lane * LANE:(lane + 1) * LANE, 6, c * P:SEQ], VP[:, c, h, :],
                                        causal.probsT(st_, c)[:, lane % 2, :], start=(c == 0), stop=(c == QT - 1))
                    if c == QT - 1:
                        last.then_inc(m_values, 1)

                paired_tensor(pe, b, causal, value)
                pe.wait_ge(m_outs, causal.groups(b, 4))
                for j in range(QT):
                    for k in range(GROUPS):
                        T.matmul(PSUM[:, 7, j * HEADS:(j + 1) * HEADS], OT[:, k, j * P:(j + 1) * P], SELsum[:, k, :],
                                 start=(k == 0), stop=(k == GROUPS - 1))
                project(6, GROUPS, SEL, s_f_o)
                pe.wait_ge(s_f_y, b + 1)
                turn_rows(YF, norm_done=False)
                for t in range(QT):
                    last = T.matmul(PSUM[:, 6, t * E:(t + 1) * E], YT[:, t * P:(t + 1) * P], gateW[:, :],
                                    start=True, stop=True)
                last.then_inc(s_f_g, 1)

                def up(e):
                    for m in range(M):
                        if e >= 1:
                            pe.wait_ge(s_f_hs, (b * E + e - 1) * M + m + 1)
                        T.matmul(bank(m), W1[:, e, m * P:(m + 1) * P], YT[:, :], start=True, stop=True).then_inc(s_f_h, 1)

                def down(e):
                    pe.wait_ge(s_f_hs, (b * E + e + 1) * M)
                    if e >= 2:
                        pe.wait_ge(s_f_acc, b * E + e - 1)
                    for t in range(QT):
                        for m in range(M):
                            last = T.matmul(PSUM[:, 4 + e % 2, t * P:(t + 1) * P], HE[:, e % 2, m, t * P:(t + 1) * P],
                                            W2[:, e, m, :], start=(m == 0), stop=(m == M - 1))
                    last.then_inc(s_f_dn, 1)

                up(0)
                up(1)
                pe.wait_ge(s_f_c, b + 1)
                for t in range(QT):
                    last = T.transpose(PSUM[0:E, 7, t * P:(t + 1) * P], comb[:, t, :], ident[:, :])
                last.then_inc(s_f_cT, 1)
                down(0)
                pe.wait_ge(s_f_cTs, b + 1)
                for t in range(QT):
                    last = T.matmul(PSUM[:, 6, t * P:(t + 1) * P], combT[:, t * P:(t + 1) * P], b2r[:, :],
                                    start=True, stop=True)
                last.then_inc(s_f_b2, 1)
                for e in range(1, E):
                    if e + 1 < E:
                        up(e + 1)
                    down(e)
                pe.wait_ge(s_rowdone, b + 1)



        @block.scalar
        def _(act):
            A = nc.scalar
            for i, (srcs, dst, rows, after) in enumerate(prep):
                n = len(srcs) * rows
                act.wait_ge(s_tr, i + 1)
                if after == "ctx":
                    A.activation(dst, PSUM[:, i % 7, 0:n].rearrange("p (b s) -> p b s", b=BATCH), ACT.Identity,
                                 bias=V[:, BM:BM + 1], scale=V[:, GM:GM + 1]).then_inc(s_ev, 1)
                else:
                    A.activation(dst, PSUM[:, i % 7, 0:n].rearrange("p (b s) -> p b s", s=rows) if len(dst.shape) == 3
                                 else PSUM[:, i % 7, 0:n], ACT.Copy).then_inc(s_ev, 1)
                if i == 0:
                    act.wait_ge(s_ev, 1)
            A.activation(vs[:, 0:1], V[:, BQ0:BQ0 + 1], ACT.Copy, scale=HD ** -0.5)
            A.activation(vs[:, 1:2], V[:, BCQ:BCQ + 1], ACT.Copy, scale=HD ** -0.5)
            A.activation(aI, ident[:, :], ACT.Copy, scale=NS_A)
            with act.Fori(0, BATCH) as c:
                act.wait_ge(s_yT, c + 1)
                A.activation(YT[:, :], bank(0), ACT.Copy).then_inc(s_yTs, 1)
                act.wait_ge(s_qkvb, c + 1)
                A.activation(sq4, VA[:, 0:1024], ACT.Square).then_inc(s_sqr, 1)
                act.wait_ge(s_ss, c + 1)
                A.activation(normw[:, 128:256], normw[:, 0:128], ACT.Sqrt).then_inc(s_nrm, 1)
                act.wait_ge(s_qkT, 2 * c + 1)
                A.activation(QTall[:, bass.ds(c * SEQ, SEQ)], bank(5), ACT.Identity, scale=V[:, QSC:QSC + 1],
                             bias=V[:, QBI:QBI + 1]).then_inc(s_qkTs, 1)
                act.wait_ge(s_qkT, 2 * c + 2)
                A.activation(KTall[:, bass.ds(c * SEQ, SEQ)], bank(6), ACT.Identity, scale=V[:, KSC:KSC + 1],
                             bias=V[:, KBI:KBI + 1]).then_inc(s_qkTs, 1)
            with act.Fori(0, STEPS) as step:
                def gate_val(t):
                    n, par = step * TILES + t, t % 2
                    act.wait_ge(s_gu, n + 1)
                    if t >= 2:
                        act.wait_ge(s_w, n - 1)
                    A.activation(sg[par], bank(0), ACT.Sigmoid).then_inc(s_sig, 1)
                    A.activation(us[par], bank(1), ACT.Copy).then_inc(s_uc, 1)

                gate_val(0)
                for t in range(TILES):
                    n = step * TILES + t
                    act.wait_ge(s_hT, n + 1)
                    A.activation(hTs, bank(2), ACT.Copy).then_inc(s_hTs, 1)
                    if t + 1 < TILES:
                        gate_val(t + 1)
                    act.wait_ge(s_dpT, n + 1)
                    A.activation(dpT, PSUM[:, 3, 128:256], ACT.Copy).then_inc(s_dpTs, 1)
                act.wait_ge(s_gs, step * 3 + 3)
                for i in range(3):
                    last = A.activation(nxT[i], nx[i], ACT.Square, accum_out=sm[:, i:i + 1])
                last.then_inc(s_sq, 1)
                for i in range(3):
                    act.wait_ge(s_xt0, step * 3 + i + 1)
                    A.activation(nxT[i], bank(1 + i), ACT.Copy).then_inc(s_xt0s, 1)
                with act.Fori(0, NS_ITERS) as it:
                    k = (step * NS_ITERS + it) * 3
                    for i in range(3):
                        act.wait_ge(s_A, k + i + 1)
                        A.activation(nA[i], PSUM[:, i, 0:P], ACT.Copy).then_inc(s_As, 1)
                    for i, bx in enumerate((3, 5, 7)):
                        act.wait_ge(s_XN, k + i + 1)
                        act.wait_ge(s_XTN, k + i + 1)
                        A.activation(nx[i], bank(bx), ACT.Copy).then_inc(s_XNs, 1)
            with act.Fori(0, BATCH) as c:
                for m in range(M):
                    n = c * M + m
                    act.wait_ge(s_fg, n + 1)
                    A.activation(fsg[:, m % 2, :], bank(m % 2), ACT.Sigmoid).then_inc(s_fs, 1)
                act.wait_ge(s_fo, c + 1)
                A.activation(foT, bank(4), ACT.Copy).then_inc(s_fos, 1)

            with act.Fori(0, BATCH) as b:
                trs = iter(range(1, NTR + 1))

                def rows_T(scale=None, bias=None):
                    act.wait_ge(s_bT, b * NTR + next(trs))
                    if scale is None:
                        A.activation(YT[:, :], bank(7), ACT.Copy).then_inc(s_bTs, 1)
                    else:
                        A.activation(YT[:, :], bank(7), ACT.Identity, scale=scale, bias=bias).then_inc(s_bTs, 1)

                act.wait_ge(s_b_k, b + 1)
                A.activation(KT0[:, 0:CTX], bank(4, CTX), ACT.Identity, bias=V[:, BK0:BK0 + 1]).then_inc(s_b_ks, 1)
                rows_T()
                act.wait_ge(s_b_q, b + 1)
                A.activation(QS, bank(6), ACT.Identity, scale=HD ** -0.5, bias=vs[:, 0:1]).then_inc(s_b_qs, 1)

                def exp(i):
                    for g in range(GH):
                        last = A.activation(PB[:, i % 2, g * CTX:(g + 1) * CTX], PSUM[:, i % 2, g * CTX:(g + 1) * CTX], ACT.Exp,
                                            bias=nmax[:, i % 2, g:g + 1], accum_out=rsum[:, i % 2, g:g + 1])
                    return last

                def move(k):
                    j, t = k // 4, k % 4
                    return A.activation(PT0[0:CTX, j % 2, :, t * P:(t + 1) * P],
                                        PSUM[0:CTX, 2 + k % 2, :].rearrange("p (g q) -> p g q", g=4), ACT.Copy)

                attention_scalar(act, b, a0, exp, move)

                rows_T()
                act.wait_ge(s_c_r1, b + 1)
                for t in range(QT):
                    act.wait_ge(s_c_u, b * QT + t + 1)
                    A.activation(HC[:, t, :], bank(t), ACT.Gelu, scale=root[:, 0, t:t + 1]).then_inc(s_c_g, 1)
                for t in range(QT):
                    act.wait_ge(s_c_T, b * QT + t + 1)
                    A.activation(HTC[:, t, :], bank(4 + t % 2), ACT.Copy).then_inc(s_c_Ts, 1)

                def exp_at(base, width):
                    def exp(i):
                        w = width(i)
                        return A.activation(PB[:, i % 2, 0:w], PSF[:, base(i):base(i) + w], ACT.Exp, bias=nmax[:, i % 2, 0:1],
                                            accum_out=rsum[:, i % 2, 0:1])
                    return exp

                rows_T()
                act.wait_ge(s_d_q, 2 * b + 1)
                A.activation(Qraw, bank(0), ACT.Identity, scale=HD ** -0.5, bias=vs[:, 1:2]).then_inc(s_d_qb, 1)
                act.wait_ge(s_d_q, 2 * b + 2)
                A.activation(Kraw, bank(1), ACT.Identity, bias=V[:, BCK:BCK + 1]).then_inc(s_d_qb, 1)

                paired_scalar(act, b, full)

                rows_T(V[:, GL:GL + 1], V[:, BL:BL + 1])
                for p in range(4):
                    act.wait_ge(s_e_q, b * 4 + p + 1)
                    A.activation(QX[:, p, :], bank(p), ACT.Copy, scale=XD ** 0.5).then_inc(s_e_qs, 1)
                for c in range(5):
                    rows = P if c < 4 else CTX
                    act.wait_ge(s_e_v, b * 5 + c + 1)
                    A.activation(VX[0:rows, c, :], PSUM[0:rows, c, :], ACT.Copy).then_inc(s_e_vs, 1)

                def move(k):
                    h, t = k // 4, k % 4
                    A.activation(PTe[0:CTX, h % 3, 4, t * P:(t + 1) * P], PSUM[0:CTX, 7, 0:P], ACT.Copy)
                    return A.activation(PTe[:, h % 3, 0:4, t * P:(t + 1) * P],
                                        bank(4 + k % 2).rearrange("p (c q) -> p c q", c=4), ACT.Copy)

                attention_scalar(act, b, ax, exp_at(lambda i: 1024 * (i % 2), lambda i: XK), move)

                rows_T()
                act.wait_ge(s_f_q, 2 * b + 1)
                A.activation(Qraw, bank(0), ACT.Copy, scale=D ** -0.5).then_inc(s_f_qs, 1)
                act.wait_ge(s_f_q, 2 * b + 2)
                A.activation(Kraw, bank(1), ACT.Copy).then_inc(s_f_qs, 1)

                paired_scalar(act, b, causal)
                rows_T()

                def relu(e):
                    if e >= 2:
                        act.wait_ge(s_f_dn, b * E + e - 1)
                    for m in range(M):
                        act.wait_ge(s_f_h, (b * E + e) * M + m + 1)
                        A.activation(HE[:, e % 2, m, :], bank(m), ACT.Relu, bias=V[:, B1C + e * M + m:B1C + e * M + m + 1])\
                            .then_inc(s_f_hs, 1)

                relu(0)
                act.wait_ge(s_f_d, b + 1)
                A.activation(tw[:, 1, :], tw[:, 0, :], ACT.Exp).then_inc(s_f_e, 1)
                relu(1)
                act.wait_ge(s_f_cT, b + 1)
                A.activation(combT, PSUM[0:E, 7, :], ACT.Copy).then_inc(s_f_cTs, 1)
                for e in range(2, E):
                    relu(e)
                act.wait_ge(s_rowdone, b + 1)

        @block.vector
        def _(dve):
            Vv = nc.vector

            def head_groups(ap):
                return ap.rearrange("p t w (h d) -> p (t w h) d", d=HD)

            dve.wait_ge(s_w0, N_W0)
            Vv.tensor_reduce(sm[:, 0:1], upraw, AX.X, ALU.add, apply_absolute_value=True)
            Vv.tensor_reduce(sm[:, 1:2], downraw, AX.X, ALU.add, apply_absolute_value=True).then_inc(s_absum, 1)
            dve.wait_ge(s_thr, 1)
            Vv.tensor_scalar(sm[:, 2:4], bank(7, 2), 0.5 / (HID * D), None, ALU.mult)
            dve.drain()
            Vv.tensor_scalar(sm[:, 4:6], sm[:, 2:4], -1.0, None, ALU.mult)
            dve.drain()
            for i, w in enumerate((upraw, downraw)):
                Vv.tensor_scalar(tern[:, i, :], w, sm[:, 2 + i:3 + i], None, ALU.is_gt)
                dve.drain()
                Vv.scalar_tensor_tensor(tern[:, i, :], w, sm[:, 4 + i:5 + i], tern[:, i, :], ALU.is_lt, ALU.subtract)
                dve.drain()
                Vv.scalar_tensor_tensor(tern[:, i, :], tern[:, i, :], -1.0, w, ALU.mult, ALU.subtract)
                dve.drain()
                last = Vv.tensor_tensor(ternq[:, i, :], tern[:, i, :], w, ALU.add)
            last.then_inc(s_tern, 1)
            ln_vector(dve, n_ctx, 1, [ctxraw[0:CTX, b, :] for b in range(BATCH)],
                      [ctxn[0:CTX, b, :] for b in range(BATCH)], CTX)
            dve.wait_ge(s_wt, N_WT)
            dve.wait_ge(s_x, 16)
            dve.wait_ge(s_ev, NPREP)
            for dst, src in ((kscale, kscale8), (kbias, kbias8)):
                Vv.tensor_copy(dst.rearrange("p (h d) -> p h d", d=HD), src.unsqueeze(1).to_broadcast([P, HEADS, HD]))
            with dve.Fori(0, BATCH) as c:
                ln_vector(dve, n_in, c + 1, [X[:, bass.ds(c * QT + j, 1), :].rearrange("p o d -> p (o d)") for j in range(QT)],
                          [YN[:, j, :] for j in range(QT)])
                for j in range(QT):
                    dve.wait_ge(s_qkv, c * QT + j + 1)
                    Vv.tensor_tensor(qkvs[:, j, :, :].rearrange("p w d -> p (w d)"), PSUM[:, 1 + j, 0:256], bqkv[:, 0:256], ALU.add)
                    last = Vv.tensor_tensor(Vn[:, bass.ds(c * QT + j, 1), :].rearrange("p o d -> p (o d)"), PSUM[:, 1 + j, 256:384],
                                     bqkv[:, 256:384], ALU.add)
                last.then_inc(s_qkvb, 1)
                dve.wait_ge(s_sqr, c + 1)
                Vv.tensor_reduce(normw[:, 0:128], sq4.rearrange("p (g d) -> p g d", d=HD), AX.X, ALU.add).then_inc(s_ss, 1)
                dve.wait_ge(s_nrm, c + 1)
                Vv.tensor_scalar(normw[:, 128:256], normw[:, 128:256], 1e-6, None, ALU.add)
                dve.drain()
                Vv.reciprocal(normw[:, 0:128], normw[:, 128:256])
                dve.drain()
                g3 = VA[:, 0:1024].rearrange("p (g d) -> p g d", d=HD)
                Vv.tensor_tensor(g3, g3, normw[:, 0:128].unsqueeze(2).to_broadcast([P, P, HD]), ALU.mult).then_inc(s_qk, 1)
                dve.drain()
                Vv.tensor_tensor(kraw, qkvs[:, :, 1, :], kscale.unsqueeze(1).to_broadcast([P, QT, D]), ALU.mult)
                dve.drain()
                Vv.tensor_tensor(Kn[:, bass.ds(c * QT, QT), :], kraw, kbias.unsqueeze(1).to_broadcast([P, QT, D]), ALU.add)\
                    .then_inc(s_kn, 1)
                dve.wait_ge(s_qkTs, 2 * c + 2)

            with dve.Fori(0, STEPS) as step:
                def silu(t):
                    n, par = step * TILES + t, t % 2
                    if t >= 2:
                        dve.wait_ge(s_w, n - 1)
                        dve.wait_ge(s_dgu, n - 1)
                    dve.wait_ge(s_sig, n + 1)
                    Vv.tensor_tensor(t1[par], bank(0), sg[par], ALU.mult).then_inc(s_t, 1)
                    dve.wait_ge(s_t, n + 1)
                    dve.wait_ge(s_uc, n + 1)
                    Vv.tensor_tensor(hh[par], us[par], t1[par], ALU.mult).then_inc(s_h, 1)

                silu(0)
                for t in range(TILES):
                    n, par = step * TILES + t, t % 2
                    if t + 1 < TILES:
                        silu(t + 1)
                    dve.wait_ge(s_pred, n + 1)
                    Vv.tensor_tensor(dp, bank(3, P), Vn[:, t, :], ALU.subtract)
                    dve.drain()
                    Vv.tensor_scalar(dp, dp, 2.0 / (TILES * P * D), None, ALU.mult).then_inc(s_dp, 1)
                    dve.wait_ge(s_dh, n + 1)
                    Vv.tensor_tensor(du, bank(4), t1[par], ALU.mult)
                    dve.wait_ge(s_w, n + 1)
                    Vv.tensor_tensor(dg, bank(4), ww[par], ALU.mult).then_inc(s_dgu, 1)
                dve.wait_ge(s_grad, step + 1)
                for i in range(3):
                    Vv.tensor_copy(nx[i], bank(5 + i)).then_inc(s_gs, 1)
                dve.wait_ge(s_tot, step + 1)
                Vv.tensor_copy(sm[:, 4:7], bank(0, 3)).then_inc(s_tots, 1)
                dve.wait_ge(s_nrt, step + 1)
                Vv.tensor_scalar(sm[:, 8:11], sm[:, 8:11], 1e-7, None, ALU.add)
                dve.drain()
                Vv.reciprocal(sm[:, 12:15], sm[:, 8:11])
                dve.drain()
                for i in range(3):
                    Vv.tensor_scalar(nx[i], nx[i], sm[:, 12 + i:13 + i], None, ALU.mult).then_inc(s_x0, 1)
                with dve.Fori(0, NS_ITERS) as it:
                    k = (step * NS_ITERS + it) * 3
                    for i in range(3):
                        dve.wait_ge(s_As, k + i + 1)
                        Vv.scalar_tensor_tensor(nC[i], nA[i], NS_B, aI, ALU.mult, ALU.add)
                    dve.drain()
                    for i in range(3):
                        dve.wait_ge(s_A2, k + i + 1)
                        Vv.scalar_tensor_tensor(nB[i], PSUM[:, i, P:2 * P], NS_C, nC[i], ALU.mult, ALU.add).then_inc(s_B, 1)
                    for i, bt in enumerate((4, 6, 3)):
                        dve.wait_ge(s_XTN, k + i + 1)
                        Vv.tensor_copy(nxT[i], bank(bt)).then_inc(s_XTNs, 1)
                dve.wait_ge(s_XNs, (step + 1) * NS_ITERS * 3)
                dve.wait_ge(s_XTNs, (step + 1) * NS_ITERS * 3)
                Vv.scalar_tensor_tensor(gate, nx[0], -LR, gate, ALU.mult, ALU.add)
                Vv.scalar_tensor_tensor(val, nx[1], -LR, val, ALU.mult, ALU.add)
                Vv.scalar_tensor_tensor(projT, nx[2], -LR, projT, ALU.mult, ALU.add)
                Vv.scalar_tensor_tensor(proj.rearrange("p m d -> p (m d)"), nxT[2], -LR,
                                        proj.rearrange("p m d -> p (m d)"), ALU.mult, ALU.add).then_inc(s_upd, 1)
            with dve.Fori(0, BATCH) as c:
                for m in range(M):
                    n = c * M + m
                    dve.wait_ge(s_fs, n + 1)
                    Vv.tensor_tensor(ft[:, m % 2, :], bank(m % 2), fsg[:, m % 2, :], ALU.mult)
                    dve.drain()
                    dve.wait_ge(s_fu, n + 1)
                    Vv.tensor_tensor(fh[:, m, :], bank(2 + m % 2), ft[:, m % 2, :], ALU.mult).then_inc(s_fh, 1)
                dve.wait_ge(s_fy, c + 1)
                xs = X[:, bass.ds(c * QT, QT), :]
                Vv.tensor_tensor(Y2[:, :, :], PSUM[:, 5, :].rearrange("p (t d) -> p t d", d=D),
                                 bproj.unsqueeze(1).to_broadcast([P, QT, D]), ALU.add)
                dve.drain()
                Vv.tensor_tensor(xs, xs, Y2[:, :, :], ALU.add).then_inc(s_fx, 1)

            Vv.memset(VPA[:, :], 0.0)
            dve.drain()
            Vv.memset(VP[:, :, :, HD:HD + 1], 1.0).then_inc(s_zero, 1)
            dve.wait_ge(s_wr, N_WR)
            dve.drain()
            with dve.Fori(0, BATCH) as b:
                lns = iter(range(1, NLN + 1))
                xs = X[:, bass.ds(b * QT, QT), :]

                def xt(j):
                    return X[:, bass.ds(b * QT + j, 1), :].rearrange("p o d -> p (o d)")

                def tiles(y):
                    return [y[:, j, :] for j in range(QT)]

                def norm(src, dst):
                    dve.drain()
                    ln_vector(dve, n_b, b * NLN + next(lns), src, dst)

                def rows(i):
                    return bc[:, i, :].unsqueeze(1).to_broadcast([P, QT, D])

                def tok(n):
                    return bank(n).rearrange("p (t d) -> p t d", d=D)

                def split(i, raw):
                    Vv.tensor_copy(PARTS[:, 2 * i, :], raw).then_inc(m_parts, 1)
                    dve.drain()
                    Vv.tensor_tensor(PARTS[:, 2 * i + 1, :], raw, PARTS[:, 2 * i, :].bitcast(F32), ALU.subtract)\
                        .then_inc(m_parts, 1)

                def normaliser(width):
                    def normalise(k):
                        Vv.reciprocal(rinv[:, k % 2, 0:1], rsum[:, k % 2, 0:1])
                        dve.drain()
                        w = width(k)
                        return Vv.tensor_scalar(PB[:, k % 2, 0:w], PB[:, k % 2, 0:w], rinv[:, k % 2, 0:1], None, ALU.mult)
                    return normalise

                def maximum_of(base, width):
                    def maximum(i):
                        return Vv.tensor_reduce(nmax[:, i % 2, 0:1], PSF[:, base(i):base(i) + width(i)], AX.X, ALU.max, negate=True)
                    return maximum

                dve.wait_ge(s_b_v, b + 1)
                Vv.tensor_tensor(VP[0:CTX, 0, :, 0:HD], PSUM[0:CTX, 5, 0:P].rearrange("p (h d) -> p h d", d=HD),
                                 bc[0:CTX, BV0, :].rearrange("p (h d) -> p h d", d=HD), ALU.add).then_inc(s_b_vs, 1)
                norm([xt(j) for j in range(QT)], tiles(YN))
                dve.wait_ge(s_b_ks, b + 1)
                Vv.tensor_tensor(KM0, KT0[:, 0:CTX].unsqueeze(1).to_broadcast([P, HEADS, CTX]),
                                 head_mask[:, :].unsqueeze(2).to_broadcast([P, HEADS, CTX]), ALU.mult).then_inc(s_b_km, 1)

                def maximum(i):
                    return Vv.tensor_reduce(nmax[:, i % 2, :], bank(i % 2, 4 * CTX).rearrange("p (g k) -> p g k", g=4),
                                            AX.X, ALU.max, negate=True)

                def normalise(k):
                    Vv.reciprocal(rinv[:, k % 2, :], rsum[:, k % 2, :])
                    dve.drain()
                    p3 = PB[:, k % 2, 0:4 * CTX].rearrange("p (g k) -> p g k", g=4)
                    return Vv.tensor_tensor(p3, p3, rinv[:, k % 2, :].unsqueeze(2).to_broadcast([P, 4, CTX]), ALU.mult)

                attention_vector(dve, b, a0, maximum, normalise, lambda v: Vv.tensor_copy(OT[:, v, :], bank(4 + v % 2)))
                dve.wait_ge(s_b_o, b + 1)
                Vv.tensor_tensor(Y2[:, :, :], tok(6), rows(BO0), ALU.add)
                dve.drain()
                Vv.tensor_tensor(xs, xs, Y2[:, :, :], ALU.add)

                norm([xt(j) for j in range(QT)], tiles(YN))
                dve.drain()
                for j in range(QT):
                    last = Vv.tensor_tensor_reduce(out=KMA[:, j * P:(j + 1) * P], in0=YN[:, j, :], in1=YN[:, j, :], scale=1.0,
                                                   scalar=0.0, op0=ALU.mult, op1=ALU.add, accum_out=ssq[:, 0, j:j + 1])
                last.then_inc(s_pow, 1)
                dve.wait_ge(s_powd, 2 * b + 1)
                Vv.tensor_scalar(root[:, 0, :], root[:, 0, :], float(D) ** -0.5, 1e-8, ALU.mult, ALU.add)
                dve.drain()
                Vv.reciprocal(root[:, 0, :], root[:, 0, :]).then_inc(s_c_r1, 1)
                for j in range(QT):
                    dve.wait_ge(s_c_g, b * QT + j + 1)
                    last = Vv.tensor_tensor_reduce(out=KMA[:, 512 * (j + 1):512 * (j + 2)], in0=HC[:, j, :], in1=HC[:, j, :],
                                                   scale=1.0, scalar=0.0, op0=ALU.mult, op1=ALU.add, accum_out=ssq[:, 1, j:j + 1])
                last.then_inc(s_pow, 1)
                dve.wait_ge(s_powd, 2 * b + 2)
                Vv.tensor_scalar(root[:, 1, :], root[:, 1, :], float(HID) ** -0.5, 1e-8, ALU.mult, ALU.add)
                dve.drain()
                Vv.reciprocal(root[:, 1, :], root[:, 1, :])
                dve.drain()
                dve.wait_ge(s_c_o, b + 1)
                for j in range(QT):
                    Vv.scalar_tensor_tensor(xt(j), PSUM[:, 6, j * P:(j + 1) * P], root[:, 1, j:j + 1], xt(j), ALU.mult, ALU.add)

                norm([xt(j) for j in range(QT)], tiles(YN))
                for i, raw in enumerate((Qraw, Kraw)):
                    dve.wait_ge(s_d_qb, 2 * b + i + 1)
                    Vv.scalar_tensor_tensor(raw, raw, SLOPE, raw, ALU.mult, ALU.max)
                    dve.drain()
                    split(i, raw)
                for n in range(8):
                    half = slice(512 * (n % 2), 512 * (n % 2 + 1))
                    dve.wait_ge(s_d_v, b * 8 + n + 1)
                    Vv.tensor_tensor(V1[:, n // 2, half], bank(2 + n % 4), bcv[:, half], ALU.add)
                    dve.drain()
                    Vv.scalar_tensor_tensor(V1[:, n // 2, half], V1[:, n // 2, half], SLOPE, V1[:, n // 2, half],
                                            ALU.mult, ALU.max).then_inc(s_d_vs, 1)
                paired_vector(dve, b, full)
                Vv.tensor_tensor(xs, xs, YN[:, :, :], ALU.add)
                dve.wait_ge(s_d_o, b + 1)
                Vv.tensor_tensor(Y2[:, :, :], tok(6), rows(BO1), ALU.add)
                dve.drain()
                Vv.scalar_tensor_tensor(Y2[:, :, :], Y2[:, :, :], SLOPE, Y2[:, :, :], ALU.mult, ALU.max)
                dve.drain()
                Vv.tensor_tensor(xs, xs, Y2[:, :, :], ALU.add)

                norm([xt(j) for j in range(QT)], tiles(YN))
                norm(tiles(YN), tiles(Y2))
                for p in range(4):
                    dve.wait_ge(s_e_k, b * 4 + p + 1)
                    kb = 512 * (4 + 2 * (p % 2))
                    for e in range(2):
                        last = Vv.tensor_scalar(KM8[:, 2 * p + e, 0:XK], PSF[:, kb:kb + XK], half_mask[:, e:e + 1], None, ALU.mult)
                    last.then_inc(s_e_ks, 1)
                attention_vector(dve, b, ax, maximum_of(lambda i: 1024 * (i % 2), lambda i: XK), normaliser(lambda i: XK),
                                 lambda v: Vv.tensor_copy(OT[:, v, :], bank(6)))
                dve.wait_ge(s_e_o, b + 1)
                Vv.tensor_tensor(xs, tok(7), xs, ALU.add)

                norm([xt(j) for j in range(QT)], tiles(YN))
                for i, raw in enumerate((Qraw, Kraw)):
                    dve.wait_ge(s_f_qs, 2 * b + i + 1)
                    split(i, raw)
                dve.wait_ge(s_f_v, b + 1)
                Vv.tensor_copy(VP[:, :, :, 0:HD].rearrange("p t h d -> p (t h) d"),
                               bank(2).rearrange("p (g d) -> p g d", d=HD)).then_inc(s_f_vs, 1)
                paired_vector(dve, b, causal)
                dve.wait_ge(s_f_o, b + 1)
                Vv.reciprocal(rsums[:, :, :].rearrange("p t h -> p (t h)"), bank(7, QT * HEADS))
                dve.drain()
                Vv.tensor_tensor(Y2[:, :, :].rearrange("p t (h d) -> p (t h) d", d=HD), bank(6).rearrange("p (g d) -> p g d", d=HD),
                                 rsums[:, :, :].rearrange("p t h -> p (t h)").unsqueeze(2).to_broadcast([P, QT * HEADS, HD]),
                                 ALU.mult)
                norm(tiles(Y2), tiles(Y2))
                dve.drain()
                Vv.tensor_tensor(Y2[:, :, :], Y2[:, :, :], rows(G1), ALU.mult)
                dve.drain()
                Vv.tensor_tensor(Y2[:, :, :], Y2[:, :, :], rows(C1), ALU.add)
                dve.drain()
                Vv.tensor_tensor(YF[:, :, :], Y2[:, :, :], YN[:, :, :], ALU.add).then_inc(s_f_y, 1)
                dve.wait_ge(s_f_g, b + 1)
                Vv.tensor_copy(logit[:, :, :], bank(6, QT * E).rearrange("p (t e) -> p t e", e=E))
                dve.drain()
                for j in range(QT):
                    Vv.max(top[:, j, :], logit[:, j, :])
                dve.drain()
                for j in range(QT):
                    Vv.max_index(topi[:, j, :], top[:, j, :], logit[:, j, :])
                Vv.tensor_tensor(tw[:, 0, :], top[:, :, 1], top[:, :, 0], ALU.subtract).then_inc(s_f_d, 1)
                dve.drain()
                Vv.tensor_copy(topf[:, :, :], topi[:, :, :])
                dve.wait_ge(s_f_e, b + 1)
                Vv.tensor_scalar(tw[:, 2, :], tw[:, 1, :], 1.0, None, ALU.add)
                dve.drain()
                Vv.reciprocal(tw[:, 2, :], tw[:, 2, :])
                dve.drain()
                Vv.tensor_tensor(tw[:, 3, :], tw[:, 1, :], tw[:, 2, :], ALU.mult)
                dve.drain()
                for j in range(QT):
                    Vv.tensor_scalar(comb[:, j, :], iota8[:, :], topf[:, j, 0:1], tw[:, 2, j:j + 1], ALU.is_equal, ALU.mult)
                    Vv.tensor_scalar(comb2[:, j, :], iota8[:, :], topf[:, j, 1:2], tw[:, 3, j:j + 1], ALU.is_equal, ALU.mult)
                dve.drain()
                Vv.tensor_tensor(comb[:, :, :], comb[:, :, :], comb2[:, :, :], ALU.add).then_inc(s_f_c, 1)
                dve.wait_ge(s_f_b2, b + 1)
                Vv.tensor_copy(Y2[:, :, :], tok(6))
                for e in range(E):
                    dve.drain()
                    dve.wait_ge(s_f_dn, b * E + e + 1)
                    for j in range(QT):
                        last = Vv.scalar_tensor_tensor(Y2[:, j, :], PSUM[:, 4 + e % 2, j * P:(j + 1) * P], comb[:, j, e:e + 1],
                                                       Y2[:, j, :], ALU.mult, ALU.add)
                    last.then_inc(s_f_acc, 1)
                norm(tiles(Y2), tiles(Y2))
                dve.drain()
                Vv.tensor_tensor(Y2[:, :, :], Y2[:, :, :], rows(G2), ALU.mult)
                dve.drain()
                Vv.tensor_tensor(Y2[:, :, :], Y2[:, :, :], rows(C2), ALU.add)
                dve.drain()
                Vv.tensor_tensor(YF[:, :, :], YF[:, :, :], Y2[:, :, :], ALU.add)
                dve.drain()
                Vv.tensor_tensor(xs, xs, YF[:, :, :], ALU.add).then_inc(s_rowdone, 1)


_INS = ["x", "ctx_1024", "L0_attn_qkv_w", "L0_attn_qkv_b", "L0_attn_qn_scale", "L0_attn_qn_bias", "L0_attn_kn_scale",
        "L0_attn_kn_bias", "L0_attn_ttt_gate", "L0_attn_ttt_val", "L0_attn_ttt_proj", "L0_attn_proj_w",
        "L0_attn_proj_b", "L0_xattn_Wq", "L0_xattn_bq", "L0_xattn_Wk", "L0_xattn_bk", "L0_xattn_Wv", "L0_xattn_bv",
        "L0_xattn_Wo", "L0_xattn_bo", "L0_ffn_w_up", "L0_ffn_w_down", "L1_attn_Wc", "L1_attn_bc", "L1_attn_Wo",
        "L1_attn_bo", "L1_xattn_Wq", "L1_xattn_Wkv", "L1_xattn_Wout", "L1_xattn_gm", "L1_xattn_bm", "L1_xattn_gl",
        "L1_xattn_bl", "L1_ffn_Wq", "L1_ffn_Wk", "L1_ffn_Wv", "L1_ffn_gate_W", "L1_ffn_W1", "L1_ffn_b1",
        "L1_ffn_W2", "L1_ffn_b2", "L1_ffn_ln1_g", "L1_ffn_ln1_b", "L1_ffn_ln2_g", "L1_ffn_ln2_b"]


def kernel(**inputs):
    import numpy as _np
    import concourse.bacc as _bacc
    from concourse import mybir as _mybir
    from concourse.bass_utils import run_bass_kernel_spmd as _run

    nc = _bacc.Bacc("TRN2", target_bir_lowering=False, num_devices=1)
    arrays, args = {}, []
    for name in _INS:
        a = _np.ascontiguousarray(inputs[name])
        arrays[f"in_{name}_dram"] = a
        args.append(nc.dram_tensor(f"in_{name}_dram", a.shape, _mybir.dt.from_np(a.dtype), kind="ExternalInput").ap())
    out = nc.dram_tensor("out_dram", (BATCH, SEQ, D), F32, kind="ExternalOutput").ap()
    decoder_kernel(nc, *args, out)
    r = _run(nc, [arrays], core_ids=[0])
    return r.results[0]["out_dram"]
```

```python
import numpy as np
import concourse.bass as bass
from concourse import mybir
from contextlib import ExitStack

F32 = mybir.dt.float32
BF16 = mybir.dt.bfloat16
F32R = mybir.dt.float32r
U32 = mybir.dt.uint32
ALU = mybir.AluOpType
ACT = mybir.ActivationFunctionType
AX = mybir.AxisListType

BATCH, SEQ, D = 4, 512, 128
P = 128
QT = SEQ // P
TILES = BATCH * QT
CTX = 77
HEADS, HD = 16, 8
PAIRS = 8
GROUPS, LANE = 4, 32
HID = 512
M = HID // P
STEPS, NS_ITERS, LR = 2, 5, 0.1
NS_A, NS_B, NS_C = 3.4445, -4.775, 2.0315
VD = 64
XH, XD = 8, 64
XK = SEQ + CTX
E = 8
LN_EPS = 1e-5
SLOPE = 0.01
MASKED = -3.0e38


def decoder_kernel(nc, x, ctx_1024, qkv_w, qkv_b, qn_scale, qn_bias, kn_scale, kn_bias, ttt_gate, ttt_val,
                   ttt_proj, proj_w, proj_b, x0_Wq, x0_bq, x0_Wk, x0_bk, x0_Wv, x0_bv, x0_Wo, x0_bo, w_up, w_down,
                   a1_Wc, a1_bc, a1_Wo, a1_bo, x1_Wq, x1_Wkv, x1_Wout, x1_gm, x1_bm, x1_gl, x1_bl,
                   f1_Wq, f1_Wk, f1_Wv, f1_gate, f1_W1, f1_b1, f1_W2, f1_b2, f1_g1, f1_c1, f1_g2, f1_c2, out):
    stack = ExitStack()
    with stack:
        def sb(name, shape, dt=F32):
            return stack.enter_context(nc.sbuf_tensor(name, shape, dt))

        def sem(name):
            return stack.enter_context(nc.semaphore(name))

        X = sb("X", [P, TILES, D])
        ident = sb("ident", [P, P])
        ident_bf = sb("ident_bf", [P, P], BF16)
        causal_bf = sb("causal_bf", [P, P], BF16)
        head_mask = sb("head_mask", [P, HEADS])
        half_mask = sb("half_mask", [P, 2])
        iota8 = sb("iota8", [P, E])
        iota_i = sb("iota_i", [P, E], mybir.dt.int32)
        neg_half = sb("neg_half", [P, 8])
        pos_half = sb("pos_half", [P, 8])
        W0T = sb("W0T", [P, 3, D])
        WoA = sb("WoA", [P, GROUPS, D])
        SEL = sb("SEL", [P, GROUPS, D + HEADS])
        upT = sb("upT", [P, HID])
        downT = sb("downT", [P, M, D])
        WcT = sb("WcT", [P, 1280])
        Wo1T = sb("Wo1T", [P, 8, D])
        Wq1 = sb("Wq1", [P, 512])
        Wkv1 = sb("Wkv1", [P, 1024])
        Wout1 = sb("Wout1", [P, 4, D])
        WF = sb("WF", [P, 3, HEADS, HD])
        gateW = sb("gateW", [P, E])
        W1 = sb("W1", [P, E, HID])
        W2 = sb("W2", [P, E, M, D])
        b2r = sb("b2r", [E, D])
        NVEC = 44
        V = sb("V", [P, NVEC])
        vs = sb("vs", [P, 2])
        bc = sb("bc", [P, 7, D])
        BV0, BO0, BO1, G1, C1, G2, C2 = range(7)
        BROW = sb("BROW", [P, 1024], F32R)
        CT_all = sb("CT_all", [P, BATCH, CTX])
        CN_all = sb("CN_all", [P, BATCH, CTX])

        with nc.sbuf_tensor("PARTS", [P, 4, SEQ], F32R) as PARTS:
            pass
        PTA = sb("PTA", [P, 7680])
        OTA = sb("OTA", [P, 4096])
        with nc.sbuf_tensor("QSTACK", [P, PAIRS, SEQ], F32R) as QSTACK:
            pass
        KMA = sb("KMA", [P, 8 * XK])
        VA = sb("VA", [P, 4096])
        VPA = sb("VPA", [P, 2048])
        QXA = sb("QXA", [P, 2048])
        PB = sb("PB", [P, 2, XK])
        YN = sb("YN", [P, QT, D])
        Y2 = sb("Y2", [P, QT, D])
        YT = sb("YT", [P, SEQ])
        YF = sb("YF", [P, QT, D])
        CT = sb("CT", [P, CTX])
        CN = sb("CN", [P, CTX])
        st = sb("st", [P, QT, 6])
        mv = sb("mv", [P, QT, 2])
        var = sb("var", [P, QT])
        rstd = sb("rstd", [P, QT])
        nmax = sb("nmax", [P, 2, 4])
        rsum = sb("rsum", [P, 2, 4])
        rinv = sb("rinv", [P, 2, 4])
        sm = sb("sm", [P, 16])

        KRING = sb("KRING", [P, 6, SEQ], F32R)
        PICKQ = sb("PICKQ", [P, 577], F32R)
        PICKK = sb("PICKK", [P, 578], F32R)
        row_mask = sb("row_mask", [P, 2])
        negmax = sb("negmax", [P, 2, 2, QT])
        maxparts = sb("maxparts", [P, 2, QT, 2, 2], F32R)
        ones_col = sb("ones_col", [P, 1])
        rsums = sb("rsums", [P, QT, HEADS])

        ones = YF[:, 0, :]
        vrow = Y2[0:NVEC, 0, :]
        scratch = OTA[:, 2048:3203]
        w0raw = VPA[:, 0:512].rearrange("p (w d) -> p w d", w=4)
        wo0pad = VPA[:, 512:1024].rearrange("p (j g c) -> p j g c", j=4, g=4)
        idpad = VPA[:, 1024:1536].rearrange("p (j g c) -> p j g c", j=4, g=4)
        upraw = QXA[:, 0:512]
        downraw = QXA[:, 512:1024]
        ctxraw = QXA[:, 1024:1536].rearrange("p (b d) -> p b d", b=4)
        ctxn = QXA[:, 1536:2048].rearrange("p (b d) -> p b d", b=4)
        wcraw = PTA[:, 0:1280]
        wo1raw = PTA[:, 1280:2304]
        tern = PTA[:, 2304:3328].rearrange("p (w n) -> p w n", w=2)
        ternq = PTA[:, 3328:4352].rearrange("p (w n) -> p w n", w=2)
        biasraw = PB[:, :, :].rearrange("p r n -> p (r n)")[:, 0:1024]
        wqkv = KMA[:, 0:384]
        gate = KMA[:, 384:896]
        val = KMA[:, 896:1408]
        proj = KMA[:, 1408:1920].rearrange("p (m d) -> p m d", m=M)
        projT = KMA[:, 1920:2432]
        pw = KMA[:, 2432:2560]
        bqkv = KMA[:, 2560:2944]
        kscale8 = KMA[:, 2944:2952]
        kbias8 = KMA[:, 2952:2960]
        kscale = KMA[:, 2960:3088]
        kbias = KMA[:, 3088:3216]
        bproj = KMA[:, 3456:3584]
        normw = KMA[:, 3584:3840]
        QTall = OTA[:, 0:2048]
        Kn = PTA[:, 0:2048].rearrange("p (t d) -> p t d", d=D)
        KTall = PTA[:, 2048:4096]
        Vn = PTA[:, 4096:6144].rearrange("p (t d) -> p t d", d=D)
        sg = [VA[:, 0:512], VA[:, 512:1024]]
        t1 = [VA[:, 1024:1536], VA[:, 1536:2048]]
        us = [VA[:, 2048:2560], VA[:, 2560:3072]]
        dg = VA[:, 3072:3584]
        du = VA[:, 3584:4096]
        hh = [OTA[:, 2048:2560], OTA[:, 2560:3072]]
        ww = [OTA[:, 3072:3584], OTA[:, 3584:4096]]
        zz = VPA[:, 512:1024]
        hTs = QXA[:, 0:512]
        dp = QXA[:, 512:640]
        dpT = QXA[:, 640:768]
        nx = [PTA[:, 6144 + 512 * i:6656 + 512 * i] for i in range(3)]
        nxT = [VA[:, 512 * i:512 * i + 512] for i in range(3)]
        nA = [QXA[:, 1024 + 128 * i:1152 + 128 * i] for i in range(3)]
        nB = [QXA[:, 1408 + 128 * i:1536 + 128 * i] for i in range(3)]
        nC = [VPA[:, 128 * i:128 * i + 128] for i in range(3)]
        aI = VPA[:, 384:512]

        qkvs = VA[:, 0:1024].rearrange("p (t w d) -> p t w d", t=QT, w=2)
        kraw = VA[:, 1024:1536].rearrange("p (t d) -> p t d", t=QT)
        sq4 = VA[:, 2048:3072]
        fh = VA[:, 0:2048].rearrange("p (m n) -> p m n", m=M)
        foT = VA[:, 2048:2560]
        fsg = VA[:, 2560:3584].rearrange("p (k n) -> p k n", k=2)
        ft = VPA[:, 512:1536].rearrange("p (k n) -> p k n", k=2)

        PSUM = stack.enter_context(nc.psum_tensor("PSUM", [P, 8, 512], F32))

        def bank(i, n=512):
            return PSUM[:, i, 0:n]

        s_x, s_w0, s_wt, s_wr, s_out = (sem(n) for n in ("x_loaded", "raw_loaded", "ttt_loaded", "rest_loaded", "stored"))
        s_const = sem("consts_ready")
        s_pad, s_absum, s_thr, s_tern = (sem(n) for n in ("pads_ready", "abs_sums", "abs_total", "ternary_ready"))
        s_tr, s_ev = sem("prep_transposed"), sem("prep_evacuated")

        class Norm:
            def __init__(self, name):
                self.var, self.rstd, self.done = sem(name + "_var"), sem(name + "_rstd"), sem(name + "_done")

        n_ctx, n_in, n_b = Norm("ctx_ln"), Norm("in_ln"), Norm("batch_ln")

        def ln_vector(dve, norm, n, srcs, dsts, rows=P):
            for j, s in enumerate(srcs):
                nc.vector.bn_stats(st[0:rows, j, :], s)
            dve.drain()
            for j in range(len(srcs)):
                nc.vector.bn_aggr(mv[0:rows, j, :], st[0:rows, j, :])
            dve.drain()
            k = len(srcs)
            nc.vector.tensor_scalar(var[0:rows, 0:k], mv[0:rows, 0:k, 1], LN_EPS, None, ALU.add).then_inc(norm.var, 1)
            dve.wait_ge(norm.rstd, n)
            for j, (s, d) in enumerate(zip(srcs, dsts)):
                nc.vector.tensor_scalar(d, s, mv[0:rows, j, 0:1], rstd[0:rows, j:j + 1], ALU.subtract, ALU.mult)\
                    .then_inc(norm.done, 1)

        def ln_pool(pool, norm, n, rows=P, k=QT):
            pool.wait_ge(norm.var, n)
            nc.gpsimd.tensor_tensor(rstd[0:rows, 0:k], var[0:rows, 0:k], neg_half[0:rows, 0:k], ALU.pow)\
                .then_inc(norm.rstd, 1)

        prep = []

        def group(srcs, dst, rows=P, after=None):
            prep.append((srcs, dst, rows, after))

        group([vrow[:, :]], V[:, :], NVEC, None)
        group([w0raw[:, i, :] for i in range(3)], W0T[:, :, :])
        group([ttt_tile for ttt_tile in (proj[:, m, :] for m in range(M))], projT)
        group([wcraw[:, i * P:(i + 1) * P] for i in range(0, 4)], WcT[:, 0:512])
        group([wcraw[:, i * P:(i + 1) * P] for i in range(4, 8)], WcT[:, 512:1024])
        group([wcraw[:, i * P:(i + 1) * P] for i in range(8, 10)], WcT[:, 1024:1280])
        group([wo1raw[:, i * P:(i + 1) * P] for i in range(0, 4)], Wo1T[:, 0:4, :])
        group([wo1raw[:, i * P:(i + 1) * P] for i in range(4, 8)], Wo1T[:, 4:8, :])
        group([ctxraw[0:CTX, b, :] for b in range(BATCH)], CT_all[:, :, :], CTX)
        group([wo0pad[:, j, :, :] for j in range(4)], WoA[:, :, :], P, "pads")
        group([idpad[:, j, :, :] for j in range(4)], SEL[:, :, 0:D], P, "pads")
        group([ctxn[0:CTX, b, :] for b in range(BATCH)], CN_all[:, :, :], CTX, "ctx")
        group([ternq[:, 0, i * P:(i + 1) * P] for i in range(4)], upT[:, :], P, "tern")
        group([ternq[:, 1, i * P:(i + 1) * P] for i in range(4)], downT[:, :, :], P, "tern")
        NPREP = len(prep)

        NLN = 8
        NTR = 6
        s_zero, s_brow = sem("value_pads_zero"), sem("value_bias_ready")
        s_ctx = sem("context_row_ready")
        s_bT, s_bTs = sem("rows_transposed"), sem("rows_T_ready")
        s_pow, s_powd = sem("square_sums_ready"), sem("roots_ready")
        s_rowdone = sem("row_done")

        (s_scores, s_max, s_exp, s_norm, s_turned, s_moved, s_values, s_outs) = (
            sem(w) for w in ("scores_ready", "maxima_ready", "exp_ready", "probs_normalised", "probs_turned", "probs_T_ready",
                             "values_ready", "values_copied"))

        class Attention:
            all_units, all_groups = 16 + 32, 4 + 4

            def __init__(self, before, units, group, out_banks, free, ring=2, lag=2):
                self.ring, self.lag = ring, lag
                self.units, self.group, self.out_banks, self.free = units, group, out_banks, free
                self.groups = units // group
                self.first_unit = before.first_unit + before.units if before else 0
                self.first_group = before.first_group + before.groups if before else 0

            def unit(self, b, i):
                return b * self.all_units + (self.first_unit + i)

            def summed(self, b, v):
                return b * self.all_groups + (self.first_group + v)

        def attention_tensor(pe, b, a, score, turn, value):
            U = a.units

            def values(v):
                pe.wait_ge(s_moved, a.unit(b, (v + 1) * a.group))
                if v >= a.out_banks:
                    pe.wait_ge(s_outs, a.summed(b, v + 1 - a.out_banks))
                value(v).then_inc(s_values, 1)

            for i in range(U + a.lag):
                if i < U:
                    if i >= 2:
                        pe.wait_ge(s_exp, a.unit(b, i - 1))
                    score(i).then_inc(s_scores, 1)
                k = i - a.lag
                if k >= 0:
                    pe.wait_ge(s_norm, a.unit(b, k + 1))
                    if k >= 2:
                        pe.wait_ge(s_moved, a.unit(b, k - 1))
                    turn(k).then_inc(s_turned, 1)
                    if k >= a.group and k % a.group == 2:
                        values(k // a.group - 1)
            values(a.groups - 1)

        def attention_scalar(act, b, a, exp, move):
            U = a.units
            for i in range(U + a.lag):
                if i < U:
                    act.wait_ge(s_max, a.unit(b, i + 1))
                    if i >= a.ring:
                        act.wait_ge(s_turned, a.unit(b, i + 1 - a.ring))
                    exp(i).then_inc(s_exp, 1)
                k = i - a.lag
                if k >= 0:
                    act.wait_ge(s_turned, a.unit(b, k + 1))
                    if a.free(k):
                        act.wait_ge(s_values, a.summed(b, a.free(k)))
                    move(k).then_inc(s_moved, 1)

        def attention_vector(dve, b, a, maximum, normalise, copy_out):
            U = a.units

            def out_of(v):
                dve.wait_ge(s_values, a.summed(b, v + 1))
                copy_out(v).then_inc(s_outs, 1)

            done = 0
            for i in range(U + 1):
                if i < U:
                    dve.wait_ge(s_scores, a.unit(b, i + 1))
                    maximum(i).then_inc(s_max, 1)
                if i >= 1:
                    dve.wait_ge(s_exp, a.unit(b, i))
                    normalise(i - 1).then_inc(s_norm, 1)
                if i == a.group * (done + 1) + 4:
                    out_of(done)
                    done += 1
            for v in range(done, a.groups):
                out_of(v)

        GH = GROUPS
        a0 = Attention(None, 16, 4, 2, lambda k: k // 4 - 1 if k % 4 == 0 and k >= 8 else 0)
        ax = Attention(a0, 32, 8, 1, lambda k: (k // 4 - 3) // 2 + 1 if k % 4 == 0 and k >= 12 else 0,
                       ring=3, lag=2)

        (m_parts, m_picked, m_stacked, m_keys, m_scores, m_max, m_split, m_turned, m_rows, m_scoresT, m_exp, m_acc01, m_acc23,
         m_acc, m_sums, m_inv, m_spread, m_norm, m_values, m_outs) = (sem("m_" + w) for w in (
            "parts", "picked", "stacked", "keys", "scores", "max", "max_split", "max_turned", "max_rows", "scores_T",
            "exp", "sum01", "sum23", "sum0123", "sums", "inverted", "spread", "normalised", "values", "values_copied"))

        class Paired:
            def __init__(self, row, causal, opening):
                self.row, self.causal, self.opening = row, causal, opening.split()

            def stacks(self, b, s):
                return (2 * b + self.row) * PAIRS + s

            def groups(self, b, v):
                return b * 12 + (8 if self.causal else 0) + v

            def width(self, t):
                return (t + 1) * P if self.causal else SEQ

            def first(self, c):
                return c * P if self.causal else 0

            def probsT(self, s, c):
                if self.causal:
                    w = SEQ - c * P
                    at = (s % 3) * 2560 + 2 * sum(SEQ - i * P for i in range(c))
                    return PTA[:, at:at + 2 * w].rearrange("p (e q) -> p e q", e=2)
                at = (4 * s + c) % 7 * 1024
                return PTA[:, at:at + 1024].rearrange("p (e q) -> p e q", e=2)

        full = Paired(0, False, "v v p p v p v t p t v t t v p t t v p t t v p t t p t x t")
        causal = Paired(1, True, "p p p t t p t t p t t p t t p x t t p t t")

        def paired_tensor(pe, b, a, value, finish, project_values=None):
            T = nc.tensor
            def pick(i):
                keys, s0 = i % 2 == 0, 2 * (i // 2)
                pe.wait_ge(m_parts, 4 * (2 * b + a.row) + (2 if keys else 4))
                if i >= 2:
                    pe.wait_ge(m_stacked, a.stacks(b, i - 1))
                weights, parts = (PICKK, 2) if keys else (PICKQ, 0)
                shift = 2 if keys else 1
                for j in range(2):
                    at = 64 * (s0 + j)
                    T.matmul(bank(2 + 2 * (i % 2) + j), weights[:, at + shift:at + shift + P], PARTS[:, parts, :],
                             start=True, stop=False)
                    last = T.matmul(bank(2 + 2 * (i % 2) + j), weights[:, at:at + P], PARTS[:, parts + 1, :],
                                    start=False, stop=True)
                last.then_inc(m_picked, 1)

            def scores(s, j):
                e, t = j // 4, j % 4
                w = a.width(t)
                if j == 0:
                    pe.wait_ge(m_stacked, a.stacks(b, 2 * (s // 2) + 2))
                if t == 0:
                    pe.wait_ge(m_keys, 2 * a.stacks(b, s) + e + 1)
                if j >= 2 or s >= 1:
                    pe.wait_ge(m_max, 8 * a.stacks(b, s) + j - 1)
                last = T.matmul(bank(j % 2, w), QSTACK[0:96, s, t * P:(t + 1) * P], KRING[0:96, (2 * s + e) % 6, 0:w],
                                start=True, stop=not a.causal)
                if a.causal:
                    last = T.matmul(PSUM[:, j % 2, t * P:(t + 1) * P], ident_bf[:, :], causal_bf[:, :], start=False, stop=True)
                last.then_inc(m_scores, 1)

            def turn_maxima(s):
                if s == 0 and not a.causal:
                    pe.wait_ge(s_d_vs, b * 8 + 8)
                pe.wait_ge(m_split, a.stacks(b, s + 1))
                if s >= 3 and not a.causal:
                    pe.wait_ge(m_norm, b * PAIRS + s - 2)
                elif s >= 1:
                    pe.wait_ge(m_rows, a.stacks(b, s))
                for t in range(QT):
                    last = T.matmul(PSUM[96:100, 7, t * P:(t + 1) * P],
                                    maxparts[:, s % 2, t, :, :].rearrange("p e w -> p (e w)").bitcast(F32), ident[:, :],
                                    start=True, stop=True)
                last.then_inc(m_turned, 1)

            def scores_T(s, c):
                k = 4 * s + c
                if k == 0:
                    pe.wait_ge(m_stacked, a.stacks(b, PAIRS))
                if c == 0:
                    pe.wait_ge(m_rows, a.stacks(b, s + 1))
                if k >= 2:
                    pe.wait_ge(m_exp, 4 * a.stacks(b, 0) + k - 1)
                w = SEQ - a.first(c)
                for e in range(2):
                    dst = PSUM[:, 2 + 2 * (k % 2) + e, :]
                    last = T.matmul(dst[:, 0:w], KRING[:, (2 * s + e) % 6, c * P:(c + 1) * P], QSTACK[:, s, a.first(c):SEQ],
                                    start=True, stop=not a.causal)
                    if a.causal:
                        last = T.matmul(dst[:, 0:P], causal_bf[:, :], ident_bf[:, :], start=False, stop=True)
                last.then_inc(m_scoresT, 1)

            def sums(s):
                pe.wait_ge(m_acc, b * PAIRS + s + 1)
                pe.wait_ge(m_rows, a.stacks(b, min(s + 3, PAIRS)))
                if s:
                    pe.wait_ge(m_norm, b * PAIRS + s)
                for t in range(QT):
                    for e in range(2):
                        at = e * SEQ + t * P
                        last = T.matmul(PSUM[:, 7, 2 * t + e:2 * t + e + 1], acc01[s % 2][:, at:at + P], ones_col[:, :],
                                        start=True, stop=True)
                last.then_inc(m_sums, 1)

            def spread(s):
                pe.wait_ge(m_inv, b * PAIRS + s + 1)
                for t in range(QT):
                    for e in range(2):
                        last = T.matmul(PSUM[e * VD:(e + 1) * VD, 7, t * P:(t + 1) * P],
                                        inv[:, 2 * t + e:2 * t + e + 1].to_broadcast([P, VD]), ident[:, :], start=True, stop=True)
                last.then_inc(m_spread, 1)

            def tiles(first, n):
                for i in range(first, min(first + n, 8 * PAIRS)):
                    scores(i // 8, i % 8)

            n = {"v": iter(range(8)), "p": iter(range(PAIRS)), "t": iter(range(12)), "x": iter(range(1))}
            for step in a.opening:
                {"v": project_values, "p": pick, "t": lambda i: tiles(i, 1), "x": turn_maxima}[step](next(n[step]))
            for s in range(PAIRS):
                ahead = 8 * s + 12
                scores_T(s, 0)
                tiles(ahead, 1)
                if s:
                    value(s - 1, 3)
                tiles(ahead + 1, 1)
                if s >= 2 and not a.causal:
                    spread(s - 2)
                scores_T(s, 1)
                tiles(ahead + 2, 2)
                value(s, 0)
                scores_T(s, 2)
                tiles(ahead + 4, 1)
                if a.causal and s + 1 < PAIRS:
                    turn_maxima(s + 1)
                value(s, 1)
                if not a.causal and s + 1 < PAIRS:
                    turn_maxima(s + 1)
                tiles(ahead + 5, 1)
                scores_T(s, 3)
                tiles(ahead + 6, 1)
                value(s, 2)
                tiles(ahead + 7, 1)
                if s and not a.causal:
                    sums(s - 1)
            value(PAIRS - 1, 3)
            if a.causal:
                finish(0, 3)
                finish(3, 1)
            else:
                spread(PAIRS - 2)
                finish(0, 6)
                sums(PAIRS - 1)
                finish(6, 1)
                spread(PAIRS - 1)
                finish(7, 1)

        def paired_scalar(act, b, a, values=None):
            A = nc.scalar
            def stack_rows(i):
                keys, s0 = i % 2 == 0, 2 * (i // 2)
                act.wait_ge(m_picked, a.stacks(b, i + 1))
                k = 2 + 2 * (i % 2)
                if keys:
                    last = A.activation(KSTACK[:, s0:s0 + 2, :], PSUM[0:64, k:k + 2, :], ACT.Copy)
                else:
                    last = A.activation(QSTACK[:, s0:s0 + 2, :], PSUM[:, k:k + 2, :], ACT.Copy)
                last.then_inc(m_stacked, 1)

            def max_rows(s):
                act.wait_ge(m_turned, a.stacks(b, s + 1))
                A.activation(QSTACK[96:100, s, :], PSUM[96:100, 7, :], ACT.Copy).then_inc(m_rows, 1)

            def copy_out(s):
                if not a.causal or s % 2:
                    v = s // 2 if a.causal else s
                    act.wait_ge(m_values, a.groups(b, v + 1))
                    A.activation(OT[:, v, :], bank(6), ACT.Copy).then_inc(m_outs, 1)

            n = {"v": iter(range(8)), "p": iter(range(PAIRS)), "x": iter(range(1))}
            for step in a.opening:
                if step in n:
                    {"v": values, "p": stack_rows, "x": max_rows}[step](next(n[step]))
            for s in range(PAIRS):
                for c in range(4):
                    k = 4 * s + c
                    act.wait_ge(m_scoresT, 4 * a.stacks(b, 0) + k + 1)
                    if a.causal:
                        if c == 0 and s >= 3:
                            act.wait_ge(m_values, a.groups(b, (s - 3) // 2 + 1))
                    elif k >= 7:
                        act.wait_ge(m_values, a.groups(b, (k - 7) // 4 + 1))
                        if c < 3:
                            act.wait_ge(m_acc, b * PAIRS + s - 1)
                        else:
                            act.wait_ge(m_acc01, b * PAIRS + s)
                    A.activation(a.probsT(s, c), PSUM[:, 2 + 2 * (k % 2):4 + 2 * (k % 2), 0:SEQ - a.first(c)], ACT.Exp)                        .then_inc(m_exp, 1)
                    if c == 0 and s:
                        copy_out(s - 1)
                    if c == 2 and s + 1 < PAIRS:
                        max_rows(s + 1)
            copy_out(PAIRS - 1)

        def paired_vector(dve, b, a, values=None):
            Vv = nc.vector

            def maxima(s, j):
                e, t = j // 4, j % 4
                dve.wait_ge(m_scores, 8 * a.stacks(b, s) + j + 1)
                Vv.tensor_reduce(negmax[:, s % 2, e, t:t + 1], bank(j % 2, a.width(t)), AX.X, ALU.max, negate=True)                    .then_inc(m_max, 1)

            def split_maxima(s):
                dve.drain()
                nm = negmax[:, s % 2, :, :].rearrange("p e t -> p t e")
                Vv.tensor_copy(maxparts[:, s % 2, :, :, 0], nm)
                dve.drain()
                Vv.tensor_tensor(maxparts[:, s % 2, :, :, 1], nm, maxparts[:, s % 2, :, :, 0].bitcast(F32), ALU.subtract)                    .then_inc(m_split, 1)

            def invert(s):
                dve.wait_ge(m_sums, b * PAIRS + s + 1)
                Vv.reciprocal(inv, PSUM[:, 7, 0:2 * QT]).then_inc(m_inv, 1)

            def normalise(s):
                dve.wait_ge(m_outs, a.groups(b, s + 1))
                dve.wait_ge(m_spread, b * PAIRS + s + 1)
                Vv.tensor_tensor(OT[:, s, :], OT[:, s, :], bank(7), ALU.mult).then_inc(m_norm, 1)

            def tiles(first, n):
                for i in range(first, min(first + n, 8 * PAIRS)):
                    maxima(i // 8, i % 8)
                    if i % 8 == 7:
                        split_maxima(i // 8)

            def add23(s):
                dve.wait_ge(m_exp, 4 * a.stacks(b, s + 1))
                if s:
                    dve.wait_ge(m_acc, b * PAIRS + s)
                Vv.tensor_tensor(acc23.rearrange("p (e q) -> p e q", e=2), a.probsT(s, 2), a.probsT(s, 3), ALU.add)                    .then_inc(m_acc23, 1)

            n = {"v": iter(range(8)), "t": iter(range(12))}
            for step in a.opening:
                if step in n:
                    {"v": values, "t": lambda i: tiles(i, 1)}[step](next(n[step]))
            for s in range(PAIRS):
                ahead = 8 * s + 12
                tiles(ahead, 2)
                if s and not a.causal:
                    add23(s - 1)
                tiles(ahead + 2, 1)
                if s >= 2 and not a.causal:
                    normalise(s - 2)
                tiles(ahead + 3, 1)
                tiles(ahead + 4, 4)
                if s and not a.causal:
                    invert(s - 1)
            if not a.causal:
                add23(PAIRS - 1)
                normalise(PAIRS - 2)
                invert(PAIRS - 1)
                normalise(PAIRS - 1)

        def paired_pool(pool, b, a):
            g = nc.gpsimd

            def keys(s):
                for e in range(2):
                    rows = slice(LANE * e, LANE * (e + 1))
                    g.tensor_tensor(KRING[rows, (2 * s + e) % 6, :], KSTACK[rows, s, :],
                                    ones_col[rows, 0:1].to_broadcast([LANE, SEQ]), ALU.mult).then_inc(m_keys, 1)

            pool.wait_ge(m_stacked, a.stacks(b, 1))
            keys(0)
            keys(1)
            pool.wait_ge(m_stacked, a.stacks(b, 3))
            keys(2)
            pool.drain()
            for s in range(PAIRS):
                if not a.causal:
                    pool.wait_ge(m_exp, 4 * a.stacks(b, s) + 2)
                    if s >= 2:
                        pool.wait_ge(m_sums, b * PAIRS + s - 1)
                    g.tensor_tensor(acc01[s % 2].rearrange("p (e q) -> p e q", e=2), a.probsT(s, 0), a.probsT(s, 1), ALU.add)                        .then_inc(m_acc01, 1)
                    pool.drain()
                if s + 3 < PAIRS:
                    pool.wait_ge(m_stacked, a.stacks(b, (s + 3) // 2 * 2 + 1))
                    pool.wait_ge(m_scoresT, 4 * a.stacks(b, s + 1))
                    keys(s + 3)
                if not a.causal:
                    pool.drain()
                    pool.wait_ge(m_acc23, b * PAIRS + s + 1)
                    g.tensor_tensor(acc01[s % 2], acc01[s % 2], acc23, ALU.add).then_inc(m_acc, 1)
            pool.drain()

        s_b_k, s_b_v, s_b_q, s_b_ks, s_b_vs, s_b_qs, s_b_km, s_b_o = (sem("x0_" + n) for n in (
            "k", "v", "q", "k_biased", "v_biased", "q_scaled", "k_masked", "out"))
        s_c_u, s_c_g, s_c_r1, s_c_T, s_c_Ts, s_c_o = (sem("ffn_" + n) for n in (
            "up", "gelu", "rms", "turned", "moved", "down"))
        s_d_q, s_d_qb, s_d_v, s_d_vx, s_d_vs, s_d_o = (sem("a1_" + n) for n in (
            "qk", "qk_biased", "v", "v_sloped", "v_ready", "out"))
        s_e_q, s_e_qs, s_e_k, s_e_ks, s_e_v, s_e_vs, s_e_o = (sem("x1_" + n) for n in (
            "q", "q_ready", "k", "k_masked", "v", "v_ready", "out"))
        s_f_q, s_f_qs, s_f_v, s_f_vs, s_f_o, s_f_y, s_f_g, s_f_d, s_f_e, s_f_c, s_f_cT, s_f_cTs, s_f_b2 = (
            sem("f1_" + n) for n in ("qk", "qk_ready", "v", "v_ready", "attn", "y_ready", "gate", 
                                     "top_gap", "top_exp", "combine", "combine_turned", "combine_T", "b2"))
        s_f_h, s_f_hs, s_f_dn, s_f_acc = (sem("moe_" + n) for n in ("hidden", "relu", "down", "added"))

        PSF = PSUM[:, :, :].rearrange("p b n -> p (b n)")
        VP = VPA[:, :].rearrange("p (t h c) -> p t h c", t=QT, h=HEADS)
        QS = QXA[:, 0:512]
        Qraw = QXA[:, 512:1024]
        Kraw = QXA[:, 1024:1536]
        KT0 = QXA[:, 1536:2048]
        KM0 = KMA[:, 0:HEADS * CTX].rearrange("p (h k) -> p h k", h=HEADS)
        KSTACK = OTA[0:64, :].rearrange("p (s k) -> p s k", s=PAIRS)
        acc01 = [QXA[:, 0:1024], PB[:, :, :].rearrange("p r n -> p (r n)")[:, 0:1024]]
        PBX = [PB[:, 0, :], PB[:, 1, :], VA[:, 2560:2560 + XK]]
        acc23 = QXA[:, 1024:2048]
        inv = rinv[:, :, :].rearrange("p a b -> p (a b)")
        KM8 = KMA[:, :].rearrange("p (h k) -> p h k", h=8)
        PT0 = PTA[:, 0:4096].rearrange("p (r g q) -> p r g q", r=2, g=4)
        PTe = PTA[:, :].rearrange("p (r k q) -> p r k q", r=3, k=5)
        OT = OTA[:, :].rearrange("p (g q) -> p g q", q=SEQ)
        V1 = VA[:, :].rearrange("p (k n) -> p k n", k=QT)
        VX = VA[:, 0:2560].rearrange("p (k n) -> p k n", k=5)
        HC = VA[:, 0:2048].rearrange("p (t n) -> p t n", t=QT)
        HTC = PTA[:, 0:2048].rearrange("p (t n) -> p t n", t=QT)
        HE = PTA[:, 0:4096].rearrange("p (r m n) -> p r m n", r=2, m=M)
        QX = QXA[:, :].rearrange("p (g q) -> p g q", q=SEQ)
        ssq = sb("ssq", [P, 2, QT])
        root = sb("root", [P, 2, QT])
        logit = sb("logit", [P, QT, E])
        top = sb("top", [P, QT, E])
        topi = sb("topi", [P, QT, E], U32)
        topf = logit[:, :, :]
        comb = sb("comb", [P, QT, E])
        comb2 = rsums[:, :, 0:E]
        tw = rsums[:, :, E:E + 4]
        combT = QXA[0:E, 512:1024]

        GM, BM, GL, BL, BQ0, BK0, BCQ, BCK = range(8)
        B1C = 8
        QSC, QBI, KSC, KBI = range(40, 44)

        block = stack.enter_context(nc.Block())

        s_yT, s_yTs = sem("in_transposed"), sem("in_yT_ready")
        s_qkv, s_ss, s_nrm, s_qk = (sem(n) for n in ("qkv_ready", "head_sums", "head_norms", "qk_ready"))
        s_qkT, s_qkTs, s_kn, s_uc = (sem(n) for n in ("qk_transposed", "qkT_stored", "k_stored", "value_copied"))
        s_gu, s_sig, s_t, s_h, s_w = (sem(n) for n in ("gu_ready", "sigmoid_ready", "silu_ready", "h_ready", "w_ready"))
        s_hT, s_hTs, s_pred, s_dp, s_dpT, s_dpTs, s_dh, s_dgu = (sem(n) for n in (
            "hT_ready", "hT_stored", "pred_ready", "dpred_ready", "dpredT_ready", "dpredT_stored", "dh_ready", "dgu_ready"))
        s_grad, s_gs, s_sq, s_tot, s_tots, s_nrt, s_x0 = (sem(n) for n in (
            "grads_ready", "grads_stored", "square_sums", "square_total", "total_stored", "norm_ready", "x_scaled"))
        s_xt0, s_xt0s = sem("ns_xT_ready"), sem("ns_xT_stored")
        s_A, s_As, s_A2, s_B, s_XN, s_XTN, s_XNs, s_XTNs, s_upd = (sem(n) for n in (
            "ns_A", "ns_A_stored", "ns_A2", "ns_B", "ns_X", "ns_XT", "ns_X_stored", "ns_XT_stored", "weights_updated"))
        s_fg, s_fu, s_fs, s_fh, s_fo, s_fos, s_fy, s_fx = (sem(n) for n in (
            "f_gate", "f_val", "f_sigmoid", "f_h", "f_o", "f_oT", "f_y", "f_x"))

        @block.sync
        def _(sp):
            def load(dst, src, s):
                sp.dma_start(dst, src).then_inc(s, 16)

            for i, w in enumerate((x0_Wq, x0_Wk, x0_Wv, x0_Wo)):
                load(w0raw[:, i, :], w, s_w0)
            load(proj, ttt_proj.rearrange("(m p) d -> p m d", p=P), s_w0)
            load(wcraw.rearrange("p (t d) -> p t d", d=D), a1_Wc.rearrange("(t p) d -> p t d", p=P), s_w0)
            load(wo1raw, a1_Wo, s_w0)
            load(ctxraw[0:CTX, :, :], ctx_1024.rearrange("b s d -> s b d"), s_w0)
            load(upraw.rearrange("p (t d) -> p t d", d=D), w_up.rearrange("(t p) d -> p t d", p=P), s_w0)
            load(downraw, w_down, s_w0)
            load(X[:, :, :], x.rearrange("b (t p) d -> p (b t) d", p=P), s_x)
            load(wqkv, qkv_w, s_wt)
            load(gate, ttt_gate, s_wt)
            load(val, ttt_val, s_wt)
            load(pw, proj_w, s_wt)
            load(bqkv, qkv_b.partition_broadcast(P), s_wt)
            load(bproj, proj_b.partition_broadcast(P), s_wt)
            load(kscale8, kn_scale.partition_broadcast(P), s_wt)
            load(kbias8, kn_bias.partition_broadcast(P), s_wt)
            for i, w in enumerate((x0_bv, x0_bo, a1_bo, f1_g1, f1_c1, f1_g2, f1_c2)):
                load(bc[:, i, :], w.partition_broadcast(P), s_wr)
            load(biasraw[96:128, :], a1_bc[256:1280].partition_broadcast(32), s_wr)
            load(Wq1[:, :], x1_Wq, s_wr)
            load(Wkv1[:, :], x1_Wkv, s_wr)
            load(Wout1[:, :, :], x1_Wout.rearrange("(m p) d -> p m d", p=P), s_wr)
            for i, w in enumerate((f1_Wq, f1_Wk, f1_Wv)):
                load(WF[:, i, :, :], w.rearrange("h d f -> d h f"), s_wr)
            load(gateW[:, :], f1_gate, s_wr)
            load(b2r[:, :], f1_b2, s_wr)
            load(W1[:, :, :], f1_W1.rearrange("e d f -> d e f"), s_wr)
            load(W2[:, :, :, :].rearrange("p e m d -> p (e m) d"), f1_W2.rearrange("e (m p) d -> p (e m) d", p=P), s_wr)
            with sp.Fori(0, BATCH) as b:
                sp.wait_ge(s_rowdone, b + 1)
                sp.dma_start(out[bass.ds(b, 1), :, :].rearrange("o (t p) d -> p (o t) d", p=P),
                             X[:, bass.ds(b * QT, QT), :]).then_inc(s_out, 16)
            sp.wait_ge(s_out, 16 * BATCH)

        N_W0, N_WT, N_WR = 16 * 22, 16 * 8, 16 * 18

        @block.gpsimd
        def _(pool):
            g = nc.gpsimd
            g.memset(ident[:, :], 0.0)
            g.memset(ones[:, :], 1.0)
            g.memset(head_mask[:, :], 1.0)
            g.memset(half_mask[:, :], 0.0)
            g.memset(causal_bf[:, :], 0.0)
            g.memset(neg_half[:, :], -0.5)
            g.memset(pos_half[:, :], 0.5)
            g.memset(VPA[:, 512:1536], 0.0)
            g.memset(ones_col[:, :], 1.0)
            g.memset(SEL[:, :, D:D + HEADS], 0.0)
            g.memset(row_mask[:, :], 1.0)
            g.iota(iota_i[:, :], pattern=[[1, E]], base=0, channel_multiplier=0)
            pool.drain()
            g.tensor_copy(iota8[:, :], iota_i[:, :])
            g.memset(half_mask[0:64, 0:1], 1.0)
            pool.drain()
            g.memset(half_mask[64:128, 1:2], 1.0)
            pool.drain()
            g.affine_select(out=ident[:, :], in_=ident[:, :], compare_op=ALU.not_equal, fill=1.0, base=0,
                            pattern=[[-1, P]], channel_multiplier=1)
            g.affine_select(out=head_mask[:, :], in_=head_mask[:, :], compare_op=ALU.is_ge, fill=0.0, base=0,
                            pattern=[[-HD, HEADS]], channel_multiplier=1)
            g.affine_select(out=causal_bf[:, :], in_=causal_bf[:, :], compare_op=ALU.is_ge, fill=MASKED, base=0,
                            pattern=[[-1, P]], channel_multiplier=1)
            g.affine_select(out=SEL[:, :, D:D + HEADS], in_=SEL[:, :, D:D + HEADS], compare_op=ALU.not_equal, fill=1.0, base=-HD,
                            pattern=[[P, GROUPS], [-LANE, HEADS]], channel_multiplier=1)
            g.affine_select(out=row_mask[:, :], in_=row_mask[:, :], compare_op=ALU.is_ge, fill=0.0, base=-96,
                            pattern=[[-2, 2]], channel_multiplier=1)
            pool.drain()
            g.affine_select(out=row_mask[:, :], in_=row_mask[:, :], compare_op=ALU.is_ge, fill=0.0, base=97,
                            pattern=[[2, 2]], channel_multiplier=-1)
            pool.drain()
            g.affine_select(out=head_mask[:, :], in_=head_mask[:, :], compare_op=ALU.is_ge, fill=0.0, base=HD - 1,
                            pattern=[[HD, HEADS]], channel_multiplier=-1)
            g.tensor_copy(ident_bf[:, :], ident[:, :])
            g.tensor_scalar(idpad[:, :, :, 0:HD], ident[:, :].rearrange("p (j g c) -> p j g c", j=4, g=4),
                            1.0, None, ALU.mult).then_inc(s_const, 1)
            pool.drain()
            pool.wait_ge(s_w0, N_W0)
            g.tensor_copy(wo0pad[:, :, :, 0:HD], w0raw[:, 3, :].rearrange("p (j g c) -> p j g c", j=4, g=4))\
                .then_inc(s_pad, 1)
            ln_pool(pool, n_ctx, 1, CTX)
            def chunk(c, more):
                if more:
                    ln_pool(pool, n_in, c + 2)
                pool.wait_ge(s_qk, c + 1)
                g.tensor_tensor(kraw, qkvs[:, :, 1, :], kscale.unsqueeze(1).to_broadcast([P, QT, D]), ALU.mult)
                pool.drain()
                g.tensor_tensor(Kn[:, bass.ds(c * QT, QT), :], kraw, kbias.unsqueeze(1).to_broadcast([P, QT, D]), ALU.add)\
                    .then_inc(s_kn, 1)

            ln_pool(pool, n_in, 1)
            with pool.Fori(0, BATCH - 1) as c:
                chunk(c, True)
            chunk(BATCH - 1, False)
            with pool.Fori(0, STEPS) as step:
                for t in range(TILES):
                    n, par = step * TILES + t, t % 2
                    pool.wait_ge(s_t, n + 1)
                    g.tensor_tensor(zz, sg[par], t1[par], ALU.mult)
                    if t >= 2:
                        pool.wait_ge(s_dgu, n - 1)
                    g.tensor_tensor(ww[par], sg[par], t1[par], ALU.add)
                    pool.drain()
                    g.tensor_tensor(ww[par], ww[par], zz, ALU.subtract)
                    pool.drain()
                    pool.wait_ge(s_uc, n + 1)
                    g.tensor_tensor(ww[par], ww[par], us[par], ALU.mult).then_inc(s_w, 1)
                pool.wait_ge(s_tots, step + 1)
                g.tensor_tensor(sm[:, 8:11], sm[:, 4:7], pos_half[:, 0:3], ALU.pow).then_inc(s_nrt, 1)


            def next_row(n):
                row = n % BATCH
                g.tensor_copy(CT[:, :], CT_all[:, bass.ds(row, 1), :].rearrange("p o s -> p (o s)"))
                g.tensor_copy(CN[:, :], CN_all[:, bass.ds(row, 1), :].rearrange("p o s -> p (o s)")).then_inc(s_ctx, 1)

            pool.drain()
            pool.wait_ge(s_upd, STEPS)
            g.memset(scratch, 0.0)
            pool.drain()
            pq, pk = scratch[:, 0:577], scratch[:, 577:1155]
            for i in range(2):
                g.affine_select(out=pq, in_=pq, compare_op=ALU.not_equal, fill=1.0, base=1 + 2 * i, pattern=[[-1, 577]],
                                channel_multiplier=4)
                g.affine_select(out=pk, in_=pk, compare_op=ALU.not_equal, fill=1.0, base=2 + i, pattern=[[-1, 578]],
                                channel_multiplier=4)
                pool.drain()
            g.tensor_copy(PICKQ[:, :], pq)
            g.tensor_copy(PICKK[:, :], pk)
            for i in range(6):
                g.tensor_copy(KRING[:, i, :], row_mask[:, i % 2:i % 2 + 1].to_broadcast([P, SEQ]))
            tail = slice(96, 128)
            pool.drain()
            pool.wait_ge(s_wr, N_WR)
            g.tensor_copy(BROW[tail, :], biasraw[tail, :])
            pool.drain()
            g.tensor_tensor(biasraw[tail, :], biasraw[tail, :], BROW[tail, :].bitcast(F32), ALU.subtract)
            pool.drain()
            g.tensor_tensor(biasraw[tail, :], biasraw[tail, :], ident[tail, 97:98].to_broadcast([32, 1024]), ALU.mult)
            g.tensor_tensor(BROW[tail, :], BROW[tail, :].bitcast(F32), ident[tail, 96:97].to_broadcast([32, 1024]), ALU.mult)
            pool.drain()
            g.tensor_tensor(BROW[tail, :], BROW[tail, :].bitcast(F32), biasraw[tail, :], ALU.add).then_inc(s_brow, 1)
            pool.drain()
            next_row(0)
            ln_pool(pool, n_b, 1)
            with pool.Fori(0, BATCH) as b:
                ln = iter(range(2, NLN + 2))

                def norm():
                    ln_pool(pool, n_b, b * NLN + next(ln))

                norm()
                for i in range(2):
                    pool.wait_ge(s_pow, 2 * b + i + 1)
                    g.tensor_tensor(root[:, i, :], ssq[:, i, :], pos_half[:, 0:QT], ALU.pow).then_inc(s_powd, 1)
                norm()
                paired_pool(pool, b, full)
                norm()
                norm()
                norm()
                paired_pool(pool, b, causal)
                norm()
                next_row(b + 1)
                norm()
                norm()
            pool.wait_ge(s_rowdone, BATCH)

        @block.tensor
        def _(pe):
            T = nc.tensor
            pe.wait_ge(s_const, 1)
            pe.wait_ge(s_w0, N_W0)
            pe.wait_ge(s_absum, 1)
            T.matmul(bank(7, 2), ones[:, :], sm[:, 0:2], start=True, stop=True).then_inc(s_thr, 1)
            for i, (srcs, dst, rows, after) in enumerate(prep):
                if after == "pads":
                    pe.wait_ge(s_pad, 1)
                if after == "ctx":
                    pe.wait_ge(n_ctx.done, BATCH)
                if after == "tern":
                    pe.wait_ge(s_tern, 1)
                if i >= 7:
                    pe.wait_ge(s_ev, i - 6)
                for j, s in enumerate(srcs):
                    last = T.transpose(PSUM[:, i % 7, j * rows:(j + 1) * rows], s, ident[0:rows, 0:rows])
                last.then_inc(s_tr, 1)
            pe.wait_ge(s_ev, NPREP)
            pe.wait_ge(s_wt, N_WT)
            def turn_inputs(c):
                for j in range(QT):
                    pe.wait_ge(n_in.done, c * QT + (j + 1))
                    last = T.transpose(PSUM[:, 0, j * P:(j + 1) * P], YN[:, j, :], ident[:, :])
                last.then_inc(s_yT, 1)

            def chunk(c, more, first=False):
                pe.wait_ge(s_yTs, c + 1)
                for j in range(QT):
                    T.matmul(PSUM[:, 1 + j, 0:384], YT[:, j * P:(j + 1) * P], wqkv, start=True, stop=True)\
                        .then_inc(s_qkv, 1)
                if more:
                    turn_inputs(c + 1)
                if not first:
                    pe.wait_ge(s_qkTs, 2 * c)
                for w in range(2):
                    pe.wait_ge(s_qk, c + 1)
                    for j in range(QT):
                        last = T.transpose(PSUM[:, 5 + w, j * P:(j + 1) * P], qkvs[:, j, w, :], ident[:, :])
                    last.then_inc(s_qkT, 1)

            turn_inputs(0)
            chunk(0, True, first=True)
            with pe.Fori(1, BATCH - 1) as c:
                chunk(c, True)
            chunk(BATCH - 1, False)
            pe.wait_ge(s_qkTs, 2 * BATCH)
            pe.wait_ge(s_kn, BATCH)

            with pe.Fori(0, STEPS) as step:
                def gate_val(t):
                    T.matmul(bank(0), KTall[:, t * P:(t + 1) * P], gate, start=True, stop=True)
                    T.matmul(bank(1), KTall[:, t * P:(t + 1) * P], val, start=True, stop=True).then_inc(s_gu, 1)

                def up_grads(t):
                    pe.wait_ge(s_dgu, step * TILES + t + 1)
                    T.matmul(bank(5), Kn[:, t, :], dg, start=(t == 0), stop=(t == TILES - 1))
                    return T.matmul(bank(6), Kn[:, t, :], du, start=(t == 0), stop=(t == TILES - 1))

                gate_val(0)
                for t in range(TILES):
                    n, par = step * TILES + t, t % 2
                    pe.wait_ge(s_h, n + 1)
                    for m in range(M):
                        last = T.transpose(PSUM[:, 2, m * P:(m + 1) * P], hh[par][:, m * P:(m + 1) * P], ident[:, :])
                    last.then_inc(s_hT, 1)
                    if t + 1 < TILES:
                        pe.wait_ge(s_uc, n + 1)
                        gate_val(t + 1)
                    if t:
                        up_grads(t - 1)
                    pe.wait_ge(s_hTs, n + 1)
                    for m in range(M):
                        last = T.matmul(bank(3, P), hTs[:, m * P:(m + 1) * P], proj[:, m, :], start=(m == 0), stop=(m == M - 1))
                    last.then_inc(s_pred, 1)
                    pe.wait_ge(s_dp, n + 1)
                    T.transpose(PSUM[:, 3, 128:256], dp, ident[:, :]).then_inc(s_dpT, 1)
                    T.matmul(bank(7), dp, hh[par], start=(t == 0), stop=(t == TILES - 1))
                    pe.wait_ge(s_dpTs, n + 1)
                    T.matmul(bank(4), dpT, projT, start=True, stop=True).then_inc(s_dh, 1)
                up_grads(TILES - 1).then_inc(s_grad, 1)
                pe.wait_ge(s_sq, step + 1)
                T.matmul(bank(0, 3), ones[:, :], sm[:, 0:3], start=True, stop=True).then_inc(s_tot, 1)
                for i in range(3):
                    pe.wait_ge(s_x0, step * 3 + i + 1)
                    for m in range(M):
                        last = T.transpose(PSUM[:, 1 + i, m * P:(m + 1) * P], nx[i][:, m * P:(m + 1) * P], ident[:, :])
                    last.then_inc(s_xt0, 1)
                with pe.Fori(0, NS_ITERS) as it:
                    pe.wait_ge(s_xt0s, step * 3 + 3)
                    k = (step * NS_ITERS + it) * 3
                    for i in range(3):
                        for m in range(M):
                            last = T.matmul(PSUM[:, i, 0:P], nxT[i][:, m * P:(m + 1) * P], nxT[i][:, m * P:(m + 1) * P],
                                            start=(m == 0), stop=(m == M - 1))
                        last.then_inc(s_A, 1)
                    for i in range(3):
                        pe.wait_ge(s_As, k + i + 1)
                        T.matmul(PSUM[:, i, P:2 * P], nA[i], nA[i], start=True, stop=True).then_inc(s_A2, 1)
                    for i, (bx, bt) in enumerate(((3, 4), (5, 6), (7, 3))):
                        pe.wait_ge(s_B, k + i + 1)
                        T.matmul(bank(bx), nB[i], nx[i], start=True, stop=True).then_inc(s_XN, 1)
                        if i == 2:
                            pe.wait_ge(s_XNs, k + 1)
                        for m in range(M):
                            last = T.matmul(PSUM[:, bt, m * P:(m + 1) * P], nx[i][:, m * P:(m + 1) * P], nB[i],
                                            start=True, stop=True)
                        last.then_inc(s_XTN, 1)
                    pe.wait_ge(s_XNs, k + 3)
                    pe.wait_ge(s_XTNs, k + 3)
                pe.wait_ge(s_upd, step + 1)

            with pe.Fori(0, BATCH) as c:
                q = QTall[:, bass.ds(c * SEQ, SEQ)]
                for m in range(M):
                    n = c * M + m
                    if m >= 2:
                        pe.wait_ge(s_fh, n - 1)
                    T.matmul(bank(m % 2), gate[:, m * P:(m + 1) * P], q, start=True, stop=True).then_inc(s_fg, 1)
                    T.matmul(bank(2 + m % 2), val[:, m * P:(m + 1) * P], q, start=True, stop=True).then_inc(s_fu, 1)
                for m in range(M):
                    pe.wait_ge(s_fh, c * M + m + 1)
                    last = T.matmul(bank(4), proj[:, m, :], fh[:, m, :], start=(m == 0), stop=(m == M - 1))
                last.then_inc(s_fo, 1)
                pe.wait_ge(s_fos, c + 1)
                for j in range(QT):
                    last = T.matmul(PSUM[:, 5, j * P:(j + 1) * P], foT[:, j * P:(j + 1) * P], pw, start=True, stop=True)
                last.then_inc(s_fy, 1)
                pe.wait_ge(s_fx, c + 1)

            def turn_tiles(src, norm=None):
                for j in range(QT):
                    if norm is not None:
                        pe.wait_ge(n_b.done, QT * (norm - 1) + (j + 1))
                    last = T.transpose(PSUM[:, 7, j * P:(j + 1) * P], src[:, j, :], ident[:, :])
                last.then_inc(s_bT, 1)

            def project_context(n):
                pe.wait_ge(s_ctx, n + 1)
                T.matmul(bank(7, CTX), W0T[:, 1, :], CT[:, :], start=True, stop=True).then_inc(s_b_k, 1)
                T.matmul(PSUM[0:CTX, 6, 0:P], CT[:, :], W0T[:, 2, :], start=True, stop=True).then_inc(s_b_v, 1)

            def turn_first(n, norm):
                pe.wait_ge(s_b_ks, n + 1)
                pe.wait_ge(s_b_vs, n + 1)
                turn_tiles(YN, norm)

            def project_queries(n):
                pe.wait_ge(s_bTs, n * NTR + 1)
                T.matmul(bank(6), W0T[:, 0, :], YT[:, :], start=True, stop=True).then_inc(s_b_q, 1)

            pe.wait_ge(s_zero, 1)
            pe.wait_ge(s_brow, 1)
            project_context(0)
            turn_first(0, 1)
            project_queries(0)
            with pe.Fori(0, BATCH) as b:
                lns = iter(range(2, NLN + 2))
                trs = iter(range(2, NTR + 2))

                def turn_rows(src, norm_done=True, extra=0):
                    for _ in range(extra):
                        next(lns)
                    norm = b * NLN + next(lns)
                    turn_tiles(src, norm if norm_done else None)
                    pe.wait_ge(s_bTs, b * NTR + next(trs))

                def project(dst, n, weights, s):
                    for j in range(QT):
                        for k in range(n):
                            last = T.matmul(PSUM[:, dst, j * P:(j + 1) * P], OT[:, k, j * P:(j + 1) * P], weights[:, k, :],
                                            start=(k == 0), stop=(k == n - 1))
                    last.then_inc(s, 1)

                pe.wait_ge(s_b_qs, b + 1)
                pe.wait_ge(s_b_km, b + 1)

                def score(i):
                    j, t = i // 4, i % 4
                    return T.matmul(bank(i % 2, 4 * CTX), QS[:, t * P:(t + 1) * P], KM0[:, 4 * j:4 * j + 4, :],
                                    start=True, stop=True)

                def turn(k):
                    for g in range(GH):
                        last = T.transpose(PSUM[0:CTX, 2 + k % 2, g * P:(g + 1) * P], PB[:, k % 2, g * CTX:(g + 1) * CTX],
                                           ident[:, :])
                    return last

                def value(v):
                    for g in range(GH):
                        last = T.matmul(PSUM[g * LANE:(g + 1) * LANE, 4 + v % 2, :], VP[0:CTX, 0, 4 * v + g, :],
                                        PT0[0:CTX, v % 2, g, :], start=True, stop=True)
                    return last

                attention_tensor(pe, b, a0, score, turn, value)
                pe.wait_ge(s_outs, a0.summed(b, 4))
                project(6, GROUPS, WoA, s_b_o)

                turn_rows(YN)
                for t in range(QT):
                    T.matmul(bank(t), YT[:, t * P:(t + 1) * P], upT[:, :], start=True, stop=True).then_inc(s_c_u, 1)
                for t in range(QT):
                    pe.wait_ge(s_c_g, b * QT + t + 1)
                    if t >= 2:
                        pe.wait_ge(s_c_Ts, b * QT + t - 1)
                    for m in range(M):
                        last = T.transpose(PSUM[:, 4 + t % 2, m * P:(m + 1) * P], HC[:, t, m * P:(m + 1) * P], ident[:, :])
                    last.then_inc(s_c_T, 1)
                for t in range(QT):
                    pe.wait_ge(s_c_Ts, b * QT + t + 1)
                    for m in range(M):
                        last = T.matmul(PSUM[:, 6, t * P:(t + 1) * P], HTC[:, t, m * P:(m + 1) * P], downT[:, m, :],
                                        start=(m == 0), stop=(m == M - 1))
                last.then_inc(s_c_o, 1)

                turn_rows(YN)
                T.matmul(bank(1), WcT[:, P:2 * P], YT[:, :], start=True, stop=True).then_inc(s_d_q, 1)
                T.matmul(bank(0), WcT[:, 0:P], YT[:, :], start=True, stop=True).then_inc(s_d_q, 1)

                def project_values(n):
                    if n >= 2:
                        pe.wait_ge(s_d_vs, b * 8 + n - 1)
                    T.matmul(bank(6 + n % 2), YT[:, (n // 2) * P:(n // 2 + 1) * P],
                             WcT[:, 256 + 512 * (n % 2):768 + 512 * (n % 2)], start=True, stop=False)
                    T.matmul(bank(6 + n % 2), KRING[96:128, 0, 0:P], BROW[96:128, 512 * (n % 2):512 * (n % 2 + 1)],
                             start=False, stop=True).then_inc(s_d_v, 1)
                def value(s, c):
                    if s == 0 and c == 0:
                        pe.wait_ge(s_d_vs, b * 8 + 8)
                    pe.wait_ge(m_exp, 4 * full.stacks(b, s) + c + 1)
                    if c == 0 and s:
                        pe.wait_ge(m_outs, full.groups(b, s))
                    for e in range(2):
                        h = 2 * s + e
                        last = T.matmul(PSUM[e * VD:(e + 1) * VD, 6, :], V1[:, c, h * VD:(h + 1) * VD],
                                        full.probsT(s, c)[:, e, :], start=(c == 0), stop=(c == QT - 1))
                    if c == QT - 1:
                        last.then_inc(m_values, 1)

                def finish(first, n):
                    for s in range(first, first + n):
                        pe.wait_ge(m_norm, b * PAIRS + s + 1)
                        for j in range(QT):
                            last = T.matmul(bank(2 + j, D), OT[:, s, j * P:(j + 1) * P], Wo1T[:, s, :],
                                            start=(s == 0), stop=(s == PAIRS - 1))
                    if first + n == PAIRS:
                        last.then_inc(s_d_o, 1)

                paired_tensor(pe, b, full, value, finish, project_values)

                turn_rows(Y2, extra=1)
                for p in range(4):
                    T.matmul(bank(p), Wq1[:, p * P:(p + 1) * P], YT[:, :], start=True, stop=True).then_inc(s_e_q, 1)
                for p in range(4):
                    kb = 4 + 2 * (p % 2)
                    if p >= 2:
                        pe.wait_ge(s_e_ks, b * 4 + p - 1)
                    T.matmul(bank(kb), Wkv1[:, p * P:(p + 1) * P], YT[:, :], start=True, stop=True)
                    T.matmul(bank(kb + 1, CTX), Wkv1[:, p * P:(p + 1) * P], CN[:, :], start=True, stop=True)\
                        .then_inc(s_e_k, 1)
                for c in range(5):
                    if c < 4:
                        pe.wait_ge(s_e_qs, b * 4 + c + 1)
                        T.matmul(bank(c), YT[:, c * P:(c + 1) * P], Wkv1[:, 512:1024], start=True, stop=True)\
                            .then_inc(s_e_v, 1)
                    else:
                        pe.wait_ge(s_e_ks, b * 4 + 3)
                        T.matmul(PSUM[0:CTX, 4, :], CN[:, :], Wkv1[:, 512:1024], start=True, stop=True)\
                            .then_inc(s_e_v, 1)
                pe.wait_ge(s_e_ks, b * 4 + 4)
                pe.wait_ge(s_e_vs, b * 5 + 5)

                def score(i):
                    h, t, sb_ = i // 4, i % 4, 2 * (i % 2)
                    T.matmul(bank(sb_), QX[:, h // 2, t * P:(t + 1) * P], KM8[:, h, 0:SEQ], start=True, stop=True)
                    return T.matmul(bank(sb_ + 1, CTX), QX[:, h // 2, t * P:(t + 1) * P], KM8[:, h, SEQ:XK],
                                    start=True, stop=True)

                def turn(k):
                    for c in range(4):
                        T.transpose(PSUM[:, 4 + k % 2, c * P:(c + 1) * P], PBX[k % 3][:, c * P:(c + 1) * P], ident[:, :])
                    if k >= 1:
                        pe.wait_ge(s_moved, ax.unit(b, k))
                    return T.transpose(PSUM[0:CTX, 7, 0:P], PBX[k % 3][:, SEQ:XK], ident[:, :])

                def value(v):
                    for c in range(5):
                        rows = P if c < 4 else CTX
                        for e in range(2):
                            h = 2 * v + e
                            last = T.matmul(PSUM[e * XD:(e + 1) * XD, 6, :], VX[0:rows, c, h * XD:(h + 1) * XD],
                                            PTe[0:rows, h % 3, c, :], start=(c == 0), stop=(c == 4))
                    return last

                attention_tensor(pe, b, ax, score, turn, value)
                pe.wait_ge(s_outs, ax.summed(b, 4))
                project(7, 4, Wout1, s_e_o)

                turn_rows(YN)
                for i in (1, 0):
                    T.matmul(bank(i), WF[:, i, :, :].rearrange("p h d -> p (h d)"), YT[:, :], start=True, stop=True)\
                        .then_inc(s_f_q, 1)
                for c in range(QT):
                    last = T.matmul(PSUM[:, 6, c * P:(c + 1) * P], YT[:, c * P:(c + 1) * P],
                                    WF[:, 2, :, :].rearrange("p h d -> p (h d)"), start=True, stop=True)
                last.then_inc(s_f_v, 1)

                def value(s, c):
                    if s % 2 == 0:
                        return
                    if s == 1 and c == 0:
                        pe.wait_ge(s_f_vs, b + 1)
                    pe.wait_ge(m_exp, 4 * causal.stacks(b, s) + c + 1)
                    if c == 0 and s >= 3:
                        pe.wait_ge(m_outs, causal.groups(b, s // 2))
                    for lane in range(4):
                        st_, h = s - 1 + lane // 2, 2 * (s - 1) + lane
                        last = T.matmul(PSUM[lane * LANE:(lane + 1) * LANE, 6, c * P:SEQ], VP[:, c, h, :],
                                        causal.probsT(st_, c)[:, lane % 2, :], start=(c == 0), stop=(c == QT - 1))
                    if c == QT - 1:
                        last.then_inc(m_values, 1)

                def finish(first, n):
                    for g in range(first, first + n):
                        pe.wait_ge(m_outs, causal.groups(b, g + 1))
                        for j in range(QT):
                            last = T.matmul(bank(2 + j, D + HEADS), OT[:, g, j * P:(j + 1) * P], SEL[:, g, :],
                                            start=(g == 0), stop=(g == GROUPS - 1))
                    if first + n == GROUPS:
                        last.then_inc(s_f_o, 1)

                paired_tensor(pe, b, causal, value, finish)
                pe.wait_ge(s_f_y, b + 1)
                turn_rows(YF, norm_done=False)
                for t in range(QT):
                    last = T.matmul(PSUM[:, 6, t * E:(t + 1) * E], YT[:, t * P:(t + 1) * P], gateW[:, :],
                                    start=True, stop=True)
                last.then_inc(s_f_g, 1)

                def up(e):
                    for m in range(M):
                        if e >= 1:
                            pe.wait_ge(s_f_hs, (b * E + e - 1) * M + m + 1)
                        T.matmul(bank(m), W1[:, e, m * P:(m + 1) * P], YT[:, :], start=True, stop=True).then_inc(s_f_h, 1)

                def down(e):
                    pe.wait_ge(s_f_hs, (b * E + e + 1) * M)
                    if e >= 2:
                        pe.wait_ge(s_f_acc, b * E + e - 1)
                    for t in range(QT):
                        for m in range(M):
                            last = T.matmul(PSUM[:, 4 + e % 2, t * P:(t + 1) * P], HE[:, e % 2, m, t * P:(t + 1) * P],
                                            W2[:, e, m, :], start=(m == 0), stop=(m == M - 1))
                    last.then_inc(s_f_dn, 1)

                up(0)
                up(1)
                pe.wait_ge(s_f_c, b + 1)
                for t in range(QT):
                    last = T.transpose(PSUM[0:E, 7, t * P:(t + 1) * P], comb[:, t, :], ident[:, :])
                last.then_inc(s_f_cT, 1)
                down(0)
                pe.wait_ge(s_f_cTs, b + 1)
                for t in range(QT):
                    last = T.matmul(PSUM[:, 6, t * P:(t + 1) * P], combT[:, t * P:(t + 1) * P], b2r[:, :],
                                    start=True, stop=True)
                last.then_inc(s_f_b2, 1)
                for e in range(1, E):
                    if e + 1 < E:
                        up(e + 1)
                    if e == 5:
                        project_context(b + 1)
                    if e == 6:
                        turn_first(b + 1, b * NLN + next(lns))
                    if e == 7:
                        project_queries(b + 1)
                    down(e)



        @block.scalar
        def _(act):
            A = nc.scalar

            def load(dst, src, s):
                act.dma_start(dst, src).then_inc(s, 16)

            for i, w in enumerate((x1_gm, x1_bm, x1_gl, x1_bl, x0_bq, x0_bk)):
                load(vrow[i:i + 1, :], w.rearrange("(o d) -> o d", o=1), s_w0)
            load(vrow[6:8, :], a1_bc[0:256].rearrange("(o d) -> o d", o=2), s_w0)
            load(vrow[8:40, :], f1_b1.rearrange("e (m d) -> (e m) d", d=D), s_w0)
            for i, w in enumerate((qn_scale, qn_bias, kn_scale, kn_bias)):
                load(vrow[40 + i:41 + i, :].rearrange("o (h d) -> o h d", d=HD),
                     w.rearrange("(o d) -> o d", o=1).unsqueeze(1).to_broadcast([1, HEADS, HD]), s_w0)
            for i, (srcs, dst, rows, after) in enumerate(prep):
                n = len(srcs) * rows
                act.wait_ge(s_tr, i + 1)
                if after == "ctx":
                    A.activation(dst, PSUM[:, i % 7, 0:n].rearrange("p (b s) -> p b s", b=BATCH), ACT.Identity,
                                 bias=V[:, BM:BM + 1], scale=V[:, GM:GM + 1]).then_inc(s_ev, 1)
                else:
                    A.activation(dst, PSUM[:, i % 7, 0:n].rearrange("p (b s) -> p b s", s=rows) if len(dst.shape) == 3
                                 else PSUM[:, i % 7, 0:n], ACT.Copy).then_inc(s_ev, 1)
                if i == 0:
                    act.wait_ge(s_ev, 1)
            A.activation(vs[:, 0:1], V[:, BQ0:BQ0 + 1], ACT.Copy, scale=HD ** -0.5)
            A.activation(vs[:, 1:2], V[:, BCQ:BCQ + 1], ACT.Copy, scale=HD ** -0.5)
            A.activation(aI, ident[:, :], ACT.Copy, scale=NS_A)
            def copy_inputs(c):
                act.wait_ge(s_yT, c + 1)
                A.activation(YT[:, :], bank(0), ACT.Copy).then_inc(s_yTs, 1)

            def chunk(c, more):
                act.wait_ge(s_ss, c + 1)
                A.activation(normw[:, 128:256], normw[:, 0:128], ACT.Sqrt).then_inc(s_nrm, 1)
                if more:
                    copy_inputs(c + 1)
                act.wait_ge(s_qkT, 2 * c + 1)
                A.activation(QTall[:, bass.ds(c * SEQ, SEQ)], bank(5), ACT.Identity, scale=V[:, QSC:QSC + 1],
                             bias=V[:, QBI:QBI + 1]).then_inc(s_qkTs, 1)
                act.wait_ge(s_qkT, 2 * c + 2)
                A.activation(KTall[:, bass.ds(c * SEQ, SEQ)], bank(6), ACT.Identity, scale=V[:, KSC:KSC + 1],
                             bias=V[:, KBI:KBI + 1]).then_inc(s_qkTs, 1)

            copy_inputs(0)
            with act.Fori(0, BATCH - 1) as c:
                chunk(c, True)
            chunk(BATCH - 1, False)
            with act.Fori(0, STEPS) as step:
                def gate_val(t):
                    n, par = step * TILES + t, t % 2
                    act.wait_ge(s_gu, n + 1)
                    if t >= 2:
                        act.wait_ge(s_w, n - 1)
                    A.activation(sg[par], bank(0), ACT.Sigmoid).then_inc(s_sig, 1)
                    A.activation(us[par], bank(1), ACT.Copy).then_inc(s_uc, 1)

                gate_val(0)
                for t in range(TILES):
                    n = step * TILES + t
                    act.wait_ge(s_hT, n + 1)
                    A.activation(hTs, bank(2), ACT.Copy).then_inc(s_hTs, 1)
                    if t + 1 < TILES:
                        gate_val(t + 1)
                    act.wait_ge(s_dpT, n + 1)
                    A.activation(dpT, PSUM[:, 3, 128:256], ACT.Copy).then_inc(s_dpTs, 1)
                act.wait_ge(s_gs, step * 3 + 3)
                for i in range(3):
                    last = A.activation(nxT[i], nx[i], ACT.Square, accum_out=sm[:, i:i + 1])
                last.then_inc(s_sq, 1)
                for i in range(3):
                    act.wait_ge(s_xt0, step * 3 + i + 1)
                    A.activation(nxT[i], bank(1 + i), ACT.Copy).then_inc(s_xt0s, 1)
                with act.Fori(0, NS_ITERS) as it:
                    k = (step * NS_ITERS + it) * 3
                    for i in range(3):
                        act.wait_ge(s_A, k + i + 1)
                        A.activation(nA[i], PSUM[:, i, 0:P], ACT.Copy).then_inc(s_As, 1)
                    for i, bx in enumerate((3, 5, 7)):
                        act.wait_ge(s_XN, k + i + 1)
                        act.wait_ge(s_XTN, k + i + 1)
                        A.activation(nx[i], bank(bx), ACT.Copy).then_inc(s_XNs, 1)
            with act.Fori(0, BATCH) as c:
                for m in range(M):
                    n = c * M + m
                    act.wait_ge(s_fg, n + 1)
                    A.activation(fsg[:, m % 2, :], bank(m % 2), ACT.Sigmoid).then_inc(s_fs, 1)
                act.wait_ge(s_fo, c + 1)
                A.activation(foT, bank(4), ACT.Copy).then_inc(s_fos, 1)

            def context_keys(n):
                act.wait_ge(s_b_k, n + 1)
                A.activation(KT0[:, 0:CTX], bank(7, CTX), ACT.Identity, bias=V[:, BK0:BK0 + 1]).then_inc(s_b_ks, 1)

            def first_queries(n):
                act.wait_ge(s_bT, n * NTR + 1)
                A.activation(YT[:, :], bank(7), ACT.Copy).then_inc(s_bTs, 1)
                act.wait_ge(s_b_q, n + 1)
                A.activation(QS, bank(6), ACT.Identity, scale=HD ** -0.5, bias=vs[:, 0:1]).then_inc(s_b_qs, 1)

            context_keys(0)
            first_queries(0)
            with act.Fori(0, BATCH) as b:
                trs = iter(range(2, NTR + 2))

                def rows_T(scale=None, bias=None):
                    act.wait_ge(s_bT, b * NTR + next(trs))
                    if scale is None:
                        A.activation(YT[:, :], bank(7), ACT.Copy).then_inc(s_bTs, 1)
                    else:
                        A.activation(YT[:, :], bank(7), ACT.Identity, scale=scale, bias=bias).then_inc(s_bTs, 1)

                def exp(i):
                    for g in range(GH):
                        last = A.activation(PB[:, i % 2, g * CTX:(g + 1) * CTX], PSUM[:, i % 2, g * CTX:(g + 1) * CTX], ACT.Exp,
                                            bias=nmax[:, i % 2, g:g + 1], accum_out=rsum[:, i % 2, g:g + 1])
                    return last

                def move(k):
                    j, t = k // 4, k % 4
                    return A.activation(PT0[0:CTX, j % 2, :, t * P:(t + 1) * P],
                                        PSUM[0:CTX, 2 + k % 2, :].rearrange("p (g q) -> p g q", g=4), ACT.Copy)

                attention_scalar(act, b, a0, exp, move)

                rows_T()
                act.wait_ge(s_c_r1, b + 1)
                for t in range(QT):
                    act.wait_ge(s_c_u, b * QT + t + 1)
                    A.activation(HC[:, t, :], bank(t), ACT.Gelu, scale=root[:, 0, t:t + 1]).then_inc(s_c_g, 1)
                for t in range(QT):
                    act.wait_ge(s_c_T, b * QT + t + 1)
                    A.activation(HTC[:, t, :], bank(4 + t % 2), ACT.Copy).then_inc(s_c_Ts, 1)

                def exp_at(base, width):
                    def exp(i):
                        w = width(i)
                        return A.activation(PBX[i % 3][:, 0:w], PSF[:, base(i):base(i) + w], ACT.Exp, bias=nmax[:, 0, i % 3:i % 3 + 1],
                                            accum_out=rsum[:, 0, i % 3:i % 3 + 1])
                    return exp

                rows_T()
                act.wait_ge(s_d_q, 2 * b + 1)
                A.activation(Kraw, bank(1), ACT.Identity, bias=V[:, BCK:BCK + 1]).then_inc(s_d_qb, 1)
                act.wait_ge(s_d_q, 2 * b + 2)
                A.activation(Qraw, bank(0), ACT.Identity, scale=HD ** -0.5, bias=vs[:, 1:2]).then_inc(s_d_qb, 1)

                def values(n):
                    act.wait_ge(s_d_v, b * 8 + n + 1)
                    A.activation(V1[:, n // 2, 512 * (n % 2):512 * (n % 2 + 1)], bank(6 + n % 2), ACT.Copy, scale=SLOPE)\
                        .then_inc(s_d_vx, 1)

                paired_scalar(act, b, full, values)

                rows_T(V[:, GL:GL + 1], V[:, BL:BL + 1])
                for p in range(4):
                    act.wait_ge(s_e_q, b * 4 + p + 1)
                    A.activation(QX[:, p, :], bank(p), ACT.Copy, scale=XD ** 0.5).then_inc(s_e_qs, 1)
                for c in range(5):
                    rows = P if c < 4 else CTX
                    act.wait_ge(s_e_v, b * 5 + c + 1)
                    A.activation(VX[0:rows, c, :], PSUM[0:rows, c, :], ACT.Copy).then_inc(s_e_vs, 1)

                def move(k):
                    h, t = k // 4, k % 4
                    A.activation(PTe[0:CTX, h % 3, 4, t * P:(t + 1) * P], PSUM[0:CTX, 7, 0:P], ACT.Copy)
                    return A.activation(PTe[:, h % 3, 0:4, t * P:(t + 1) * P],
                                        bank(4 + k % 2).rearrange("p (c q) -> p c q", c=4), ACT.Copy)

                attention_scalar(act, b, ax, exp_at(lambda i: 1024 * (i % 2), lambda i: XK), move)

                rows_T()
                act.wait_ge(s_f_q, 2 * b + 1)
                A.activation(Kraw, bank(1), ACT.Copy).then_inc(s_f_qs, 1)
                act.wait_ge(s_f_q, 2 * b + 2)
                A.activation(Qraw, bank(0), ACT.Copy, scale=D ** -0.5).then_inc(s_f_qs, 1)

                paired_scalar(act, b, causal)
                rows_T()

                def relu(e):
                    if e >= 2:
                        act.wait_ge(s_f_dn, b * E + e - 1)
                    for m in range(M):
                        act.wait_ge(s_f_h, (b * E + e) * M + m + 1)
                        A.activation(HE[:, e % 2, m, :], bank(m), ACT.Relu, bias=V[:, B1C + e * M + m:B1C + e * M + m + 1])\
                            .then_inc(s_f_hs, 1)

                relu(0)
                act.wait_ge(s_f_d, b + 1)
                A.activation(tw[:, 1, :], tw[:, 0, :], ACT.Exp).then_inc(s_f_e, 1)
                relu(1)
                act.wait_ge(s_f_cT, b + 1)
                A.activation(combT, PSUM[0:E, 7, :], ACT.Copy).then_inc(s_f_cTs, 1)
                for e in range(2, E):
                    relu(e)
                    if e == 6:
                        context_keys(b + 1)
                first_queries(b + 1)
            act.wait_ge(s_rowdone, BATCH)

        @block.vector
        def _(dve):
            Vv = nc.vector

            def head_groups(ap):
                return ap.rearrange("p t w (h d) -> p (t w h) d", d=HD)

            dve.wait_ge(s_w0, N_W0)
            Vv.tensor_reduce(sm[:, 0:1], upraw, AX.X, ALU.add, apply_absolute_value=True)
            Vv.tensor_reduce(sm[:, 1:2], downraw, AX.X, ALU.add, apply_absolute_value=True).then_inc(s_absum, 1)
            dve.wait_ge(s_thr, 1)
            Vv.tensor_scalar(sm[:, 2:4], bank(7, 2), 0.5 / (HID * D), None, ALU.mult)
            dve.drain()
            Vv.tensor_scalar(sm[:, 4:6], sm[:, 2:4], -1.0, None, ALU.mult)
            dve.drain()
            for i, w in enumerate((upraw, downraw)):
                Vv.tensor_scalar(tern[:, i, :], w, sm[:, 2 + i:3 + i], None, ALU.is_gt)
                dve.drain()
                Vv.scalar_tensor_tensor(tern[:, i, :], w, sm[:, 4 + i:5 + i], tern[:, i, :], ALU.is_lt, ALU.subtract)
                dve.drain()
                Vv.scalar_tensor_tensor(tern[:, i, :], tern[:, i, :], -1.0, w, ALU.mult, ALU.subtract)
                dve.drain()
                last = Vv.tensor_tensor(ternq[:, i, :], tern[:, i, :], w, ALU.add)
            last.then_inc(s_tern, 1)
            ln_vector(dve, n_ctx, 1, [ctxraw[0:CTX, b, :] for b in range(BATCH)],
                      [ctxn[0:CTX, b, :] for b in range(BATCH)], CTX)
            dve.wait_ge(s_wt, N_WT)
            dve.wait_ge(s_x, 16)
            dve.wait_ge(s_ev, NPREP)
            for dst, src in ((kscale, kscale8), (kbias, kbias8)):
                Vv.tensor_copy(dst.rearrange("p (h d) -> p h d", d=HD), src.unsqueeze(1).to_broadcast([P, HEADS, HD]))
            def norm_inputs(c):
                ln_vector(dve, n_in, c + 1, [X[:, bass.ds(c * QT + j, 1), :].rearrange("p o d -> p (o d)") for j in range(QT)],
                          [YN[:, j, :] for j in range(QT)])

            def chunk(c, more, first=False):
                if more:
                    dve.wait_ge(s_yT, c + 1)
                    norm_inputs(c + 1)
                if not first:
                    dve.wait_ge(s_qkT, 2 * c)
                    dve.wait_ge(s_kn, c)
                for j in range(QT):
                    dve.wait_ge(s_qkv, c * QT + (j + 1))
                    Vv.tensor_tensor(qkvs[:, j, :, :].rearrange("p w d -> p (w d)"), PSUM[:, 1 + j, 0:256], bqkv[:, 0:256], ALU.add)
                    Vv.tensor_tensor(Vn[:, bass.ds(c * QT + j, 1), :].rearrange("p o d -> p (o d)"), PSUM[:, 1 + j, 256:384],
                                     bqkv[:, 256:384], ALU.add)
                dve.drain()
                g3 = VA[:, 0:1024].rearrange("p (g d) -> p g d", d=HD)
                Vv.tensor_tensor(sq4, VA[:, 0:1024], VA[:, 0:1024], ALU.mult)
                dve.drain()
                Vv.tensor_reduce(normw[:, 0:128], sq4.rearrange("p (g d) -> p g d", d=HD), AX.X, ALU.add).then_inc(s_ss, 1)
                dve.wait_ge(s_nrm, c + 1)
                Vv.tensor_scalar(normw[:, 128:256], normw[:, 128:256], 1e-6, None, ALU.add)
                dve.drain()
                Vv.reciprocal(normw[:, 0:128], normw[:, 128:256])
                dve.drain()
                Vv.tensor_tensor(g3, g3, normw[:, 0:128].unsqueeze(2).to_broadcast([P, P, HD]), ALU.mult).then_inc(s_qk, 1)

            norm_inputs(0)
            chunk(0, True, first=True)
            with dve.Fori(1, BATCH - 1) as c:
                chunk(c, True)
            chunk(BATCH - 1, False)
            dve.wait_ge(s_qkTs, 2 * BATCH)
            with dve.Fori(0, STEPS) as step:
                def silu(t):
                    n, par = step * TILES + t, t % 2
                    if t >= 2:
                        dve.wait_ge(s_w, n - 1)
                        dve.wait_ge(s_dgu, n - 1)
                    dve.wait_ge(s_sig, n + 1)
                    Vv.tensor_tensor(t1[par], bank(0), sg[par], ALU.mult).then_inc(s_t, 1)
                    dve.wait_ge(s_t, n + 1)
                    dve.wait_ge(s_uc, n + 1)
                    Vv.tensor_tensor(hh[par], us[par], t1[par], ALU.mult).then_inc(s_h, 1)

                silu(0)
                for t in range(TILES):
                    n, par = step * TILES + t, t % 2
                    if t + 1 < TILES:
                        silu(t + 1)
                    dve.wait_ge(s_pred, n + 1)
                    Vv.tensor_tensor(dp, bank(3, P), Vn[:, t, :], ALU.subtract)
                    dve.drain()
                    Vv.tensor_scalar(dp, dp, 2.0 / (TILES * P * D), None, ALU.mult).then_inc(s_dp, 1)
                    dve.wait_ge(s_dh, n + 1)
                    Vv.tensor_tensor(du, bank(4), t1[par], ALU.mult)
                    dve.wait_ge(s_w, n + 1)
                    Vv.tensor_tensor(dg, bank(4), ww[par], ALU.mult).then_inc(s_dgu, 1)
                dve.wait_ge(s_grad, step + 1)
                for i in range(3):
                    Vv.tensor_copy(nx[i], bank(5 + i)).then_inc(s_gs, 1)
                dve.wait_ge(s_tot, step + 1)
                Vv.tensor_copy(sm[:, 4:7], bank(0, 3)).then_inc(s_tots, 1)
                dve.wait_ge(s_nrt, step + 1)
                Vv.tensor_scalar(sm[:, 8:11], sm[:, 8:11], 1e-7, None, ALU.add)
                dve.drain()
                Vv.reciprocal(sm[:, 12:15], sm[:, 8:11])
                dve.drain()
                for i in range(3):
                    Vv.tensor_scalar(nx[i], nx[i], sm[:, 12 + i:13 + i], None, ALU.mult).then_inc(s_x0, 1)
                with dve.Fori(0, NS_ITERS) as it:
                    k = (step * NS_ITERS + it) * 3
                    for i in range(3):
                        dve.wait_ge(s_As, k + i + 1)
                        Vv.scalar_tensor_tensor(nC[i], nA[i], NS_B, aI, ALU.mult, ALU.add)
                    dve.drain()
                    for i in range(3):
                        dve.wait_ge(s_A2, k + i + 1)
                        Vv.scalar_tensor_tensor(nB[i], PSUM[:, i, P:2 * P], NS_C, nC[i], ALU.mult, ALU.add).then_inc(s_B, 1)
                    for i, bt in enumerate((4, 6, 3)):
                        dve.wait_ge(s_XTN, k + i + 1)
                        Vv.tensor_copy(nxT[i], bank(bt)).then_inc(s_XTNs, 1)
                dve.wait_ge(s_XNs, (step + 1) * NS_ITERS * 3)
                dve.wait_ge(s_XTNs, (step + 1) * NS_ITERS * 3)
                Vv.scalar_tensor_tensor(gate, nx[0], -LR, gate, ALU.mult, ALU.add)
                Vv.scalar_tensor_tensor(val, nx[1], -LR, val, ALU.mult, ALU.add)
                Vv.scalar_tensor_tensor(projT, nx[2], -LR, projT, ALU.mult, ALU.add)
                Vv.scalar_tensor_tensor(proj.rearrange("p m d -> p (m d)"), nxT[2], -LR,
                                        proj.rearrange("p m d -> p (m d)"), ALU.mult, ALU.add).then_inc(s_upd, 1)
            with dve.Fori(0, BATCH) as c:
                for m in range(M):
                    n = c * M + m
                    dve.wait_ge(s_fs, n + 1)
                    Vv.tensor_tensor(ft[:, m % 2, :], bank(m % 2), fsg[:, m % 2, :], ALU.mult)
                    dve.drain()
                    dve.wait_ge(s_fu, n + 1)
                    Vv.tensor_tensor(fh[:, m, :], bank(2 + m % 2), ft[:, m % 2, :], ALU.mult).then_inc(s_fh, 1)
                dve.wait_ge(s_fy, c + 1)
                xs = X[:, bass.ds(c * QT, QT), :]
                Vv.tensor_tensor(Y2[:, :, :], PSUM[:, 5, :].rearrange("p (t d) -> p t d", d=D),
                                 bproj.unsqueeze(1).to_broadcast([P, QT, D]), ALU.add)
                dve.drain()
                Vv.tensor_tensor(xs, xs, Y2[:, :, :], ALU.add).then_inc(s_fx, 1)

            Vv.memset(VPA[:, :], 0.0)
            dve.drain()
            Vv.memset(VP[:, :, :, HD:HD + 1], 1.0).then_inc(s_zero, 1)
            dve.wait_ge(s_wr, N_WR)
            dve.drain()
            def context_values(n):
                dve.wait_ge(s_b_v, n + 1)
                Vv.tensor_tensor(VP[0:CTX, 0, :, 0:HD], PSUM[0:CTX, 6, 0:P].rearrange("p (h d) -> p h d", d=HD),
                                 bc[0:CTX, BV0, :].rearrange("p (h d) -> p h d", d=HD), ALU.add).then_inc(s_b_vs, 1)

            def context_masked(n):
                dve.wait_ge(s_b_ks, n + 1)
                Vv.tensor_tensor(KM0, KT0[:, 0:CTX].unsqueeze(1).to_broadcast([P, HEADS, CTX]),
                                 head_mask[:, :].unsqueeze(2).to_broadcast([P, HEADS, CTX]), ALU.mult).then_inc(s_b_km, 1)

            def first_norm(n, norm):
                row = n % BATCH
                ln_vector(dve, n_b, norm,
                          [X[:, bass.ds(row * QT + j, 1), :].rearrange("p o d -> p (o d)") for j in range(QT)],
                          [YN[:, j, :] for j in range(QT)])

            first_norm(0, 1)
            context_values(0)
            context_masked(0)
            with dve.Fori(0, BATCH) as b:
                lns = iter(range(2, NLN + 2))
                xs = X[:, bass.ds(b * QT, QT), :]

                def xt(j):
                    return X[:, bass.ds(b * QT + j, 1), :].rearrange("p o d -> p (o d)")

                def tiles(y):
                    return [y[:, j, :] for j in range(QT)]

                def norm(src, dst):
                    dve.drain()
                    ln_vector(dve, n_b, b * NLN + next(lns), src, dst)

                def rows(i):
                    return bc[:, i, :].unsqueeze(1).to_broadcast([P, QT, D])

                def tok(n):
                    return bank(n).rearrange("p (t d) -> p t d", d=D)

                def split(i, raw):
                    Vv.tensor_copy(PARTS[:, 2 * i, :], raw).then_inc(m_parts, 1)
                    dve.drain()
                    Vv.tensor_tensor(PARTS[:, 2 * i + 1, :], raw, PARTS[:, 2 * i, :].bitcast(F32), ALU.subtract)\
                        .then_inc(m_parts, 1)

                def normaliser(width):
                    def normalise(k):
                        Vv.reciprocal(rinv[:, 0, k % 3:k % 3 + 1], rsum[:, 0, k % 3:k % 3 + 1])
                        dve.drain()
                        w = width(k)
                        return Vv.tensor_scalar(PBX[k % 3][:, 0:w], PBX[k % 3][:, 0:w], rinv[:, 0, k % 3:k % 3 + 1], None, ALU.mult)
                    return normalise

                def maximum_of(base, width):
                    def maximum(i):
                        return Vv.tensor_reduce(nmax[:, 0, i % 3:i % 3 + 1], PSF[:, base(i):base(i) + width(i)], AX.X, ALU.max, negate=True)
                    return maximum

                def maximum(i):
                    return Vv.tensor_reduce(nmax[:, i % 2, :], bank(i % 2, 4 * CTX).rearrange("p (g k) -> p g k", g=4),
                                            AX.X, ALU.max, negate=True)

                def normalise(k):
                    Vv.reciprocal(rinv[:, k % 2, :], rsum[:, k % 2, :])
                    dve.drain()
                    p3 = PB[:, k % 2, 0:4 * CTX].rearrange("p (g k) -> p g k", g=4)
                    return Vv.tensor_tensor(p3, p3, rinv[:, k % 2, :].unsqueeze(2).to_broadcast([P, 4, CTX]), ALU.mult)

                attention_vector(dve, b, a0, maximum, normalise, lambda v: Vv.tensor_copy(OT[:, v, :], bank(4 + v % 2)))
                dve.wait_ge(s_b_o, b + 1)
                Vv.tensor_tensor(Y2[:, :, :], tok(6), rows(BO0), ALU.add)
                dve.drain()
                Vv.tensor_tensor(xs, xs, Y2[:, :, :], ALU.add)

                norm([xt(j) for j in range(QT)], tiles(YN))
                dve.drain()
                for j in range(QT):
                    last = Vv.tensor_tensor_reduce(out=KMA[:, j * P:(j + 1) * P], in0=YN[:, j, :], in1=YN[:, j, :], scale=1.0,
                                                   scalar=0.0, op0=ALU.mult, op1=ALU.add, accum_out=ssq[:, 0, j:j + 1])
                last.then_inc(s_pow, 1)
                dve.wait_ge(s_powd, 2 * b + 1)
                Vv.tensor_scalar(root[:, 0, :], root[:, 0, :], float(D) ** -0.5, 1e-8, ALU.mult, ALU.add)
                dve.drain()
                Vv.reciprocal(root[:, 0, :], root[:, 0, :]).then_inc(s_c_r1, 1)
                for j in range(QT):
                    dve.wait_ge(s_c_g, b * QT + j + 1)
                    last = Vv.tensor_tensor_reduce(out=KMA[:, 512 * (j + 1):512 * (j + 2)], in0=HC[:, j, :], in1=HC[:, j, :],
                                                   scale=1.0, scalar=0.0, op0=ALU.mult, op1=ALU.add, accum_out=ssq[:, 1, j:j + 1])
                last.then_inc(s_pow, 1)
                dve.wait_ge(s_powd, 2 * b + 2)
                Vv.tensor_scalar(root[:, 1, :], root[:, 1, :], float(HID) ** -0.5, 1e-8, ALU.mult, ALU.add)
                dve.drain()
                Vv.reciprocal(root[:, 1, :], root[:, 1, :])
                dve.drain()
                dve.wait_ge(s_c_o, b + 1)
                for j in range(QT):
                    Vv.scalar_tensor_tensor(xt(j), PSUM[:, 6, j * P:(j + 1) * P], root[:, 1, j:j + 1], xt(j), ALU.mult, ALU.add)

                norm([xt(j) for j in range(QT)], tiles(YN))
                for i, raw in ((1, Kraw), (0, Qraw)):
                    dve.wait_ge(s_d_qb, 2 * b + 2 - i)
                    Vv.scalar_tensor_tensor(raw, raw, SLOPE, raw, ALU.mult, ALU.max)
                    dve.drain()
                    split(i, raw)

                def values(n):
                    dve.wait_ge(s_d_vx, b * 8 + n + 1)
                    v1 = V1[:, n // 2, 512 * (n % 2):512 * (n % 2 + 1)]
                    Vv.tensor_tensor(v1, bank(6 + n % 2), v1, ALU.max).then_inc(s_d_vs, 1)

                paired_vector(dve, b, full, values)
                Vv.tensor_tensor(xs, xs, YN[:, :, :], ALU.add)
                dve.wait_ge(s_d_o, b + 1)
                Vv.tensor_tensor(Y2[:, :, :], PSUM[:, 2:6, 0:D], rows(BO1), ALU.add)
                dve.drain()
                Vv.scalar_tensor_tensor(Y2[:, :, :], Y2[:, :, :], SLOPE, Y2[:, :, :], ALU.mult, ALU.max)
                dve.drain()
                Vv.tensor_tensor(xs, xs, Y2[:, :, :], ALU.add)

                norm([xt(j) for j in range(QT)], tiles(YN))
                norm(tiles(YN), tiles(Y2))
                for p in range(4):
                    dve.wait_ge(s_e_k, b * 4 + p + 1)
                    kb = 512 * (4 + 2 * (p % 2))
                    for e in range(2):
                        last = Vv.tensor_scalar(KM8[:, 2 * p + e, 0:XK], PSF[:, kb:kb + XK], half_mask[:, e:e + 1], None, ALU.mult)
                    last.then_inc(s_e_ks, 1)
                attention_vector(dve, b, ax, maximum_of(lambda i: 1024 * (i % 2), lambda i: XK), normaliser(lambda i: XK),
                                 lambda v: Vv.tensor_copy(OT[:, v, :], bank(6)))
                dve.wait_ge(s_e_o, b + 1)
                Vv.tensor_tensor(xs, tok(7), xs, ALU.add)

                norm([xt(j) for j in range(QT)], tiles(YN))
                for i, raw in ((1, Kraw), (0, Qraw)):
                    dve.wait_ge(s_f_qs, 2 * b + 2 - i)
                    split(i, raw)
                dve.wait_ge(s_f_v, b + 1)
                Vv.tensor_copy(VP[:, :, :, 0:HD].rearrange("p t h d -> p (t h) d"),
                               bank(6).rearrange("p (g d) -> p g d", d=HD)).then_inc(s_f_vs, 1)
                paired_vector(dve, b, causal)
                Vv.tensor_tensor(YF[:, :, :], YN[:, :, :], rows(C1), ALU.add)
                dve.wait_ge(s_f_o, b + 1)
                Vv.reciprocal(rsums[:, :, :], PSUM[:, 2:6, D:D + HEADS])
                dve.drain()
                for j in range(QT):
                    Vv.tensor_tensor(Y2[:, j, :].rearrange("p (h d) -> p h d", d=HD), bank(2 + j, D).rearrange("p (h d) -> p h d", d=HD),
                                     rsums[:, j, :].unsqueeze(2).to_broadcast([P, HEADS, HD]), ALU.mult)
                norm(tiles(Y2), tiles(Y2))
                dve.drain()
                Vv.tensor_tensor(Y2[:, :, :], Y2[:, :, :], rows(G1), ALU.mult)
                dve.drain()
                Vv.tensor_tensor(YF[:, :, :], Y2[:, :, :], YF[:, :, :], ALU.add).then_inc(s_f_y, 1)
                dve.wait_ge(s_f_g, b + 1)
                Vv.tensor_copy(logit[:, :, :], bank(6, QT * E).rearrange("p (t e) -> p t e", e=E))
                dve.drain()
                for j in range(QT):
                    Vv.max(top[:, j, :], logit[:, j, :])
                dve.drain()
                for j in range(QT):
                    Vv.max_index(topi[:, j, :], top[:, j, :], logit[:, j, :])
                Vv.tensor_tensor(tw[:, 0, :], top[:, :, 1], top[:, :, 0], ALU.subtract).then_inc(s_f_d, 1)
                dve.drain()
                Vv.tensor_copy(topf[:, :, :], topi[:, :, :])
                dve.wait_ge(s_f_e, b + 1)
                Vv.tensor_scalar(tw[:, 2, :], tw[:, 1, :], 1.0, None, ALU.add)
                dve.drain()
                Vv.reciprocal(tw[:, 2, :], tw[:, 2, :])
                dve.drain()
                Vv.tensor_tensor(tw[:, 3, :], tw[:, 1, :], tw[:, 2, :], ALU.mult)
                dve.drain()
                for j in range(QT):
                    Vv.tensor_scalar(comb[:, j, :], iota8[:, :], topf[:, j, 0:1], tw[:, 2, j:j + 1], ALU.is_equal, ALU.mult)
                    Vv.tensor_scalar(comb2[:, j, :], iota8[:, :], topf[:, j, 1:2], tw[:, 3, j:j + 1], ALU.is_equal, ALU.mult)
                dve.drain()
                Vv.tensor_tensor(comb[:, :, :], comb[:, :, :], comb2[:, :, :], ALU.add).then_inc(s_f_c, 1)
                dve.wait_ge(s_f_b2, b + 1)
                Vv.tensor_copy(Y2[:, :, :], tok(6))
                for e in range(E):
                    dve.drain()
                    dve.wait_ge(s_f_dn, b * E + e + 1)
                    for j in range(QT):
                        last = Vv.scalar_tensor_tensor(Y2[:, j, :], PSUM[:, 4 + e % 2, j * P:(j + 1) * P], comb[:, j, e:e + 1],
                                                       Y2[:, j, :], ALU.mult, ALU.add)
                    last.then_inc(s_f_acc, 1)
                    if e == 1:
                        dve.drain()
                        first_norm(b + 1, b * NLN + next(lns))
                    if e == 2:
                        dve.drain()
                        Vv.tensor_tensor(xs, xs, YF[:, :, :], ALU.add)
                    if e == 3:
                        Vv.tensor_tensor(xs, xs, rows(C2), ALU.add)
                    if e == 5:
                        context_values(b + 1)
                        context_masked(b + 1)
                norm(tiles(Y2), tiles(Y2))
                dve.drain()
                Vv.tensor_tensor(Y2[:, :, :], Y2[:, :, :], rows(G2), ALU.mult)
                dve.drain()
                Vv.tensor_tensor(xs, xs, Y2[:, :, :], ALU.add).then_inc(s_rowdone, 1)


_INS = ["x", "ctx_1024", "L0_attn_qkv_w", "L0_attn_qkv_b", "L0_attn_qn_scale", "L0_attn_qn_bias", "L0_attn_kn_scale",
        "L0_attn_kn_bias", "L0_attn_ttt_gate", "L0_attn_ttt_val", "L0_attn_ttt_proj", "L0_attn_proj_w",
        "L0_attn_proj_b", "L0_xattn_Wq", "L0_xattn_bq", "L0_xattn_Wk", "L0_xattn_bk", "L0_xattn_Wv", "L0_xattn_bv",
        "L0_xattn_Wo", "L0_xattn_bo", "L0_ffn_w_up", "L0_ffn_w_down", "L1_attn_Wc", "L1_attn_bc", "L1_attn_Wo",
        "L1_attn_bo", "L1_xattn_Wq", "L1_xattn_Wkv", "L1_xattn_Wout", "L1_xattn_gm", "L1_xattn_bm", "L1_xattn_gl",
        "L1_xattn_bl", "L1_ffn_Wq", "L1_ffn_Wk", "L1_ffn_Wv", "L1_ffn_gate_W", "L1_ffn_W1", "L1_ffn_b1",
        "L1_ffn_W2", "L1_ffn_b2", "L1_ffn_ln1_g", "L1_ffn_ln1_b", "L1_ffn_ln2_g", "L1_ffn_ln2_b"]


def kernel(**inputs):
    import numpy as _np
    import concourse.bacc as _bacc
    from concourse import mybir as _mybir
    from concourse.bass_utils import run_bass_kernel_spmd as _run

    nc = _bacc.Bacc("TRN2", target_bir_lowering=False, num_devices=1)
    arrays, args = {}, []
    for name in _INS:
        a = _np.ascontiguousarray(inputs[name])
        arrays[f"in_{name}_dram"] = a
        args.append(nc.dram_tensor(f"in_{name}_dram", a.shape, _mybir.dt.from_np(a.dtype), kind="ExternalInput").ap())
    out = nc.dram_tensor("out_dram", (BATCH, SEQ, D), F32, kind="ExternalOutput").ap()
    decoder_kernel(nc, *args, out)
    r = _run(nc, [arrays], core_ids=[0])
    return r.results[0]["out_dram"]
```
